# Optimizing a Trainium2 kernel written in Bass

```python
import numpy as np
import jax
import jax.numpy as jnp

def _softmax(x, axis=-1):
    return jax.nn.softmax(x, axis=axis)

def _gelu(x):
    return jax.nn.gelu(x, approximate=True)

def _silu(x):
    return jax.nn.silu(x)

def _sigmoid(x):
    return jax.nn.sigmoid(x)

def _layernorm(x, axis=-1, eps=1e-05):
    m = jnp.mean(x, axis=axis, keepdims=True)
    v = jnp.var(x, axis=axis, keepdims=True)
    return (x - m) / jnp.sqrt(v + eps)

def _scatter_add(tgt, idx, src, axis=0):
    return tgt.at[idx].add(src)

def _segment_sum(src, seg, n):
    return jax.ops.segment_sum(src, seg, n)
kernel_name = 'mk_hybrid_d2_jaxref_r8_5c1448'

def setup_inputs(seed: int=0):
    np.random.seed(seed)
    _w = jnp.asarray

    def _L0_attn_a_setup():
        import jax, jax.numpy as jnp
        import numpy as np
        EPS = 1e-06
        H, NOPE, ROPE, VD = (16, 128, 64, 128)
        QHD = NOPE + ROPE
        SCALE = QHD ** (-0.5)
        THETA = 10000.0

        def rmsnorm(x, w):
            x32 = x.astype(jnp.float32)
            var = jnp.mean(x32 * x32, axis=-1, keepdims=True)
            return (w * (x32 * jax.lax.rsqrt(var + EPS))).astype(x.dtype)

        def rope_cos_sin(seq_len):
            inv_freq = 1.0 / THETA ** (jnp.arange(0, ROPE, 2, dtype=jnp.float32) / ROPE)
            t = jnp.arange(seq_len, dtype=jnp.float32)
            freqs = jnp.outer(t, inv_freq)
            emb = jnp.concatenate([freqs, freqs], -1)
            return (jnp.cos(emb), jnp.sin(emb))

        def rotate_half(x):
            x1, x2 = (x[..., :x.shape[-1] // 2], x[..., x.shape[-1] // 2:])
            return jnp.concatenate([-x2, x1], axis=-1)
        key = jax.random.key(seed)
        ks = jax.random.split(key, 6)
        B, S, D = (2, 256, 256)
        return {'hidden_states': jax.random.normal(ks[0], (B, S, D), jnp.float32), 'q_a_w': jax.random.normal(ks[1], (192, D), jnp.float32) * 0.02, 'q_a_ln_w': jnp.ones((192,), jnp.float32), 'q_b_w': jax.random.normal(ks[2], (H * QHD, 192), jnp.float32) * 0.02, 'kv_a_w': jax.random.normal(ks[3], (64 + ROPE, D), jnp.float32) * 0.02, 'kv_a_ln_w': jnp.ones((64,), jnp.float32), 'kv_b_w': jax.random.normal(ks[4], (H * (NOPE + VD), 64), jnp.float32) * 0.02, 'o_w': jax.random.normal(ks[5], (D, H * VD), jnp.float32) * 0.02}
    _L0_attn_a_in = _L0_attn_a_setup()

    def _L0_attn_b_setup():
        import jax, jax.numpy as jnp
        import numpy as np
        HID, H, DK, DV, KS = (256, 16, 128, 128, 4)

        def _p(key, shape, scale=0.02):
            return jax.random.normal(key, shape, dtype=jnp.float32) * scale

        def _dwconv_causal(y, w, b):
            out = jax.lax.conv_general_dilated(y.transpose(0, 2, 1), w, window_strides=(1,), padding=[(KS - 1, 0)], feature_group_count=w.shape[0])
            return out.transpose(0, 2, 1) + b

        def _silu(x):
            return x * jax.nn.sigmoid(x)

        def _gated_delta(q, k, v, alpha, beta, scale):
            B, T, nH, _ = q.shape
            qs = q.transpose(1, 0, 2, 3)
            ks = k.transpose(1, 0, 2, 3) * scale
            vs = v.transpose(1, 0, 2, 3)
            al = alpha.transpose(1, 0, 2)
            be = beta.transpose(1, 0, 2)

            def step(S, inp):
                qt, kt, vt, at, bt = inp
                err = jnp.einsum('bhvk,bhk->bhv', S, kt) - vt
                S = at[..., None, None] * S - bt[..., None, None] * err[..., None] * kt[:, :, None, :]
                o = jnp.einsum('bhvk,bhk->bhv', S, qt)
                return (S, o)
            S0 = jnp.zeros((B, nH, DV, DK), dtype=q.dtype)
            _, o = jax.lax.scan(step, S0, (qs, ks, vs, al, be))
            return o.transpose(1, 0, 2, 3)
        key = jax.random.key(seed)
        ks = jax.random.split(key, 20)
        B, T = (2, 256)
        x = jax.random.normal(ks[0], (B, T, HID), dtype=jnp.float32)
        inp = {'x': x, 'Wq': _p(ks[1], (HID, H * DK)), 'Wk': _p(ks[2], (HID, H * DK)), 'Wv': _p(ks[3], (HID, H * DV)), 'Wa': _p(ks[4], (HID, H)), 'ba': jnp.zeros((H,), jnp.float32), 'Wb': _p(ks[5], (HID, H)), 'bb': jnp.zeros((H,), jnp.float32), 'Wg': _p(ks[6], (HID, H * DV)), 'Wo': _p(ks[7], (H * DV, HID)), 'conv_q_w': _p(ks[8], (H * DK, 1, KS), 0.3), 'conv_q_b': jnp.zeros((H * DK,), jnp.float32), 'conv_k_w': _p(ks[9], (H * DK, 1, KS), 0.3), 'conv_k_b': jnp.zeros((H * DK,), jnp.float32), 'conv_v_w': _p(ks[10], (H * DV, 1, KS), 0.3), 'conv_v_b': jnp.zeros((H * DV,), jnp.float32), 'ln_w': jnp.ones((DV,), jnp.float32), 'ln_b': jnp.zeros((DV,), jnp.float32)}
        return inp
    _L0_attn_b_in = _L0_attn_b_setup()

    def _L0_ffn_setup():
        import jax, jax.numpy as jnp
        import numpy as np
        B, S, D_IN, D_OUT = (4, 256, 256, 256)
        EPS = 1e-10
        key = jax.random.key(seed)
        kx, kw, kb = jax.random.split(key, 3)
        x = jax.random.normal(kx, (B, S, D_IN), dtype=jnp.float32)
        weight = jax.random.normal(kw, (D_OUT, D_IN), dtype=jnp.float32) * 0.02
        bias = jax.random.normal(kb, (D_OUT,), dtype=jnp.float32) * 0.02
        return {'x': x, 'weight': weight, 'bias': bias}
    _L0_ffn_in = _L0_ffn_setup()

    def _L1_attn_a_setup():
        import jax, jax.numpy as jnp
        import numpy as np
        H = 16
        D_NOPE = 128
        D_ROPE = 64
        D_QK = 192
        D_V = 128
        THETA = 10000.0
        EPS = 1e-06

        def rmsnorm(x, w):
            x32 = x.astype(jnp.float32)
            x32 = x32 * jax.lax.rsqrt(jnp.mean(x32 * x32, axis=-1, keepdims=True) + EPS)
            return (x32 * w).astype(x.dtype)

        def rope_cos_sin(seq_len, dim, dtype):
            inv_freq = 1.0 / THETA ** (jnp.arange(0, dim, 2, dtype=jnp.float32) / dim)
            t = jnp.arange(seq_len, dtype=jnp.float32)
            freqs = jnp.outer(t, inv_freq)
            return (jnp.cos(freqs).astype(dtype), jnp.sin(freqs).astype(dtype))

        def apply_rope(x, cos, sin):
            d2 = x.shape[-1] // 2
            x1, x2 = (x[..., :d2], x[..., d2:])
            c = cos[None, :, None, :]
            s = sin[None, :, None, :]
            return jnp.concatenate([x1 * c - x2 * s, x2 * c + x1 * s], axis=-1)
        key = jax.random.key(seed)
        ks = jax.random.split(key, 8)
        B, T, D = (2, 256, 256)
        q_lora, kv_lora = (192, 64)

        def w(k, fan_in, fan_out):
            return jax.random.normal(k, (fan_in, fan_out), dtype=jnp.float32) * (1.0 / np.sqrt(fan_in))
        return {'hidden_states': jax.random.normal(ks[0], (B, T, D), dtype=jnp.float32), 'Wq_a': w(ks[1], D, q_lora), 'q_norm_w': jnp.ones((q_lora,), dtype=jnp.float32), 'Wq_b': w(ks[2], q_lora, H * D_QK), 'Wk_rope': w(ks[3], D, D_ROPE), 'Wkv_a': w(ks[4], D, kv_lora), 'kv_norm_w': jnp.ones((kv_lora,), dtype=jnp.float32), 'Wkv_b': w(ks[5], kv_lora, H * (D_NOPE + D_V)), 'Wo': w(ks[6], H * D_V, D)}
    _L1_attn_a_in = _L1_attn_a_setup()

    def _L1_attn_b_setup():
        import jax, jax.numpy as jnp
        import numpy as np
        B, T, E, H = (2, 256, 256, 16)
        D = E // H
        ROPE_BASE = 10000.0

        def _rope(x):
            t, d = (x.shape[-2], x.shape[-1])
            j = jnp.arange(d // 2, dtype=x.dtype)
            thetas = ROPE_BASE ** (-2.0 * j / d)
            m = jnp.arange(1, t + 1, dtype=x.dtype)
            ang = m[:, None] * thetas[None, :]
            C = jnp.concatenate([ang, ang], axis=-1)
            x_rot = jnp.concatenate([-x[..., d // 2:], x[..., :d // 2]], axis=-1)
            return x * jnp.cos(C) + x_rot * jnp.sin(C)
        key = jax.random.key(seed)
        ks = jax.random.split(key, 9)
        s = 1.0 / np.sqrt(E)
        return {'x': jax.random.normal(ks[0], (B, T, E), jnp.float32), 'Wq': jax.random.normal(ks[1], (E, E), jnp.float32) * s, 'bq': jax.random.normal(ks[2], (E,), jnp.float32) * s, 'Wk': jax.random.normal(ks[3], (E, E), jnp.float32) * s, 'bk': jax.random.normal(ks[4], (E,), jnp.float32) * s, 'Wv': jax.random.normal(ks[5], (E, E), jnp.float32) * s, 'bv': jax.random.normal(ks[6], (E,), jnp.float32) * s, 'Wo': jax.random.normal(ks[7], (E, E), jnp.float32) * s, 'bo': jax.random.normal(ks[8], (E,), jnp.float32) * s}
    _L1_attn_b_in = _L1_attn_b_setup()

    def _L1_ffn_setup():
        import jax, jax.numpy as jnp
        import numpy as np
        B_, S, D = (2, 256, 256)
        F_ = 1024
        R = 16
        H = 16
        HD = D // H
        MOD_SCALE = 0.1
        EPS = 1e-06

        def _rmsnorm(x, w):
            v = jnp.mean(x * x, axis=-1, keepdims=True)
            return x * jax.lax.rsqrt(v + EPS) * w

        def _attention(x, Wq, Wk, Wv, Wo):
            b, s, d = x.shape
            q = (x @ Wq.T).reshape(b, s, H, HD)
            k = (x @ Wk.T).reshape(b, s, H, HD)
            v = (x @ Wv.T).reshape(b, s, H, HD)
            scores = jnp.einsum('bqhd,bkhd->bhqk', q, k) / np.sqrt(HD).astype(np.float32)
            causal = jnp.tril(jnp.ones((s, s), bool))
            scores = jnp.where(causal, scores, jnp.finfo(scores.dtype).min)
            probs = jax.nn.softmax(scores, axis=-1)
            out = jnp.einsum('bhqk,bkhd->bqhd', probs, v).reshape(b, s, d)
            return out @ Wo.T
        key = jax.random.key(seed)
        ks = jax.random.split(key, 12)
        sd = 0.02
        return {'hidden_states': jax.random.normal(ks[0], (B_, S, D), jnp.float32), 'ln1_w': jnp.ones((D,), jnp.float32), 'ln2_w': jnp.ones((D,), jnp.float32), 'Wq': jax.random.normal(ks[1], (D, D), jnp.float32) * sd, 'Wk': jax.random.normal(ks[2], (D, D), jnp.float32) * sd, 'Wv': jax.random.normal(ks[3], (D, D), jnp.float32) * sd, 'Wo': jax.random.normal(ks[4], (D, D), jnp.float32) * sd, 'A': jax.random.normal(ks[5], (D, R), jnp.float32) * (0.01 / np.sqrt(D)), 'B': jax.random.normal(ks[6], (R, F_), jnp.float32) * (0.01 / np.sqrt(R)), 'W_in_base': jax.random.normal(ks[7], (F_, D), jnp.float32) * sd, 'W_up_base': jax.random.normal(ks[8], (F_, D), jnp.float32) * sd, 'W_down': jax.random.normal(ks[9], (D, F_), jnp.float32) * sd}
    _L1_ffn_in = _L1_ffn_setup()
    _d = {'L0_attn_a_hidden_states': _L0_attn_a_in['hidden_states'], 'L0_attn_a_q_a_w': _L0_attn_a_in['q_a_w'], 'L0_attn_a_q_a_ln_w': _L0_attn_a_in['q_a_ln_w'], 'L0_attn_a_q_b_w': _L0_attn_a_in['q_b_w'], 'L0_attn_a_kv_a_w': _L0_attn_a_in['kv_a_w'], 'L0_attn_a_kv_a_ln_w': _L0_attn_a_in['kv_a_ln_w'], 'L0_attn_a_kv_b_w': _L0_attn_a_in['kv_b_w'], 'L0_attn_a_o_w': _L0_attn_a_in['o_w'], 'L0_attn_b_Wq': _L0_attn_b_in['Wq'], 'L0_attn_b_Wk': _L0_attn_b_in['Wk'], 'L0_attn_b_Wv': _L0_attn_b_in['Wv'], 'L0_attn_b_Wa': _L0_attn_b_in['Wa'], 'L0_attn_b_ba': _L0_attn_b_in['ba'], 'L0_attn_b_Wb': _L0_attn_b_in['Wb'], 'L0_attn_b_bb': _L0_attn_b_in['bb'], 'L0_attn_b_Wg': _L0_attn_b_in['Wg'], 'L0_attn_b_Wo': _L0_attn_b_in['Wo'], 'L0_attn_b_conv_q_w': _L0_attn_b_in['conv_q_w'], 'L0_attn_b_conv_q_b': _L0_attn_b_in['conv_q_b'], 'L0_attn_b_conv_k_w': _L0_attn_b_in['conv_k_w'], 'L0_attn_b_conv_k_b': _L0_attn_b_in['conv_k_b'], 'L0_attn_b_conv_v_w': _L0_attn_b_in['conv_v_w'], 'L0_attn_b_conv_v_b': _L0_attn_b_in['conv_v_b'], 'L0_attn_b_ln_w': _L0_attn_b_in['ln_w'], 'L0_attn_b_ln_b': _L0_attn_b_in['ln_b'], 'L0_ffn_weight': _L0_ffn_in['weight'], 'L0_ffn_bias': _L0_ffn_in['bias'], 'L1_attn_a_Wq_a': _L1_attn_a_in['Wq_a'], 'L1_attn_a_q_norm_w': _L1_attn_a_in['q_norm_w'], 'L1_attn_a_Wq_b': _L1_attn_a_in['Wq_b'], 'L1_attn_a_Wk_rope': _L1_attn_a_in['Wk_rope'], 'L1_attn_a_Wkv_a': _L1_attn_a_in['Wkv_a'], 'L1_attn_a_kv_norm_w': _L1_attn_a_in['kv_norm_w'], 'L1_attn_a_Wkv_b': _L1_attn_a_in['Wkv_b'], 'L1_attn_a_Wo': _L1_attn_a_in['Wo'], 'L1_attn_b_Wq': _L1_attn_b_in['Wq'], 'L1_attn_b_bq': _L1_attn_b_in['bq'], 'L1_attn_b_Wk': _L1_attn_b_in['Wk'], 'L1_attn_b_bk': _L1_attn_b_in['bk'], 'L1_attn_b_Wv': _L1_attn_b_in['Wv'], 'L1_attn_b_bv': _L1_attn_b_in['bv'], 'L1_attn_b_Wo': _L1_attn_b_in['Wo'], 'L1_attn_b_bo': _L1_attn_b_in['bo'], 'L1_ffn_ln1_w': _L1_ffn_in['ln1_w'], 'L1_ffn_ln2_w': _L1_ffn_in['ln2_w'], 'L1_ffn_Wq': _L1_ffn_in['Wq'], 'L1_ffn_Wk': _L1_ffn_in['Wk'], 'L1_ffn_Wv': _L1_ffn_in['Wv'], 'L1_ffn_Wo': _L1_ffn_in['Wo'], 'L1_ffn_A': _L1_ffn_in['A'], 'L1_ffn_B': _L1_ffn_in['B'], 'L1_ffn_W_in_base': _L1_ffn_in['W_in_base'], 'L1_ffn_W_up_base': _L1_ffn_in['W_up_base'], 'L1_ffn_W_down': _L1_ffn_in['W_down']}
    _x0 = _d['L0_attn_a_hidden_states']
    _d['L0_attn_a_hidden_states'] = jax.random.normal(jax.random.fold_in(jax.random.key(seed), 1), (8, 256, 256), dtype=_x0.dtype)
    del _x0
    return _d

def reference(L0_attn_a_hidden_states, L0_attn_a_q_a_w, L0_attn_a_q_a_ln_w, L0_attn_a_q_b_w, L0_attn_a_kv_a_w, L0_attn_a_kv_a_ln_w, L0_attn_a_kv_b_w, L0_attn_a_o_w, L0_attn_b_Wq, L0_attn_b_Wk, L0_attn_b_Wv, L0_attn_b_Wa, L0_attn_b_ba, L0_attn_b_Wb, L0_attn_b_bb, L0_attn_b_Wg, L0_attn_b_Wo, L0_attn_b_conv_q_w, L0_attn_b_conv_q_b, L0_attn_b_conv_k_w, L0_attn_b_conv_k_b, L0_attn_b_conv_v_w, L0_attn_b_conv_v_b, L0_attn_b_ln_w, L0_attn_b_ln_b, L0_ffn_weight, L0_ffn_bias, L1_attn_a_Wq_a, L1_attn_a_q_norm_w, L1_attn_a_Wq_b, L1_attn_a_Wk_rope, L1_attn_a_Wkv_a, L1_attn_a_kv_norm_w, L1_attn_a_Wkv_b, L1_attn_a_Wo, L1_attn_b_Wq, L1_attn_b_bq, L1_attn_b_Wk, L1_attn_b_bk, L1_attn_b_Wv, L1_attn_b_bv, L1_attn_b_Wo, L1_attn_b_bo, L1_ffn_ln1_w, L1_ffn_ln2_w, L1_ffn_Wq, L1_ffn_Wk, L1_ffn_Wv, L1_ffn_Wo, L1_ffn_A, L1_ffn_B, L1_ffn_W_in_base, L1_ffn_W_up_base, L1_ffn_W_down):

    def _L0_attn_a_ref(hidden_states, q_a_w, q_a_ln_w, q_b_w, kv_a_w, kv_a_ln_w, kv_b_w, o_w):
        import jax, jax.numpy as jnp
        import numpy as np
        EPS = 1e-06
        H, NOPE, ROPE, VD = (16, 128, 64, 128)
        QHD = NOPE + ROPE
        SCALE = QHD ** (-0.5)
        THETA = 10000.0

        def rmsnorm(x, w):
            x32 = x.astype(jnp.float32)
            var = jnp.mean(x32 * x32, axis=-1, keepdims=True)
            return (w * (x32 * jax.lax.rsqrt(var + EPS))).astype(x.dtype)

        def rope_cos_sin(seq_len):
            inv_freq = 1.0 / THETA ** (jnp.arange(0, ROPE, 2, dtype=jnp.float32) / ROPE)
            t = jnp.arange(seq_len, dtype=jnp.float32)
            freqs = jnp.outer(t, inv_freq)
            emb = jnp.concatenate([freqs, freqs], -1)
            return (jnp.cos(emb), jnp.sin(emb))

        def rotate_half(x):
            x1, x2 = (x[..., :x.shape[-1] // 2], x[..., x.shape[-1] // 2:])
            return jnp.concatenate([-x2, x1], axis=-1)
        B, S, D = hidden_states.shape
        q_a = hidden_states @ q_a_w.T
        q = rmsnorm(q_a, q_a_ln_w) @ q_b_w.T
        q = q.reshape(B, S, H, QHD).transpose(0, 2, 1, 3)
        q_nope, q_pe = (q[..., :NOPE], q[..., NOPE:])
        ckv_full = hidden_states @ kv_a_w.T
        ckv, k_pe_raw = (ckv_full[..., :64], ckv_full[..., 64:])
        kv = rmsnorm(ckv, kv_a_ln_w) @ kv_b_w.T
        kv = kv.reshape(B, S, H, NOPE + VD).transpose(0, 2, 1, 3)
        k_nope, v = (kv[..., :NOPE], kv[..., NOPE:])
        k_pe = k_pe_raw.reshape(B, 1, S, ROPE)
        cos, sin = rope_cos_sin(S)
        cos, sin = (cos[None, None], sin[None, None])
        q_pe = q_pe * cos + rotate_half(q_pe) * sin
        k_pe = k_pe * cos + rotate_half(k_pe) * sin
        query = jnp.concatenate([q_nope, q_pe], -1)
        key_s = jnp.concatenate([k_nope, jnp.broadcast_to(k_pe, (B, H, S, ROPE))], -1)
        scores = jnp.einsum('bhqd,bhkd->bhqk', query, key_s) * SCALE
        causal = jnp.tril(jnp.ones((S, S), bool))
        scores = jnp.where(causal[None, None], scores, -jnp.inf)
        probs = jax.nn.softmax(scores.astype(jnp.float32), axis=-1).astype(query.dtype)
        attn = jnp.einsum('bhqk,bhkd->bhqd', probs, v)
        attn = attn.transpose(0, 2, 1, 3).reshape(B, S, H * VD)
        return attn @ o_w.T

    def _L0_attn_b_ref(x, Wq, Wk, Wv, Wa, ba, Wb, bb, Wg, Wo, conv_q_w, conv_q_b, conv_k_w, conv_k_b, conv_v_w, conv_v_b, ln_w, ln_b):
        import jax, jax.numpy as jnp
        import numpy as np
        HID, H, DK, DV, KS = (256, 16, 128, 128, 4)

        def _p(key, shape, scale=0.02):
            return jax.random.normal(key, shape, dtype=jnp.float32) * scale

        def _dwconv_causal(y, w, b):
            out = jax.lax.conv_general_dilated(y.transpose(0, 2, 1), w, window_strides=(1,), padding=[(KS - 1, 0)], feature_group_count=w.shape[0])
            return out.transpose(0, 2, 1) + b

        def _silu(x):
            return x * jax.nn.sigmoid(x)

        def _gated_delta(q, k, v, alpha, beta, scale):
            B, T, nH, _ = q.shape
            qs = q.transpose(1, 0, 2, 3)
            ks = k.transpose(1, 0, 2, 3) * scale
            vs = v.transpose(1, 0, 2, 3)
            al = alpha.transpose(1, 0, 2)
            be = beta.transpose(1, 0, 2)

            def step(S, inp):
                qt, kt, vt, at, bt = inp
                err = jnp.einsum('bhvk,bhk->bhv', S, kt) - vt
                S = at[..., None, None] * S - bt[..., None, None] * err[..., None] * kt[:, :, None, :]
                o = jnp.einsum('bhvk,bhk->bhv', S, qt)
                return (S, o)
            S0 = jnp.zeros((B, nH, DV, DK), dtype=q.dtype)
            _, o = jax.lax.scan(step, S0, (qs, ks, vs, al, be))
            return o.transpose(1, 0, 2, 3)
        B, T, _ = x.shape
        scale = DK ** (-0.5)
        q = _silu(_dwconv_causal(x @ Wq, conv_q_w, conv_q_b))
        k = _silu(_dwconv_causal(x @ Wk, conv_k_w, conv_k_b))
        v = _silu(_dwconv_causal(x @ Wv, conv_v_w, conv_v_b))
        q = q.reshape(B, T, H, DK)
        k = k.reshape(B, T, H, DK)
        v = v.reshape(B, T, H, DV)
        alpha = jax.nn.sigmoid(x @ Wa + ba)
        beta = jax.nn.sigmoid(x @ Wb + bb)
        o = _gated_delta(q, k, v, alpha, beta, scale)
        mu = o.mean(-1, keepdims=True)
        var = ((o - mu) ** 2).mean(-1, keepdims=True)
        o = (o - mu) * jax.lax.rsqrt(var + 1e-05) * ln_w + ln_b
        g = jax.nn.sigmoid(x @ Wg).reshape(B, T, H, DV)
        o = (o * g).reshape(B, T, H * DV)
        return o @ Wo

    def _L0_ffn_ref(x, weight, bias):
        import jax, jax.numpy as jnp
        import numpy as np
        B, S, D_IN, D_OUT = (4, 256, 256, 256)
        EPS = 1e-10
        scale = jnp.mean(jnp.abs(weight))
        w_t = jnp.clip(jnp.round(weight / (scale + EPS)), -1.0, 1.0)
        w_ste = weight + jax.lax.stop_gradient(w_t * scale - weight)
        return jnp.einsum('bsi,oi->bso', x, w_ste) + bias

    def _L1_attn_a_ref(hidden_states, Wq_a, q_norm_w, Wq_b, Wk_rope, Wkv_a, kv_norm_w, Wkv_b, Wo):
        import jax, jax.numpy as jnp
        import numpy as np
        H = 16
        D_NOPE = 128
        D_ROPE = 64
        D_QK = 192
        D_V = 128
        THETA = 10000.0
        EPS = 1e-06

        def rmsnorm(x, w):
            x32 = x.astype(jnp.float32)
            x32 = x32 * jax.lax.rsqrt(jnp.mean(x32 * x32, axis=-1, keepdims=True) + EPS)
            return (x32 * w).astype(x.dtype)

        def rope_cos_sin(seq_len, dim, dtype):
            inv_freq = 1.0 / THETA ** (jnp.arange(0, dim, 2, dtype=jnp.float32) / dim)
            t = jnp.arange(seq_len, dtype=jnp.float32)
            freqs = jnp.outer(t, inv_freq)
            return (jnp.cos(freqs).astype(dtype), jnp.sin(freqs).astype(dtype))

        def apply_rope(x, cos, sin):
            d2 = x.shape[-1] // 2
            x1, x2 = (x[..., :d2], x[..., d2:])
            c = cos[None, :, None, :]
            s = sin[None, :, None, :]
            return jnp.concatenate([x1 * c - x2 * s, x2 * c + x1 * s], axis=-1)
        B, T, D = hidden_states.shape
        q = rmsnorm(hidden_states @ Wq_a, q_norm_w) @ Wq_b
        q = q.reshape(B, T, H, D_QK)
        q_pass, q_rot = (q[..., :D_NOPE], q[..., D_NOPE:])
        kv = rmsnorm(hidden_states @ Wkv_a, kv_norm_w) @ Wkv_b
        kv = kv.reshape(B, T, H, D_NOPE + D_V)
        k_pass, v = (kv[..., :D_NOPE], kv[..., D_NOPE:])
        k_rot = (hidden_states @ Wk_rope)[:, :, None, :]
        cos, sin = rope_cos_sin(T, D_ROPE, hidden_states.dtype)
        q_rot = apply_rope(q_rot, cos, sin)
        k_rot = apply_rope(k_rot, cos, sin)
        k_rot = jnp.broadcast_to(k_rot, (B, T, H, D_ROPE))
        qf = jnp.concatenate([q_pass, q_rot], axis=-1)
        kf = jnp.concatenate([k_pass, k_rot], axis=-1)
        scale = 1.0 / np.sqrt(D_QK)
        scores = jnp.einsum('bqhd,bkhd->bhqk', qf, kf) * scale
        mask = jnp.tril(jnp.ones((T, T), dtype=bool))
        scores = jnp.where(mask[None, None], scores, jnp.finfo(scores.dtype).min)
        p = jax.nn.softmax(scores, axis=-1)
        o = jnp.einsum('bhqk,bkhd->bqhd', p, v)
        o = o.reshape(B, T, H * D_V) @ Wo
        return o

    def _L1_attn_b_ref(x, Wq, bq, Wk, bk, Wv, bv, Wo, bo):
        import jax, jax.numpy as jnp
        import numpy as np
        B, T, E, H = (2, 256, 256, 16)
        D = E // H
        ROPE_BASE = 10000.0

        def _rope(x):
            t, d = (x.shape[-2], x.shape[-1])
            j = jnp.arange(d // 2, dtype=x.dtype)
            thetas = ROPE_BASE ** (-2.0 * j / d)
            m = jnp.arange(1, t + 1, dtype=x.dtype)
            ang = m[:, None] * thetas[None, :]
            C = jnp.concatenate([ang, ang], axis=-1)
            x_rot = jnp.concatenate([-x[..., d // 2:], x[..., :d // 2]], axis=-1)
            return x * jnp.cos(C) + x_rot * jnp.sin(C)
        b, t, e = x.shape

        def proj(W, bias):
            y = jnp.einsum('bte,fe->btf', x, W) + bias
            return y.reshape(b, t, H, D).transpose(0, 2, 1, 3)
        q = _rope(proj(Wq, bq))
        k = _rope(proj(Wk, bk))
        v = proj(Wv, bv)
        scale = jnp.sqrt(jnp.asarray(D, x.dtype))
        att = jnp.einsum('bhqd,bhkd->bhqk', q, k) / scale
        causal = jnp.tril(jnp.ones((t, t), bool))
        att = jnp.where(causal, att, -jnp.inf)
        att = jax.nn.softmax(att, axis=-1)
        y = jnp.einsum('bhqk,bhkd->bhqd', att, v)
        y = y.transpose(0, 2, 1, 3).reshape(b, t, e)
        y = jnp.einsum('bte,fe->btf', y, Wo) + bo
        return y

    def _L1_ffn_ref(hidden_states, ln1_w, ln2_w, Wq, Wk, Wv, Wo, A, B, W_in_base, W_up_base, W_down):
        import jax, jax.numpy as jnp
        import numpy as np
        B_, S, D = (2, 256, 256)
        F_ = 1024
        R = 16
        H = 16
        HD = D // H
        MOD_SCALE = 0.1
        EPS = 1e-06

        def _rmsnorm(x, w):
            v = jnp.mean(x * x, axis=-1, keepdims=True)
            return x * jax.lax.rsqrt(v + EPS) * w

        def _attention(x, Wq, Wk, Wv, Wo):
            b, s, d = x.shape
            q = (x @ Wq.T).reshape(b, s, H, HD)
            k = (x @ Wk.T).reshape(b, s, H, HD)
            v = (x @ Wv.T).reshape(b, s, H, HD)
            scores = jnp.einsum('bqhd,bkhd->bhqk', q, k) / np.sqrt(HD).astype(np.float32)
            causal = jnp.tril(jnp.ones((s, s), bool))
            scores = jnp.where(causal, scores, jnp.finfo(scores.dtype).min)
            probs = jax.nn.softmax(scores, axis=-1)
            out = jnp.einsum('bhqk,bkhd->bqhd', probs, v).reshape(b, s, d)
            return out @ Wo.T
        residual = hidden_states
        x = _rmsnorm(hidden_states, ln1_w)
        attn = _attention(x, Wq, Wk, Wv, Wo)
        mod = MOD_SCALE * jnp.tanh(attn @ A)
        h = _rmsnorm(residual, ln2_w)
        gate_pre = h @ W_in_base.T + mod * (h @ A) @ B
        gate = jax.nn.silu(gate_pre)
        up = h @ W_up_base.T
        mlp_out = gate * up @ W_down.T
        return residual + mlp_out
    x = L0_attn_a_hidden_states
    x = x + _L0_attn_a_ref(_layernorm(x, axis=-1), L0_attn_a_q_a_w, L0_attn_a_q_a_ln_w, L0_attn_a_q_b_w, L0_attn_a_kv_a_w, L0_attn_a_kv_a_ln_w, L0_attn_a_kv_b_w, L0_attn_a_o_w)
    x = x + _L0_ffn_ref(_layernorm(x, axis=-1), L0_ffn_weight, L0_ffn_bias)
    x = x + _L0_attn_b_ref(_layernorm(x, axis=-1), L0_attn_b_Wq, L0_attn_b_Wk, L0_attn_b_Wv, L0_attn_b_Wa, L0_attn_b_ba, L0_attn_b_Wb, L0_attn_b_bb, L0_attn_b_Wg, L0_attn_b_Wo, L0_attn_b_conv_q_w, L0_attn_b_conv_q_b, L0_attn_b_conv_k_w, L0_attn_b_conv_k_b, L0_attn_b_conv_v_w, L0_attn_b_conv_v_b, L0_attn_b_ln_w, L0_attn_b_ln_b)
    x = x + _L0_ffn_ref(_layernorm(x, axis=-1), L0_ffn_weight, L0_ffn_bias)
    x = x + _L1_attn_a_ref(_layernorm(x, axis=-1), L1_attn_a_Wq_a, L1_attn_a_q_norm_w, L1_attn_a_Wq_b, L1_attn_a_Wk_rope, L1_attn_a_Wkv_a, L1_attn_a_kv_norm_w, L1_attn_a_Wkv_b, L1_attn_a_Wo)
    x = x + _L1_ffn_ref(_layernorm(x, axis=-1), L1_ffn_ln1_w, L1_ffn_ln2_w, L1_ffn_Wq, L1_ffn_Wk, L1_ffn_Wv, L1_ffn_Wo, L1_ffn_A, L1_ffn_B, L1_ffn_W_in_base, L1_ffn_W_up_base, L1_ffn_W_down)
    x = x + _L1_attn_b_ref(_layernorm(x, axis=-1), L1_attn_b_Wq, L1_attn_b_bq, L1_attn_b_Wk, L1_attn_b_bk, L1_attn_b_Wv, L1_attn_b_bv, L1_attn_b_Wo, L1_attn_b_bo)
    x = x + _L1_ffn_ref(_layernorm(x, axis=-1), L1_ffn_ln1_w, L1_ffn_ln2_w, L1_ffn_Wq, L1_ffn_Wk, L1_ffn_Wv, L1_ffn_Wo, L1_ffn_A, L1_ffn_B, L1_ffn_W_in_base, L1_ffn_W_up_base, L1_ffn_W_down)
    return x

_drawn_inputs = setup_inputs


def setup_inputs(seed=0):
    import zlib

    import numpy as np

    out = dict(_drawn_inputs(seed))
    spreads = {'L0_attn_a_q_a_ln_w': (1.0, 0.6),
     'L0_attn_a_kv_a_ln_w': (1.0, 0.6),
     'L0_attn_b_ba': (0.0, 2.0),
     'L0_attn_b_bb': (0.0, 0.8),
     'L0_attn_b_conv_q_b': (0.0, 0.1),
     'L0_attn_b_conv_k_b': (0.0, 0.1),
     'L0_attn_b_conv_v_b': (0.0, 0.1),
     'L0_attn_b_ln_w': (1.0, 0.6),
     'L0_attn_b_ln_b': (0.0, 0.1),
     'L1_attn_a_q_norm_w': (1.0, 0.2),
     'L1_attn_a_kv_norm_w': (1.0, 0.2),
     'L1_ffn_ln1_w': (1.0, 0.6),
     'L1_ffn_ln2_w': (1.0, 0.6)}
    factors = {'L0_attn_a_q_a_w': 8.0,
     'L0_attn_a_q_b_w': 8.0,
     'L0_attn_b_Wa': 5.863,
     'L0_attn_b_Wb': 3.866,
     'L0_attn_b_Wg': 3.1,
     'L1_attn_b_bq': 8.0,
     'L1_attn_b_bk': 8.0,
     'L1_ffn_Wq': 200.0,
     'L1_ffn_Wk': 200.0,
     'L1_ffn_Wv': 200.0,
     'L1_ffn_Wo': 200.0,
     'L1_ffn_A': 200.0,
     'L1_ffn_B': 200.0}
    for name, (base, spread) in spreads.items():
        noise = np.random.default_rng([zlib.crc32(name.encode()), seed]).standard_normal(out[name].shape)
        drawn = base * np.exp(spread * noise) if base else spread * noise
        out[name] = jnp.asarray(drawn.astype(out[name].dtype))
    for name, factor in factors.items():
        out[name] = (out[name] * factor).astype(out[name].dtype)
    return out
```

```python
import concourse.bass as bass
from concourse import mybir
from contextlib import ExitStack

F32 = mybir.dt.float32
BF16 = mybir.dt.bfloat16
ALU = mybir.AluOpType
ACT = mybir.ActivationFunctionType
AX = mybir.AxisListType

P = 128
NB = 8
T = 256
NT = T // P
D = 256
KC = D // P
H = 16
STAGES = ['mla0', 'ffn0', 'delta', 'ffn1', 'mla1', 'l1ffn', 'l1b', 'l1ffn']
MASKED = -1.0e30


class Signal:

    def __init__(self, ctx, nc, name, per):
        self.sem = ctx.enter_context(nc.semaphore(name))
        self.per, self.base = per, 0

    def prime(self, eng, iterations):
        eng.sem_inc(self.sem, iterations * self.per)

    def __call__(self, it, k):
        return self.sem, it * self.per + (self.base + 2 * self.per + k)

    def ran(self, iterations):
        self.base += iterations * self.per


class Core:

    def __init__(self, ctx, nc, ins, loaded):
        def sb(name, shape, dt=F32):
            return ctx.enter_context(nc.sbuf_tensor(name, shape, dt))

        self.nc, self.ins, self.ctx = nc, ins, ctx
        self.x = sb("x", [P, NB + 1, NT, D])
        self.ident = sb("ident", [P, P])
        self.ident_bf = sb("ident_bf", [P, P], BF16)
        self.mask_bf = sb("mask_bf", [P, 2 * P], BF16)
        self.mask_f = sb("mask_f", [P, P])
        self.minus_half = sb("minus_half", [P, 16])
        self.ones_row = sb("ones_row", [1, T])
        self.stats = sb("stats", [P, NT, 6])
        self.mean_var = sb("mean_var", [P, NT, 2])
        self.carrier = sb("carrier", [P, 1])
        self.var_eps = sb("var_eps", [P, NT])
        self.rstd = sb("rstd", [P, NT])
        self.xn = sb("xn", [P, NT, D])
        self.xnT = sb("xnT", [P, KC, T])
        self.bank = [ctx.enter_context(nc.psum_tensor(f"bank{i}", [P, 512], F32)) for i in range(8)]
        self.ready = ctx.enter_context(nc.semaphore("constants_ready"))
        self.weights_in = ctx.enter_context(nc.semaphore("weights_in"))
        self.weights_count = 0
        self.steps = ctx.enter_context(nc.semaphore("setup_steps"))
        self.steps_count = 0
        sig = lambda name, per: Signal(ctx, nc, name, per)
        self.ln_stats = sig("ln_stats", NT)
        self.ln_mv = sig("ln_mv", NT)
        self.ln_var = sig("ln_var", 1)
        self.ln_rstd = sig("ln_rstd", 1)
        self.ln_out = sig("ln_out", NT)
        self.xnT_in_psum = sig("xnT_in_psum", 1)
        self.xnT_ready = sig("xnT_ready", 1)
        self.x_updated = sig("x_updated", 1)

    def ln_ran(self):
        for s in (self.ln_stats, self.ln_mv, self.ln_var, self.ln_rstd, self.ln_out,
                  self.xnT_in_psum, self.xnT_ready):
            s.ran(NB + 1)
        self.x_updated.ran(NB)


def load_inputs(core):
    nc, ins = core.nc, core.ins
    with nc.Block() as block:
        @block.sync
        def _(sp):
            for b in range(NB):
                sp.dma_start(core.x[:, b], ins["x"][b]).then_inc(core.ready, 16)
            sp.dma_start(core.ident[:], ins["ident"][:]).then_inc(core.ready, 16)
            sp.dma_start(core.mask_f[:], ins["mask"][:]).then_inc(core.ready, 16)
            sp.wait_ge(core.ready, 16 * (NB + 2))

        @block.vector
        def _(dve):
            for s in (core.ln_stats, core.ln_mv, core.ln_var, core.ln_out):
                s.prime(dve, 1)
            core.x_updated.prime(dve, 2)
            dve.wait_ge(core.ready, 16 * (NB + 2))
            nc.vector.tensor_copy(core.ident_bf[:], core.ident[:])
            nc.vector.memset(core.mask_bf[:, 0:P], 0.0)
            nc.vector.tensor_copy(core.mask_bf[:, P:2 * P], core.mask_f[:])

        @block.gpsimd
        def _(pool):
            core.ln_rstd.prime(pool, 1)
            nc.gpsimd.memset(core.x[:, NB], 0.0)
            nc.gpsimd.memset(core.minus_half[:], -0.5)
            nc.gpsimd.memset(core.ones_row[:], 1.0)

        @block.scalar
        def _(act):
            core.xnT_ready.prime(act, 1)

        @block.tensor
        def _(pe):
            core.xnT_in_psum.prime(pe, 1)



def ln_stats_dve(core, dve, it, b):
    nc = core.nc
    for t in range(NT):
        nc.vector.bn_stats(core.stats[:, t], core.x[:, b, t]).then_inc(core.ln_stats.sem, 1)
    dve.wait_ge(*core.ln_stats(it, NT))
    nc.vector.memset(core.carrier[:], 0.0)
    for t in range(NT):
        nc.vector.bn_aggr(core.mean_var[:, t], core.stats[:, t]).then_inc(core.ln_mv.sem, 1)
    dve.wait_ge(*core.ln_mv(it, NT))
    nc.vector.tensor_scalar(core.var_eps[:], core.mean_var[:, :, 1], 1e-5, None,
                            ALU.add).then_inc(core.ln_var.sem, 1)


def ln_normalize_dve(core, dve, it, b):
    nc = core.nc
    dve.wait_ge(*core.ln_rstd(it, 1))
    dve.wait_ge(*core.xnT_in_psum(it, 0))
    for t in range(NT):
        nc.vector.tensor_scalar(core.xn[:, t], core.x[:, b, t], core.mean_var[:, t, 0:1],
                                core.rstd[:, t:t + 1], ALU.subtract,
                                ALU.mult).then_inc(core.ln_out.sem, 1)


def ln_rstd_pool(core, pool, it):
    pool.wait_ge(*core.ln_var(it, 1))
    pool.wait_ge(*core.ln_out(it, 0))
    core.nc.gpsimd.tensor_tensor(core.rstd[:], core.var_eps[:], core.minus_half[:, 0:NT],
                                 ALU.pow).then_inc(core.ln_rstd.sem, 1)


def transpose_tokens_pe(core, bank, src, ready, it):
    out = bank[:, :].rearrange("p (c t) -> p c t", c=KC)
    for t in range(NT):
        for c in range(KC):
            last = core.nc.tensor.transpose(out[:, c, t * P:(t + 1) * P], src[:, t, c * P:(c + 1) * P],
                                            core.ident[:])
    return last



QL = 192
QL1 = QL - P
CL = 64
R = 64
LAT = QL + CL + 2 * R
PAIRS = H // 2


class Mla:
    def __init__(self, ctx, core):
        nc = core.nc
        sig = lambda name, per: Signal(ctx, nc, name, per)
        self.lat_in_psum = sig("lat_in_psum", NT)
        self.lat_ready = sig("lat_ready", NT)
        self.squares_ready = sig("squares_ready", 2 * NT)
        self.ms_ready = sig("ms_ready", 1)
        self.ms_eps_ready = sig("ms_eps_ready", 1)
        self.rms_pow = sig("rms_pow", 1)
        self.rms_ready = sig("rms_ready", 1)
        self.norm_ready = sig("norm_ready", 2 * NT)
        self.kpe_products = sig("kpe_products", 2)
        self.kpe_ready = sig("kpe_ready", 1)
        self.latT_in_psum = sig("latT_in_psum", 2)
        self.latT_ready = sig("latT_ready", 2)
        self.v_ready = sig("v_ready", 1)
        self.q_in_psum = sig("q_in_psum", PAIRS)
        self.q_cos = sig("q_cos", PAIRS)
        self.q_sin = sig("q_sin", PAIRS)
        self.q_abs_ready = sig("q_abs_ready", PAIRS)
        self.q_rope_ready = sig("q_rope_ready", PAIRS)
        self.pv_in_psum = sig("pv_in_psum", PAIRS)
        self.recip_ready = sig("recip_ready", PAIRS)
        self.o_ready = sig("o_ready", PAIRS)
        self.oT_in_psum = sig("oT_in_psum", PAIRS)
        self.oT_ready = sig("oT_ready", PAIRS)
        self.y_done = sig("y_done", PAIRS)
        self.prep = [self.lat_in_psum, self.lat_ready, self.squares_ready, self.ms_ready,
                     self.ms_eps_ready, self.rms_pow, self.rms_ready, self.norm_ready,
                     self.kpe_products, self.kpe_ready, self.latT_in_psum, self.latT_ready,
                     self.v_ready]
        self.loop = [self.q_in_psum, self.q_cos, self.q_sin, self.q_abs_ready, self.q_rope_ready,
                     self.pv_in_psum, self.recip_ready, self.o_ready, self.oT_in_psum,
                     self.oT_ready, self.y_done]


class Softmax:

    def __init__(self, ctx, core):
        nc = core.nc
        self.scores_in_psum = Signal(ctx, nc, "scores_in_psum", H)
        self.max_ready = Signal(ctx, nc, "max_ready", H)
        self.probs_ready = Signal(ctx, nc, "probs_ready", H)
        self.probsT_in_psum = Signal(ctx, nc, "probsT_in_psum", H)
        self.probsT_ready = Signal(ctx, nc, "probsT_ready", H)
        self.pv_done = Signal(ctx, nc, "pv_done", H)
        self.loop = [self.scores_in_psum, self.max_ready, self.probs_ready, self.probsT_in_psum,
                     self.probsT_ready, self.pv_done]


def prime_signals(core, prepared, looped):
    with core.nc.Block() as block:
        @block.gpsimd
        def _(pool):
            for s in prepared:
                s.prime(pool, 1)
            for s in looped:
                s.prime(pool, 2)


SCORE_COLS = 3 * P


def scores_pe(core, pe, sm, it, h, banks, q, k):
    nc = core.nc
    bank = banks[h % 2]
    pe.wait_ge(*sm.probs_ready(it, h - 1))
    nc.tensor.matmul(bank[:, 0:P], q(0), k(P), start=True, stop=False)
    nc.tensor.matmul(bank[:, 0:P], core.ident_bf[:], core.mask_bf[:, P:2 * P], start=False,
                     stop=True)
    nc.tensor.matmul(bank[:, P:3 * P], q(1), k(2 * P), start=True, stop=False)
    nc.tensor.matmul(bank[:, P:3 * P], core.ident_bf[:], core.mask_bf[:], start=False,
                     stop=True).then_inc(sm.scores_in_psum.sem, 1)


def max_dve(core, dve, sm, it, h, banks, nmax):
    nc = core.nc
    bank = banks[h % 2]
    dve.wait_ge(*sm.scores_in_psum(it, h + 1))
    dve.wait_ge(*sm.probs_ready(it, h - 1))
    nc.vector.tensor_reduce(nmax[:, h % 2, 0:1], bank[:, 0:P], AX.X, ALU.max, negate=True)
    nc.vector.tensor_reduce(nmax[:, h % 2, 1:2], bank[:, P:3 * P], AX.X, ALU.max,
                            negate=True).then_inc(sm.max_ready.sem, 1)


def exp_act(core, act, sm, it, h, banks, nmax, probs, sums, sums_free):
    nc = core.nc
    bank = banks[h % 2]
    act.wait_ge(*sm.max_ready(it, h + 1))
    act.wait_ge(*sm.probsT_in_psum(it, h - 1))
    act.wait_ge(*sums_free)
    nc.scalar.activation(probs[:, h % 2, 0:P], bank[:, 0:P], ACT.Exp, bias=nmax[:, h % 2, 0:1],
                         accum_out=sums[:, h, 0:1])
    nc.scalar.activation(probs[:, h % 2, P:3 * P], bank[:, P:3 * P], ACT.Exp,
                         bias=nmax[:, h % 2, 1:2],
                         accum_out=sums[:, h, 1:2]).then_inc(sm.probs_ready.sem, 1)


def transpose_probs_pe(core, pe, sm, it, h, bank, probs):
    nc = core.nc
    pe.wait_ge(*sm.probs_ready(it, h + 1))
    pe.wait_ge(*sm.probsT_ready(it, h))
    for j in range(3):
        last = nc.tensor.transpose(bank[:, j * P:(j + 1) * P], probs[:, h % 2, j * P:(j + 1) * P],
                                   core.ident[:])
    last.then_inc(sm.probsT_in_psum.sem, 1)


def probsT_act(core, act, sm, it, h, bank, probsT):
    act.wait_ge(*sm.probsT_in_psum(it, h + 1))
    act.wait_ge(*sm.pv_done(it, h - 1))
    core.nc.scalar.copy(probsT[:, h % 2], bank[:, 0:SCORE_COLS]).then_inc(sm.probsT_ready.sem, 1)


def pv_pe(core, pe, sm, it, h, probsT, out, v):
    nc = core.nc
    pe.wait_ge(*sm.probsT_ready(it, h + 1))
    nc.tensor.matmul(out(0), probsT[:, h % 2, 0:P], v(0), start=True, stop=True)
    nc.tensor.matmul(out(1), probsT[:, h % 2, P:2 * P], v(0), start=True, stop=False)
    last = nc.tensor.matmul(out(1), probsT[:, h % 2, 2 * P:3 * P], v(1), start=False, stop=True)
    last.then_inc(sm.pv_done.sem, 1)
    return last


def mla_sublayer(core, sm, g, tag):
    nc, ins = core.nc, core.ins
    with ExitStack() as ctx:
        def sb(name, shape, dt=F32):
            return ctx.enter_context(nc.sbuf_tensor(f"{tag}{name}", shape, dt))

        w_lat = sb("w_lat", [P, KC, LAT])
        norm_w = sb("norm_w", [P, QL + CL])
        wq0 = sb("wq0", [P, H, P])
        wq1 = sb("wq1", [QL1, H, P])
        ws0 = sb("ws0", [P, H, R])
        ws1 = sb("ws1", [QL1, H, R])
        w_out = sb("w_out", [P, PAIRS, D])
        cosT = sb("cosT", [P, T])
        sinT = sb("sinT", [P, T])
        cos_tok = sb("cos_tok", [P, NT, R])
        sin_tok = sb("sin_tok", [P, NT, R])
        ms_scale = sb("ms_scale", [P, NT, 2])
        q_scale = sb("q_scale", [P, NT, 2])

        with ExitStack() as stage_ctx:
            def stage(name, shape):
                return stage_ctx.enter_context(nc.sbuf_tensor(f"{tag}{name}", shape, F32))
            q_nope = stage("q_nope", [P, H, QL])
            k_nope = stage("k_nope", [P, H, CL])
            w_v = stage("w_v", [P, H, CL])
            w_o = stage("w_o", [P, H, D])
            w0, s0 = core.weights_count, core.steps_count
            loads = [(q_nope[:], "q_nope"), (k_nope[:], "k_nope"), (w_v[:], "w_v"), (w_o[:], "w_o"),
                     (w_lat[:], "w_lat"), (norm_w[:], "norm_w"), (wq0[:, :, CL:P], "q_pe0"),
                     (wq1[:, :, CL:P], "q_pe1"), (ws0[:], "q_swap0"), (ws1[:], "q_swap1")]
            tables = [(cosT[:], "cosT"), (sinT[:], "sinT"), (cos_tok[:], "cos_tok"),
                      (sin_tok[:], "sin_tok"), (ms_scale[:], "ms_scale"), (q_scale[:], "q_scale")]
            core.weights_count += 16 * (len(loads) + len(tables))
            core.steps_count += 16

            with nc.Block() as block:
                @block.sync
                def _(sp):
                    for dst, name in loads:
                        sp.dma_start(dst, ins[f"{tag}{name}"][:]).then_inc(core.weights_in, 16)
                    for dst, name in tables:
                        sp.dma_start(dst, ins[name][:]).then_inc(core.weights_in, 16)

                @block.tensor
                def _(pe):
                    pe.wait_ge(core.weights_in, core.weights_count)
                    for half in range(2):
                        for c in range(2):
                            m = (P, QL1)[c]
                            for j in range(8):
                                h = half * 8 + j
                                last = nc.tensor.matmul(
                                    core.bank[2 * half + c][0:m, j * CL:(j + 1) * CL],
                                    q_nope[:, h, c * P:c * P + m], k_nope[:, h], start=True, stop=True)
                            last.then_inc(core.steps, 1)
                    for n in range(4):
                        for j in range(4):
                            h = 4 * n + j
                            lo = CL * (h % 2)
                            last = nc.tensor.matmul(
                                core.bank[4 + n][lo:lo + CL, (j // 2) * D:(j // 2 + 1) * D],
                                w_v[:, h], w_o[:, h], start=True, stop=True)
                        last.then_inc(core.steps, 1)

                @block.vector
                def _(dve):
                    for half in range(2):
                        for c, dst in ((0, wq0), (1, wq1)):
                            m = (P, QL1)[c]
                            dve.wait_ge(core.steps, s0 + 2 * half + c + 1)
                            nc.vector.tensor_copy(
                                dst[0:m, half * 8:half * 8 + 8, 0:CL],
                                core.bank[2 * half + c][0:m].rearrange("p (h c) -> p h c", h=8))

                @block.scalar
                def _(act):
                    for n in range(4):
                        act.wait_ge(core.steps, s0 + 5 + n)
                        nc.scalar.copy(w_out[:, 2 * n:2 * n + 2].rearrange("p a b -> p (a b)"),
                                       core.bank[4 + n][:, :])
            core.steps_count = s0 + 8

        lat = sb("lat", [P, NT, LAT])
        squares = sb("squares", [P, NT, QL + CL])
        sumsq = sb("sumsq", [P, NT, 2])
        ms = sb("ms", [P, NT, 2])
        ms_eps = sb("ms_eps", [P, NT, 2])
        inv_rms0 = sb("inv_rms0", [P, NT, 2])
        inv_rms = sb("inv_rms", [P, NT, 2])
        q_tok = sb("q_tok", [P, NT, QL])
        k_tok = sb("k_tok", [P, NT, CL + R])
        k_t1 = sb("k_t1", [P, NT, R])
        k_t2 = sb("k_t2", [P, NT, R])
        latT = sb("latT", [P, 2, T])
        qT1 = sb("qT1", [QL1, T])
        values = sb("values", [P, NT, CL])
        q = sb("q", [P, 2, 2, T])
        rope1 = sb("rope1", [P, 2, T])
        rope2 = sb("rope2", [P, 2, T])
        nmax = sb("nmax", [P, 2, NT])
        sums = sb("sums", [P, H, NT])
        recip = sb("recip", [P, H, NT])
        probs = sb("probs", [P, 2, SCORE_COLS])
        probsT = sb("probsT", [P, 2, SCORE_COLS])
        o = sb("o", [P, 2, NT, 2, CL])
        oT = sb("oT", [P, 2, T])

        b_prep, b_q, b_swap, b_s, b_pT, b_o, b_y = (core.bank[0], core.bank[1], core.bank[2],
                                                    core.bank[3:5], core.bank[5], core.bank[6],
                                                    core.bank[7])
        pv_out = b_o[:, 0:2 * P].rearrange("p (t j c) -> p t j c", t=NT, j=2)

        def prep_rms_dve(dve, it):
            dve.wait_ge(*g.squares_ready(it, 2 * NT))
            nc.vector.tensor_tensor(ms[:], sumsq[:], ms_scale[:], ALU.mult)\
                .then_inc(g.ms_ready.sem, 1)
            dve.wait_ge(*g.ms_ready(it, 1))
            nc.vector.tensor_scalar(ms_eps[:], ms[:], 1e-6, None, ALU.add)\
                .then_inc(g.ms_eps_ready.sem, 1)

        def prep_norm_dve(dve, it):
            dve.wait_ge(*g.rms_ready(it, 1))
            dve.wait_ge(*g.latT_in_psum(it, 0))
            dve.wait_ge(*g.v_ready(it, 0))
            for t in range(NT):
                nc.vector.scalar_tensor_tensor(
                    out=q_tok[:, t], in0=lat[:, t, 0:QL], scalar=inv_rms[:, t, 0:1],
                    in1=norm_w[:, 0:QL], op0=ALU.mult, op1=ALU.mult).then_inc(g.norm_ready.sem, 1)
                nc.vector.scalar_tensor_tensor(
                    out=k_tok[:, t, 0:CL], in0=lat[:, t, QL:QL + CL], scalar=inv_rms[:, t, 1:2],
                    in1=norm_w[:, QL:QL + CL], op0=ALU.mult, op1=ALU.mult)\
                    .then_inc(g.norm_ready.sem, 1)

        def prep_latent_pool(pool, it):
            pool.wait_ge(*g.lat_ready(it, NT))
            nc.gpsimd.tensor_tensor(k_t1[:], lat[:, :, QL + CL:QL + CL + R], cos_tok[:],
                                    ALU.mult).then_inc(g.kpe_products.sem, 1)
            nc.gpsimd.tensor_tensor(k_t2[:], lat[:, :, QL + CL + R:LAT], sin_tok[:],
                                    ALU.mult).then_inc(g.kpe_products.sem, 1)
            pool.wait_ge(*g.kpe_products(it, 2))
            pool.wait_ge(*g.latT_in_psum(it, 0))
            nc.gpsimd.tensor_tensor(k_tok[:, :, CL:CL + R], k_t1[:], k_t2[:], ALU.add)\
                .then_inc(g.kpe_ready.sem, 1)
            pool.wait_ge(*g.ms_eps_ready(it, 1))
            nc.gpsimd.tensor_tensor(inv_rms0[:], ms_eps[:], core.minus_half[:, 0:2 * NT].rearrange(
                "p (t c) -> p t c", t=NT), ALU.pow).then_inc(g.rms_pow.sem, 1)
            pool.wait_ge(*g.rms_pow(it, 1))
            pool.wait_ge(*g.norm_ready(it, 0))
            nc.gpsimd.tensor_tensor(inv_rms[:], inv_rms0[:], q_scale[:], ALU.mult)\
                .then_inc(g.rms_ready.sem, 1)

        def prep_early_pe(pe, it):
            pe.wait_ge(*core.ln_out(it, NT))
            pe.wait_ge(*g.latT_ready(it, 0))
            transpose_tokens_pe(core, b_prep, core.xn, core.ln_out, it)\
                .then_inc(core.xnT_in_psum.sem, 1)
            pe.wait_ge(*core.xnT_ready(it, 1))

        def prep_lat_pe(pe, it):
            for t in range(NT):
                if t > 0:
                    pe.wait_ge(*g.lat_ready(it, t))
                for c in range(KC):
                    last = nc.tensor.matmul(b_prep[:, 0:LAT], core.xnT[:, c, t * P:(t + 1) * P],
                                            w_lat[:, c], start=(c == 0), stop=(c == KC - 1))
                last.then_inc(g.lat_in_psum.sem, 1)

        def prep_early_act(act, it):
            act.wait_ge(*core.xnT_in_psum(it, 1))
            act.wait_ge(*g.lat_in_psum(it, 0))
            nc.scalar.copy(core.xnT[:].rearrange("p c t -> p (c t)"), b_prep[:, :])\
                .then_inc(core.xnT_ready.sem, 1)

        def prep_lat_act(act, it):
            act.wait_ge(*g.norm_ready(it, 0))
            act.wait_ge(*g.kpe_products(it, 0))
            for t in range(NT):
                act.wait_ge(*g.lat_in_psum(it, t + 1))
                nc.scalar.copy(lat[:, t], b_prep[:, 0:LAT]).then_inc(g.lat_ready.sem, 1)
            for t in range(NT):
                act.wait_ge(*g.lat_ready(it, t + 1))
                nc.scalar.activation(squares[:, t, 0:QL], lat[:, t, 0:QL], ACT.Square,
                                     accum_out=sumsq[:, t, 0:1]).then_inc(g.squares_ready.sem, 1)
                nc.scalar.activation(squares[:, t, QL:QL + CL], lat[:, t, QL:QL + CL], ACT.Square,
                                     accum_out=sumsq[:, t, 1:2]).then_inc(g.squares_ready.sem, 1)

        def prep_late_pe(pe, it):
            pe.wait_ge(*g.norm_ready(it, 2 * NT))
            pe.wait_ge(*g.kpe_ready(it, 1))
            pe.wait_ge(*g.lat_ready(it, NT))
            for t in range(NT):
                nc.tensor.transpose(b_prep[:, t * P:(t + 1) * P], q_tok[:, t, 0:P], core.ident[:])
                last = nc.tensor.transpose(b_prep[:, T + t * P:T + (t + 1) * P], k_tok[:, t],
                                           core.ident[:])
            last.then_inc(g.latT_in_psum.sem, 1)
            pe.wait_ge(core.ready, 16)
            pe.wait_ge(*g.latT_ready(it, 1))
            for t in range(NT):
                last = nc.tensor.transpose(b_prep[0:QL1, t * P:(t + 1) * P], q_tok[:, t, P:QL],
                                           core.ident[:])
            last.then_inc(g.latT_in_psum.sem, 1)

        def prep_late_act(act, it, last_scores):
            act.wait_ge(*g.latT_in_psum(it, 1))
            act.wait_ge(*last_scores)
            nc.scalar.copy(latT[:].rearrange("p a t -> p (a t)"), b_prep[:, :])\
                .then_inc(g.latT_ready.sem, 1)
            act.wait_ge(*g.latT_in_psum(it, 2))
            nc.scalar.copy(qT1[:], b_prep[0:QL1, 0:T]).then_inc(g.latT_ready.sem, 1)

        def prep_late_dve(dve, it, last_pv):
            dve.wait_ge(*g.norm_ready(it, 2 * NT))
            dve.wait_ge(*last_pv)
            nc.vector.tensor_copy(values[:], k_tok[:, :, 0:CL]).then_inc(g.v_ready.sem, 1)

        def project_pe(pe, it, p):
            if p == 0:
                pe.wait_ge(*g.latT_ready(it - 1, 2))
            pe.wait_ge(*g.q_cos(it, p))
            pe.wait_ge(*g.q_sin(it, p))
            pe.wait_ge(*g.q_abs_ready(it, p))
            for j in range(2):
                h = 2 * p + j
                out = b_q[:, j * T:(j + 1) * T]
                nc.tensor.matmul(out, wq0[:, h], latT[:, 0], start=True, stop=False)
                nc.tensor.matmul(out, wq1[:, h], qT1[:], start=False, stop=True)
            nc.tensor.matmul(b_swap[:, 0:T], ws0[:, 2 * p:2 * p + 2].rearrange("p a b -> p (a b)"),
                             latT[:, 0], start=True, stop=False)
            nc.tensor.matmul(b_swap[:, 0:T], ws1[:, 2 * p:2 * p + 2].rearrange("p a b -> p (a b)"),
                             qT1[:], start=False, stop=True).then_inc(g.q_in_psum.sem, 1)

        def rope_dve(dve, it, p):
            dve.wait_ge(*g.q_in_psum(it, p + 1))
            dve.wait_ge(*g.q_rope_ready(it, p))
            nc.vector.tensor_tensor(
                rope1[CL:P], b_q[CL:P, :].rearrange("p (j t) -> p j t", j=2),
                cosT[CL:P].rearrange("p (j t) -> p j t", j=1).broadcast_to([R, 2, T]),
                ALU.mult).then_inc(g.q_cos.sem, 1)
            for j in range(2):
                last = nc.vector.tensor_tensor(rope2[CL:P, j], b_swap[j * R:(j + 1) * R, 0:T],
                                               sinT[j * R:(j + 1) * R], ALU.mult)
            last.then_inc(g.q_sin.sem, 1)

        def rope_pool(pool, it, p):
            pool.wait_ge(*g.q_cos(it, p + 1))
            pool.wait_ge(*g.q_sin(it, p + 1))
            pool.wait_ge(*sm.scores_in_psum(it, 2 * p - 2))
            nc.gpsimd.tensor_tensor(q[CL:P, p % 2], rope1[CL:P], rope2[CL:P], ALU.add)\
                .then_inc(g.q_rope_ready.sem, 1)

        def abs_act(act, it, p):
            act.wait_ge(*g.q_in_psum(it, p + 1))
            act.wait_ge(*sm.scores_in_psum(it, 2 * p - 2))
            nc.scalar.copy(q[0:CL, p % 2].rearrange("p j t -> p (j t)"), b_q[0:CL, :])\
                .then_inc(g.q_abs_ready.sem, 1)

        def head_scores_pe(pe, it, h):
            if h % 2 == 0:
                pe.wait_ge(*g.q_abs_ready(it, h // 2 + 1))
                pe.wait_ge(*g.q_rope_ready(it, h // 2 + 1))
            scores_pe(core, pe, sm, it, h, b_s,
                      lambda t: q[:, (h // 2) % 2, h % 2, t * P:(t + 1) * P],
                      lambda n: latT[:, 1, 0:n])

        def head_pv_pe(pe, it, h):
            if h == 0:
                pe.wait_ge(*g.v_ready(it - 1, 1))
            if h % 2 == 0:
                pe.wait_ge(*g.oT_ready(it, h // 2))
            pv_pe(core, pe, sm, it, h, probsT, lambda t: pv_out[:, t, h % 2],
                  lambda kt: values[:, kt])

        def normalise_dve(dve, it, p):
            dve.wait_ge(*sm.pv_done(it, 2 * p + 2))
            nc.vector.reciprocal(recip[:, 2 * p:2 * p + 2], sums[:, 2 * p:2 * p + 2])\
                .then_inc(g.recip_ready.sem, 1)
            dve.wait_ge(*g.recip_ready(it, p + 1))
            dve.wait_ge(*g.oT_in_psum(it, p - 1))
            nc.vector.tensor_tensor(
                o[:, p % 2], pv_out,
                recip[:, 2 * p:2 * p + 2].rearrange("p j (t c) -> p t j c", c=1)
                .broadcast_to([P, NT, 2, CL]), ALU.mult).then_inc(g.o_ready.sem, 1)

        def transpose_o_pe(pe, it, p):
            pe.wait_ge(*g.o_ready(it, p + 1))
            for t in range(NT):
                last = nc.tensor.transpose(b_o[:, T + t * P:T + (t + 1) * P],
                                           o[:, p % 2, t].rearrange("p j c -> p (j c)"), core.ident[:])
            last.then_inc(g.oT_in_psum.sem, 1)

        def oT_dve(dve, it, p):
            dve.wait_ge(*g.oT_in_psum(it, p + 1))
            dve.wait_ge(*g.y_done(it, p))
            nc.vector.tensor_copy(oT[:, p % 2], b_o[:, T:2 * T])\
                .then_inc(g.oT_ready.sem, 1)

        def project_out_pe(pe, it, p):
            pe.wait_ge(*g.oT_ready(it, p + 1))
            if p == 0:
                pe.wait_ge(*core.x_updated(it, 0))
            for t in range(NT):
                last = nc.tensor.matmul(b_y[:, t * D:(t + 1) * D], oT[:, p % 2, t * P:(t + 1) * P],
                                        w_out[:, p], start=(p == 0 and t == 0),
                                        stop=(p == PAIRS - 1), skip_group_check=True)
            last.then_inc(g.y_done.sem, 1)

        with nc.Block() as block:
            @block.tensor
            def _(pe):
                def prepare(it):
                    prep_early_pe(pe, it)
                    prep_lat_pe(pe, it)
                prepare(-1)
                prep_late_pe(pe, -1)
                with pe.Fori(0, NB) as it:
                    project_pe(pe, it, 0)
                    for s in range(H + 3):
                        if s < H:
                            head_scores_pe(pe, it, s)
                        if s % 2 == 0 and s // 2 + 1 < PAIRS:
                            project_pe(pe, it, s // 2 + 1)
                        if 1 <= s <= H:
                            transpose_probs_pe(core, pe, sm, it, s - 1, b_pT, probs)
                        if s % 2 == 0 and s >= 4:
                            transpose_o_pe(pe, it, s // 2 - 2)
                        if 2 <= s < H + 2:
                            head_pv_pe(pe, it, s - 2)
                        if s % 2 == 1 and s >= 5:
                            project_out_pe(pe, it, s // 2 - 2)
                        if s == 5:
                            prep_early_pe(pe, it)
                        if s == 6:
                            prep_lat_pe(pe, it)
                    project_out_pe(pe, it, PAIRS - 1)
                    prep_late_pe(pe, it)

            @block.vector
            def _(dve):
                ln_stats_dve(core, dve, -1, 0)
                ln_normalize_dve(core, dve, -1, 0)
                prep_rms_dve(dve, -1)
                prep_norm_dve(dve, -1)
                prep_late_dve(dve, -1, sm.pv_done(-1, H))
                with dve.Fori(0, NB) as it:
                    rope_dve(dve, it, 0)
                    for s in range(H + 3):
                        if s < H:
                            max_dve(core, dve, sm, it, s, b_s, nmax)
                        if s % 2 == 0 and s // 2 + 1 < PAIRS:
                            rope_dve(dve, it, s // 2 + 1)
                        if s % 2 == 0 and s >= 4:
                            oT_dve(dve, it, s // 2 - 2)
                        if s % 2 == 1 and s >= 3:
                            normalise_dve(dve, it, s // 2 - 1)
                        if s == 3:
                            ln_stats_dve(core, dve, it, it + 1)
                        if s == 4:
                            ln_normalize_dve(core, dve, it, it + 1)
                        if s == 8:
                            prep_rms_dve(dve, it)
                        if s == 10:
                            prep_norm_dve(dve, it)
                    prep_late_dve(dve, it, sm.pv_done(it, H))
                    dve.wait_ge(*g.y_done(it, PAIRS))
                    nc.vector.tensor_tensor(
                        core.x[:, it].rearrange("p t d -> p (t d)"),
                        core.x[:, it].rearrange("p t d -> p (t d)"), b_y[:, :], ALU.add)\
                        .then_inc(core.x_updated.sem, 1)

            @block.scalar
            def _(act):
                prep_early_act(act, -1)
                prep_lat_act(act, -1)
                prep_late_act(act, -1, sm.scores_in_psum(-1, H))
                with act.Fori(0, NB) as it:
                    abs_act(act, it, 0)
                    for s in range(H + 3):
                        if s < H:
                            exp_act(core, act, sm, it, s, b_s, nmax, probs, sums,
                                    g.recip_ready(it - 1, s // 2 + 1))
                        if s % 2 == 0 and s // 2 + 1 < PAIRS:
                            abs_act(act, it, s // 2 + 1)
                        if 1 <= s <= H:
                            probsT_act(core, act, sm, it, s - 1, b_pT, probsT)
                        if s == 5:
                            prep_early_act(act, it)
                        if s == 6:
                            prep_lat_act(act, it)
                    prep_late_act(act, it, sm.scores_in_psum(it, H))

            @block.gpsimd
            def _(pool):
                ln_rstd_pool(core, pool, -1)
                prep_latent_pool(pool, -1)
                with pool.Fori(0, NB) as it:
                    pool.wait_ge(*g.rms_ready(it - 1, 1))
                    rope_pool(pool, it, 0)
                    for s in range(H + 3):
                        if s % 2 == 0 and s // 2 + 1 < PAIRS:
                            if s == 4:
                                pool.wait_ge(*core.ln_rstd(it, 1))
                            if s == 10:
                                pool.wait_ge(*g.rms_ready(it, 1))
                            rope_pool(pool, it, s // 2 + 1)
                        if s == 3:
                            pool.wait_ge(*g.q_rope_ready(it, 3))
                            ln_rstd_pool(core, pool, it)
                        if s == 8:
                            pool.wait_ge(*g.q_rope_ready(it, 6))
                            prep_latent_pool(pool, it)

        core.ln_ran()
        for s in g.prep:
            s.ran(NB + 1)
        for s in g.loop + sm.loop:
            s.ran(NB)



class Ternary:
    def __init__(self, ctx, core):
        self.y_in_psum = Signal(ctx, core.nc, "t_y_in_psum", 1)
        self.loop = [self.y_in_psum]


def ternary_sublayer(core, g, call):
    nc, ins = core.nc, core.ins
    with ExitStack() as ctx:
        def sb(name, shape, dt=F32):
            return ctx.enter_context(nc.sbuf_tensor(f"t{call}_{name}", shape, dt))

        w = sb("w", [P, KC, D])
        bias = sb("bias", [1, D])
        ones = sb("ones", [P, P])
        row_sum = sb("row_sum", [P, 1])
        scale = sb("scale", [P, 1])
        inv = sb("inv", [P, 2])
        z, up, down, wt, delta, w_ste = (sb(n, [P, KC, D]) for n in
                                         ("z", "up", "down", "wt", "delta", "w_ste"))
        core.weights_count += 32
        s0 = core.steps_count
        core.steps_count += 10

        with nc.Block() as block:
            @block.sync
            def _(sp):
                sp.dma_start(w[:], ins["f0_w"][:]).then_inc(core.weights_in, 16)
                sp.dma_start(bias[:], ins["f0_b"][:]).then_inc(core.weights_in, 16)

            @block.gpsimd
            def _(pool):
                nc.gpsimd.memset(ones[:], 1.0).then_inc(core.steps, 1)

            @block.tensor
            def _(pe):
                pe.wait_ge(core.steps, s0 + 2)
                nc.tensor.matmul(core.bank[0][:, 0:1], ones[:], row_sum[:], start=True, stop=True)\
                    .then_inc(core.steps, 1)

            @block.vector
            def _(dve):
                dve.wait_ge(core.weights_in, core.weights_count)
                nc.vector.tensor_reduce(row_sum[:], w[:], AX.XY, ALU.add,
                                        apply_absolute_value=True).then_inc(core.steps, 1)
                dve.wait_ge(core.steps, s0 + 3)
                nc.vector.tensor_scalar(scale[:], core.bank[0][:, 0:1], 1.0 / (D * D), None,
                                        ALU.mult).then_inc(core.steps, 1)
                dve.wait_ge(core.steps, s0 + 4)
                nc.vector.tensor_scalar(inv[:, 0:1], scale[:], 1e-10, None, ALU.add)\
                    .then_inc(core.steps, 1)
                dve.wait_ge(core.steps, s0 + 5)
                nc.vector.reciprocal(inv[:, 1:2], inv[:, 0:1]).then_inc(core.steps, 1)
                dve.wait_ge(core.steps, s0 + 6)
                nc.vector.tensor_scalar(z[:], w[:], inv[:, 1:2], None, ALU.mult)\
                    .then_inc(core.steps, 1)
                dve.wait_ge(core.steps, s0 + 7)
                nc.vector.tensor_scalar(up[:], z[:], 0.5, scale[:, 0:1], ALU.is_gt, ALU.mult)
                nc.vector.tensor_scalar(down[:], z[:], -0.5, scale[:, 0:1], ALU.is_lt, ALU.mult)\
                    .then_inc(core.steps, 1)
                dve.wait_ge(core.steps, s0 + 8)
                nc.vector.tensor_tensor(wt[:], up[:], down[:], ALU.subtract)\
                    .then_inc(core.steps, 1)
                dve.wait_ge(core.steps, s0 + 9)
                nc.vector.tensor_tensor(delta[:], wt[:], w[:], ALU.subtract)\
                    .then_inc(core.steps, 1)
                dve.wait_ge(core.steps, s0 + 10)
                nc.vector.tensor_tensor(w_ste[:], w[:], delta[:], ALU.add)

        b_prep, b_y = core.bank[0:2], core.bank[2:4]
        with nc.Block() as block:
            def transpose_pe(pe, it):
                pe.wait_ge(*core.ln_out(it, NT))
                pe.wait_ge(*core.xnT_ready(it, 0))
                transpose_tokens_pe(core, b_prep[0], core.xn, core.ln_out, it)\
                    .then_inc(core.xnT_in_psum.sem, 1)

            @block.tensor
            def _(pe):
                transpose_pe(pe, -1)
                with pe.Fori(0, NB) as it:
                    pe.wait_ge(*core.xnT_ready(it - 1, 1))
                    pe.wait_ge(*core.x_updated(it, 0))
                    for t in range(NT):
                        out = b_y[0][:, t * D:(t + 1) * D]
                        for c in range(KC):
                            nc.tensor.matmul(out, core.xnT[:, c, t * P:(t + 1) * P], w_ste[:, c],
                                             start=(c == 0), stop=False)
                        last = nc.tensor.matmul(out, core.ones_row[:, 0:P], bias[:], start=False,
                                                stop=True)
                    last.then_inc(g.y_in_psum.sem, 1)
                    transpose_pe(pe, it)

            @block.vector
            def _(dve):
                ln_stats_dve(core, dve, -1, 0)
                ln_normalize_dve(core, dve, -1, 0)
                with dve.Fori(0, NB) as it:
                    ln_stats_dve(core, dve, it, it + 1)
                    ln_normalize_dve(core, dve, it, it + 1)
                    dve.wait_ge(*g.y_in_psum(it, 1))
                    xb = core.x[:, it].rearrange("p t d -> p (t d)")
                    nc.vector.tensor_tensor(xb, xb, b_y[0][:, :], ALU.add)\
                        .then_inc(core.x_updated.sem, 1)

            @block.gpsimd
            def _(pool):
                ln_rstd_pool(core, pool, -1)
                with pool.Fori(0, NB) as it:
                    ln_rstd_pool(core, pool, it)

            @block.scalar
            def _(act):
                def copy(it):
                    act.wait_ge(*core.xnT_in_psum(it, 1))
                    act.wait_ge(*g.y_in_psum(it, 1))
                    nc.scalar.copy(core.xnT[:].rearrange("p c t -> p (c t)"), b_prep[0][:, :])\
                        .then_inc(core.xnT_ready.sem, 1)
                copy(-1)
                with act.Fori(0, NB) as it:
                    copy(it)

        core.ln_ran()
        for s in g.loop:
            s.ran(NB)



GH = 4
GROUPS = H // GH
CHUNKS = GROUPS * NT
LEVELS = 7
A_PER = LEVELS - 2
B_PER = LEVELS - 1
TAPS = 4
RPG = 8
CONV = 6
KSCALE = 128 ** -0.5


class Delta:
    def __init__(self, ctx, core):
        def sig(name, per, peeled=0):
            s = Signal(ctx, core.nc, name, per)
            s.start = 2 * per - peeled
            self.all.append(s)
            return s
        self.all = []
        self.ab_in_psum = sig("ab_in_psum", 1, 1)
        self.ab_ready = sig("ab_ready", 1, 1)
        self.proj_in_psum = sig("proj_in_psum", GROUPS * RPG, RPG)
        self.proj_out = sig("proj_out", GROUPS * RPG, RPG)
        self.tap_done = sig("tap_done", GROUPS * CONV * 3, CONV * 3)
        self.sigmoid_ready = sig("sigmoid_ready", GROUPS * CONV, CONV)
        self.qkv_ready = sig("qkv_ready", GROUPS * CONV, CONV)
        self.abc_in_psum = sig("abc_in_psum", CHUNKS, 1)
        self.decay_ready = sig("decay_ready", CHUNKS, 1)
        self.kk_in_psum = sig("kk_in_psum", CHUNKS, 1)
        self.nT_ready = sig("nT_ready", CHUNKS, 1)
        self.qk_in_psum = sig("d_qk_in_psum", CHUNKS, 1)
        self.pT_ready = sig("pT_ready", CHUNKS, 1)
        self.n_in_psum = sig("n_in_psum", CHUNKS, 1)
        self.n_ready = sig("n_ready", CHUNKS, 1)
        self.v_in_psum = sig("d_v_in_psum", CHUNKS, 1)
        self.v_ready = sig("d_v_ready", CHUNKS, 1)
        self.k_in_psum = sig("d_k_in_psum", GROUPS, 1)
        self.k_ready = sig("d_k_ready", GROUPS, 1)
        self.kq_decayed = sig("kq_decayed", GROUPS * 2)
        self.a_in_psum = sig("a_in_psum", CHUNKS * A_PER)
        self.a_ready = sig("a_ready", CHUNKS * A_PER)
        self.b_in_psum = sig("b_in_psum", CHUNKS * B_PER)
        self.b_ready = sig("b_ready", CHUNKS * B_PER)
        self.ay_in_psum = sig("ay_in_psum", CHUNKS * LEVELS)
        self.y_ready = sig("dy_ready", CHUNKS * LEVELS)
        self.ks_in_psum = sig("ks_in_psum", GROUPS)
        self.rhs_ready = sig("rhs_ready", GROUPS)
        self.yw_ready = sig("yw_ready", GROUPS)
        self.state_in_psum = sig("state_in_psum", GROUPS)
        self.state_ready = sig("state_ready", GROUPS)
        self.o_in_psum = sig("do_in_psum", CHUNKS)
        self.o_stats = sig("o_stats", CHUNKS)
        self.o_mv = sig("o_mv", CHUNKS)
        self.o_var = sig("o_var", CHUNKS)
        self.o_rstd = sig("o_rstd", CHUNKS)
        self.o_normal = sig("o_normal", CHUNKS)
        self.oT_in_psum = sig("doT_in_psum", CHUNKS)
        self.oT_affine = sig("oT_affine", CHUNKS)
        self.og_ready = sig("og_ready", CHUNKS)
        self.out_done = sig("out_done", CHUNKS)


def delta_sublayer(core):
    nc, ins = core.nc, core.ins
    with ExitStack() as ctx:
        def sb(name, shape, dt=F32):
            return ctx.enter_context(nc.sbuf_tensor(f"d_{name}", shape, dt))
        g = Delta(ctx, core)

        HW = H * P
        w_k, w_q, w_v, w_g = (sb(n, [P, KC, HW]) for n in ("wk", "wq", "wv", "wg"))
        w_o = sb("wo", [P, H, D])
        w_a, w_b = sb("wa", [P, KC, H]), sb("wb", [P, KC, H])
        b_a, b_b = sb("ba", [H, 1]), sb("bb", [1, H])
        taps = sb("taps", [P, 3, H, TAPS])
        tap_bias = sb("tap_bias", [P, 3, H])
        o_w, o_b = sb("o_w", [P, 1]), sb("o_b", [P, 1])
        loads = [(w_k, "wk"), (w_q, "wq"), (w_v, "wv"), (w_g, "wg"), (w_o, "wo"), (w_a, "wa"),
                 (w_b, "wb"), (b_a, "ba"), (b_b, "bb"), (taps, "taps"), (tap_bias, "tap_bias"),
                 (o_w, "o_w"), (o_b, "o_b")]
        core.weights_count += 16 * len(loads)

        alphaT = sb("alphaT", [H, T])
        beta = sb("beta", [P, NT, H])
        raw, acc, sigm = (sb(n, [P, 2, 2, T]) for n in ("raw", "acc", "sigm"))
        kT, qT, vT, gT = (sb(n, [P, 2, GH, T]) for n in ("kT", "qT", "vT", "gT"))
        decay = sb("decay", [P, 2, GH, P + 1])
        g_decay = sb("g_decay", [P, GH, P + 1])
        zeros = sb("zeros", [P, P])
        nT0, n0, pT, v_tok = (sb(n, [P, 2, GH, P]) for n in ("nT0", "n0", "pT", "v_tok"))
        k_tok, kg, qg = (sb(n, [P, GH, P]) for n in ("k_tok", "kg", "qg"))
        pow_a, pow_b, y = (sb(n, [P, 2, GH, P]) for n in ("pow_a", "pow_b", "y"))
        yw, state = sb("yw", [P, GH, P]), sb("state", [P, GH, P])
        o_st, o_mv = sb("o_st", [P, GH, 6]), sb("o_mv", [P, GH, 2])
        o_var, o_rs = sb("o_var", [P, GH]), sb("o_rs", [P, GH])
        o_n, oT, og = (sb(n, [P, GH, P]) for n in ("o_n", "oT", "og"))

        b_proj, b_pre, b_a2, b_b2, b_y, b_o, b_abc, b_out = core.bank
        wide = lambda ap: ap.rearrange("p h t -> p (h t)")
        quad = lambda bank: bank[:, :].rearrange("p (h t) -> p h t", h=GH)

        with nc.Block() as block:
            @block.sync
            def _(sp):
                for dst, name in loads:
                    sp.dma_start(dst[:], ins["d_" + name][:]).then_inc(core.weights_in, 16)
                sp.wait_ge(core.weights_in, core.weights_count)

            @block.gpsimd
            def _(pool):
                for s in g.all:
                    pool.sem_inc(s.sem, s.start)
                nc.gpsimd.memset(zeros[:], 0.0)
                nc.gpsimd.memset(decay[:, :, :, 0:1], 0.0)
                nc.gpsimd.memset(g_decay[:, :, 0:1], 1.0)

        def xnT_pe(pe, it):
            pe.wait_ge(*core.ln_out(it, NT))
            pe.wait_ge(*g.proj_out(it, 3 * RPG))
            transpose_tokens_pe(core, b_proj, core.xn, core.ln_out, it)\
                .then_inc(core.xnT_in_psum.sem, 1)

        def xnT_act(act, it):
            act.wait_ge(*core.xnT_in_psum(it, 1))
            act.wait_ge(*g.proj_in_psum(it, 3 * RPG))
            nc.scalar.copy(core.xnT[:].rearrange("p c t -> p (c t)"), b_proj[:, :])\
                .then_inc(core.xnT_ready.sem, 1)

        def ab_pe(pe, it):
            pe.wait_ge(*core.xnT_ready(it, 1))
            pe.wait_ge(*g.v_ready(it, 7))
            for c in range(KC):
                nc.tensor.matmul(b_pre[0:H, 0:T], w_a[:, c], core.xnT[:, c], start=(c == 0),
                                 stop=(c == KC - 1))
            for t in range(NT):
                out = b_pre[:, T + t * H:T + (t + 1) * H]
                for c in range(KC):
                    nc.tensor.matmul(out, core.xnT[:, c, t * P:(t + 1) * P], w_b[:, c],
                                     start=(c == 0), stop=False)
                last = nc.tensor.matmul(out, core.ones_row[:, 0:P], b_b[:], start=False, stop=True)
            last.then_inc(g.ab_in_psum.sem, 1)

        def ab_act(act, it):
            act.wait_ge(*g.ab_in_psum(it, 1))
            act.wait_ge(*g.abc_in_psum(it, 7))
            act.wait_ge(*g.pT_ready(it, 7))
            act.wait_ge(*g.yw_ready(it, GROUPS))
            nc.scalar.activation(alphaT[:], b_pre[0:H, 0:T], ACT.Sigmoid, bias=b_a[:])
            nc.scalar.activation(beta[:].rearrange("p t h -> p (t h)"), b_pre[:, T:T + NT * H],
                                 ACT.Sigmoid).then_inc(g.ab_ready.sem, 1)

        def round_of(pos, r):
            return pos * RPG + r, pos * CONV + r, (pos + 1) % GROUPS, (pos + 1) % 2

        def project_pe(pe, it, pos, r):
            n, _, grp, _ = round_of(pos, r)
            if r == 0:
                pe.wait_ge(*core.xnT_ready(it if pos == 3 else it - 1, 1))
            pe.wait_ge(*g.proj_out(it, n))
            w = (w_k, w_q, w_v, w_g)[r // 2]
            for j in range(2):
                h = grp * GH + 2 * (r % 2) + j
                for c in range(KC):
                    last = nc.tensor.matmul(b_proj[:, j * T:(j + 1) * T], w[:, c, h * P:(h + 1) * P],
                                            core.xnT[:, c], start=(c == 0), stop=(c == KC - 1))
            last.then_inc(g.proj_in_psum.sem, 1)

        def evacuate_act(act, it, pos, r):
            n, m, grp, buf = round_of(pos, r)
            act.wait_ge(*g.proj_in_psum(it, n + 1))
            if r >= CONV:
                act.wait_ge(*g.og_ready(it, 2 * pos))
                hp = 2 * (r % 2)
                nc.scalar.activation(wide(gT[:, buf, hp:hp + 2]), b_proj[:, :], ACT.Sigmoid)\
                    .then_inc(g.proj_out.sem, 1)
                return
            act.wait_ge(*g.qkv_ready(it, m - 1))
            for j in range(2):
                h = grp * GH + 2 * (r % 2) + j
                nc.scalar.activation(acc[:, r % 2, j], b_proj[:, j * T:(j + 1) * T], ACT.Identity,
                                     scale=taps[:, r // 2, h, 3:4], bias=tap_bias[:, r // 2, h:h + 1])
            nc.scalar.copy(wide(raw[:, r % 2]), b_proj[:, :]).then_inc(g.proj_out.sem, 1)

        def taps_dve(dve, it, pos, r):
            n, m, grp, buf = round_of(pos, r)
            dve.wait_ge(*g.proj_out(it, n + 1))
            for d in range(1, TAPS):
                if d > 1:
                    dve.wait_ge(*g.tap_done(it, 3 * m + d - 1))
                for j in range(2):
                    h = grp * GH + 2 * (r % 2) + j
                    last = nc.vector.scalar_tensor_tensor(
                        out=acc[:, r % 2, j, d:T], in0=raw[:, r % 2, j, 0:T - d],
                        scalar=taps[:, r // 2, h, 3 - d:4 - d], in1=acc[:, r % 2, j, d:T],
                        op0=ALU.mult, op1=ALU.add)
                last.then_inc(g.tap_done.sem, 1)

        def sigmoid_act(act, it, pos, r):
            _, m, _, _ = round_of(pos, r)
            act.wait_ge(*g.tap_done(it, 3 * m + 3))
            act.wait_ge(*g.qkv_ready(it, m - 1))
            nc.scalar.activation(wide(sigm[:, r % 2]), wide(acc[:, r % 2]), ACT.Sigmoid)\
                .then_inc(g.sigmoid_ready.sem, 1)

        def silu(eng, it, pos, r):
            _, m, _, buf = round_of(pos, r)
            hp = 2 * (r % 2)
            eng.wait_ge(*g.sigmoid_ready(it, m + 1))
            eng.wait_ge(*g.v_in_psum(it, 2 * pos - 1))
            eng.wait_ge(*g.k_in_psum(it, pos - 1))
            eng.wait_ge(*g.kq_decayed(it, 2 * pos))
            eng.wait_ge(*g.qkv_ready(it, m))
            if r < 2:
                nc.vector.scalar_tensor_tensor(
                    out=wide(kT[:, buf, hp:hp + 2]), in0=wide(acc[:, r % 2]), scalar=KSCALE,
                    in1=wide(sigm[:, r % 2]), op0=ALU.mult, op1=ALU.mult)\
                    .then_inc(g.qkv_ready.sem, 1)
            else:
                nc.gpsimd.tensor_tensor((qT if r < 4 else vT)[:, buf, hp:hp + 2], acc[:, r % 2],
                                        sigm[:, r % 2], ALU.mult).then_inc(g.qkv_ready.sem, 1)

        def where(m):
            grp, c = (m // 2) % GROUPS, m % 2
            return grp, c, grp % 2, m % 2, slice(c * P, (c + 1) * P)

        def kT_count(m):
            return ((m // 2) - 1) * CONV

        def decay_pe(pe, it, m):
            grp, c, hb, cb, tok = where(m)
            if m == CHUNKS:
                pe.wait_ge(*g.ab_ready(it, 1))
            pe.wait_ge(*g.decay_ready(it, m - 1))
            for j in range(GH):
                h = grp * GH + j
                last = nc.tensor.matmul(b_abc[:, j * P:(j + 1) * P],
                                        core.ident[0:H, h:h + 1].broadcast_to([H, P]),
                                        alphaT[:, tok], start=True, stop=True)
            last.then_inc(g.abc_in_psum.sem, 1)

        def decay_dve(dve, it, m):
            grp, c, hb, cb, tok = where(m)
            dve.wait_ge(*g.abc_in_psum(it, m))
            for j in range(GH):
                last = nc.vector.tensor_tensor_scan(
                    decay[:, cb, j, 1:P + 1], b_abc[:, j * P:(j + 1) * P], core.ident[:], 0.0,
                    ALU.mult, ALU.add)
            if c == 1:
                dve.wait_ge(*g.kq_decayed(it, m - 1))
                for j in range(GH):
                    last = nc.vector.tensor_tensor_scan(
                        g_decay[:, j, 1:P + 1], b_abc[:, j * P:(j + 1) * P], zeros[:], 1.0,
                        ALU.mult, ALU.add)
            last.then_inc(g.decay_ready.sem, 1)

        def kk_pe(pe, it, m):
            grp, c, hb, cb, tok = where(m)
            pe.wait_ge(*g.qkv_ready(it, kT_count(m) + 2))
            pe.wait_ge(*g.v_ready(it, m - 1))
            pe.wait_ge(*g.k_ready(it, (m - 1) // 2))
            if m == CHUNKS:
                pe.wait_ge(*g.ab_ready(it, 1))
            for j in range(GH):
                last = nc.tensor.matmul(b_pre[:, j * P:(j + 1) * P], kT[:, hb, j, tok],
                                        kT[:, hb, j, tok], start=True, stop=True)
            last.then_inc(g.kk_in_psum.sem, 1)

        def nT_dve(dve, it, m):
            grp, c, hb, cb, tok = where(m)
            dve.wait_ge(*g.kk_in_psum(it, m))
            dve.wait_ge(*g.decay_ready(it, m))
            dve.wait_ge(*g.b_in_psum(it, (m - 2) * B_PER + 1))
            dve.wait_ge(*g.ay_in_psum(it, (m - 2) * LEVELS + 1))
            for j in range(GH):
                h = grp * GH + j
                last = nc.vector.scalar_tensor_tensor(
                    out=nT0[:, cb, j], in0=b_pre[:, j * P:(j + 1) * P], scalar=beta[:, c, h:h + 1],
                    in1=decay[:, cb, j, 0:P], op0=ALU.mult, op1=ALU.mult)
            last.then_inc(g.nT_ready.sem, 1)

        def qk_pe(pe, it, m):
            grp, c, hb, cb, tok = where(m)
            pe.wait_ge(*g.qkv_ready(it, kT_count(m) + 4))
            pe.wait_ge(*g.nT_ready(it, m))
            for j in range(GH):
                last = nc.tensor.matmul(b_pre[:, j * P:(j + 1) * P], kT[:, hb, j, tok],
                                        qT[:, hb, j, tok], start=True, stop=True)
            last.then_inc(g.qk_in_psum.sem, 1)

        def pT_dve(dve, it, m):
            grp, c, hb, cb, tok = where(m)
            dve.wait_ge(*g.qk_in_psum(it, m))
            dve.wait_ge(*g.o_in_psum(it, m - 1))
            for j in range(GH):
                h = grp * GH + j
                last = nc.vector.scalar_tensor_tensor(
                    out=pT[:, cb, j], in0=b_pre[:, j * P:(j + 1) * P], scalar=beta[:, c, h:h + 1],
                    in1=decay[:, cb, j, 1:P + 1], op0=ALU.mult, op1=ALU.mult)
            last.then_inc(g.pT_ready.sem, 1)

        def n_pe(pe, it, m):
            cb = where(m)[3]
            pe.wait_ge(*g.nT_ready(it, m))
            pe.wait_ge(*g.pT_ready(it, m))
            for j in range(GH):
                last = nc.tensor.transpose(b_pre[:, j * P:(j + 1) * P], nT0[:, cb, j], core.ident[:])
            last.then_inc(g.n_in_psum.sem, 1)

        def n_act(act, it, m):
            cb = where(m)[3]
            act.wait_ge(*g.n_in_psum(it, m))
            act.wait_ge(*g.b_in_psum(it, (m - 2) * B_PER + 1))
            nc.scalar.copy(wide(n0[:, cb]), b_pre[:, :]).then_inc(g.n_ready.sem, 1)

        def v_pe(pe, it, m):
            grp, c, hb, cb, tok = where(m)
            pe.wait_ge(*g.qkv_ready(it, kT_count(m) + 6))
            pe.wait_ge(*g.n_ready(it, m))
            for j in range(GH):
                last = nc.tensor.transpose(b_pre[:, j * P:(j + 1) * P], vT[:, hb, j, tok],
                                           core.ident[:])
            last.then_inc(g.v_in_psum.sem, 1)

        def v_act(act, it, m):
            cb = where(m)[3]
            act.wait_ge(*g.v_in_psum(it, m))
            act.wait_ge(*g.y_ready(it, (m - 2) * LEVELS + 1))
            act.wait_ge(*g.ay_in_psum(it, (m - 2) * LEVELS + 1))
            nc.scalar.copy(wide(v_tok[:, cb]), b_pre[:, :]).then_inc(g.v_ready.sem, 1)

        def k_pe(pe, it, m):
            grp, c, hb, cb, tok = where(m)
            pe.wait_ge(*g.v_ready(it, m))
            for j in range(GH):
                last = nc.tensor.transpose(b_pre[:, j * P:(j + 1) * P], kT[:, hb, j, tok],
                                           core.ident[:])
            last.then_inc(g.k_in_psum.sem, 1)

        def k_act(act, it, m):
            act.wait_ge(*g.k_in_psum(it, m // 2))
            act.wait_ge(*g.state_in_psum(it, m // 2 - 1))
            nc.scalar.copy(wide(k_tok[:]), b_pre[:, :]).then_inc(g.k_ready.sem, 1)

        def kq_pool(pool, it, m):
            grp, c, hb, cb, tok = where(m)
            pool.wait_ge(*g.decay_ready(it, m))
            pool.wait_ge(*g.qkv_ready(it, kT_count(m) + 4))
            pool.wait_ge(*g.ks_in_psum(it, m // 2))
            pool.wait_ge(*g.o_in_psum(it, m - 1))
            nc.gpsimd.tensor_tensor(kg[:], kT[:, hb, :, tok], g_decay[:, :, 0:P], ALU.mult)\
                .then_inc(g.kq_decayed.sem, 1)
            nc.gpsimd.tensor_tensor(qg[:], qT[:, hb, :, tok], g_decay[:, :, 1:P + 1], ALU.mult)\
                .then_inc(g.kq_decayed.sem, 1)

        def level(n, l):
            cb = n % 2
            a = n0[:, cb] if l == 0 else pow_a[:, l % 2]
            b = nT0[:, cb] if l == 0 else pow_b[:, l % 2]
            y_in = (v_tok[:, cb] if cb == 0 else y[:, 1]) if l == 0 else y[:, (l + 1) % 2]
            return n * LEVELS + l, a, b, y_in, y[:, l % 2]

        def powers_ready(pe, it, n, l):
            at = level(n, l)[0]
            if l == 0:
                pe.wait_ge(*g.nT_ready(it, n))
                pe.wait_ge(*g.n_ready(it, n))
            else:
                pe.wait_ge(*g.a_ready(it, n * A_PER + min(l, A_PER)))
                pe.wait_ge(*g.b_ready(it, n * B_PER + min(l, B_PER)))

        def square_a_pe(pe, it, n, l):
            at, a, b, _, _ = level(n, l)
            powers_ready(pe, it, n, l)
            pe.wait_ge(*g.a_ready(it, n * A_PER + min(l, A_PER)))
            if l < LEVELS - 2:
                for j in range(GH):
                    last = nc.tensor.matmul(b_a2[:, j * P:(j + 1) * P], b[:, j], a[:, j],
                                            start=True, stop=True)
                last.then_inc(g.a_in_psum.sem, 1)

        def square_b_pe(pe, it, n, l):
            at, a, b, _, _ = level(n, l)
            pe.wait_ge(*g.b_ready(it, n * B_PER + min(l, B_PER)))
            if l < LEVELS - 1:
                for j in range(GH):
                    last = nc.tensor.matmul(b_b2[:, j * P:(j + 1) * P], a[:, j], b[:, j],
                                            start=True, stop=True)
                last.then_inc(g.b_in_psum.sem, 1)

        def apply_pe(pe, it, n, l):
            at, a, b, y_in, _ = level(n, l)
            if l == 0 and n % 2 == 0:
                pe.wait_ge(*g.v_ready(it, n))
            elif l == 0:
                pe.wait_ge(*g.rhs_ready(it, n // 2 + 1))
            else:
                pe.wait_ge(*g.y_ready(it, at))
            pe.wait_ge(*g.y_ready(it, at))
            for j in range(GH):
                last = nc.tensor.matmul(b_y[:, j * P:(j + 1) * P], b[:, j], y_in[:, j],
                                        start=True, stop=True)
            last.then_inc(g.ay_in_psum.sem, 1)

        def powers_act(act, it, n, l):
            at = level(n, l)[0]
            if l < LEVELS - 2:
                act.wait_ge(*g.a_in_psum(it, n * A_PER + l + 1))
                act.wait_ge(*g.b_in_psum(it, n * B_PER + l))
                nc.scalar.copy(wide(pow_a[:, (l + 1) % 2]), b_a2[:, :]).then_inc(g.a_ready.sem, 1)
            if l < LEVELS - 1:
                act.wait_ge(*g.b_in_psum(it, n * B_PER + l + 1))
                act.wait_ge(*g.ay_in_psum(it, at))
                nc.scalar.copy(wide(pow_b[:, (l + 1) % 2]), b_b2[:, :]).then_inc(g.b_ready.sem, 1)

        def apply_dve(dve, it, n, l):
            at, _, _, y_in, y_out = level(n, l)
            dve.wait_ge(*g.ay_in_psum(it, at + 1))
            if l == 0:
                dve.wait_ge(*g.o_in_psum(it, n))
            dve.wait_ge(*g.y_ready(it, at))
            nc.vector.tensor_tensor(wide(y_out), wide(y_in), b_y[:, :],
                                    ALU.subtract if l == 0 else ALU.add).then_inc(g.y_ready.sem, 1)

        def yw_dve(dve, it, n):
            dve.wait_ge(*g.y_ready(it, (n + 1) * LEVELS))
            dve.wait_ge(*g.state_in_psum(it, n // 2))
            for j in range(GH):
                h = (n // 2) * GH + j
                last = nc.vector.tensor_scalar(yw[:, j], y[:, 0, j], decay[:, n % 2, j, P:P + 1],
                                               beta[:, 0, h:h + 1], ALU.mult, ALU.mult)
            last.then_inc(g.yw_ready.sem, 1)

        def state_pe(pe, it, n):
            grp = n // 2
            pe.wait_ge(*g.yw_ready(it, grp + 1))
            pe.wait_ge(*g.k_ready(it, grp))
            pe.wait_ge(*g.o_normal(it, n))
            pe.wait_ge(*g.oT_affine(it, n))
            for j in range(GH):
                last = nc.tensor.matmul(b_o[:, j * P:(j + 1) * P], k_tok[:, j], yw[:, j],
                                        start=True, stop=True)
            last.then_inc(g.state_in_psum.sem, 1)

        def state_act(act, it, n):
            grp = n // 2
            act.wait_ge(*g.state_in_psum(it, grp + 1))
            act.wait_ge(*g.ks_in_psum(it, grp))
            act.wait_ge(*g.o_in_psum(it, n))
            nc.scalar.copy(wide(state[:]), b_o[:, :]).then_inc(g.state_ready.sem, 1)

        def rhs_pe(pe, it, n):
            grp = n // 2
            pe.wait_ge(*g.state_ready(it, grp + 1))
            pe.wait_ge(*g.kq_decayed(it, 2 * grp + 2))
            pe.wait_ge(*g.y_ready(it, n * LEVELS))
            for j in range(GH):
                last = nc.tensor.matmul(b_y[:, j * P:(j + 1) * P], kg[:, j], state[:, j],
                                        start=True, stop=True)
            last.then_inc(g.ks_in_psum.sem, 1)

        def rhs_dve(dve, it, n):
            grp = n // 2
            dve.wait_ge(*g.ks_in_psum(it, grp + 1))
            dve.wait_ge(*g.v_ready(it, n))
            nc.vector.tensor_tensor(wide(y[:, 1]), wide(v_tok[:, 1]), b_y[:, :], ALU.subtract)\
                .then_inc(g.rhs_ready.sem, 1)

        def o_pe(pe, it, n):
            grp, c, hb, cb, tok = where(n)
            pe.wait_ge(*g.y_ready(it, (n + 1) * LEVELS))
            pe.wait_ge(*g.pT_ready(it, n))
            pe.wait_ge(*g.oT_affine(it, n))
            if c == 0:
                pe.wait_ge(*g.state_ready(it, grp + 1))
            for j in range(GH):
                out = b_o[:, j * P:(j + 1) * P]
                last = nc.tensor.matmul(out, pT[:, cb, j], y[:, 0, j], start=True, stop=(c == 0))
                if c == 1:
                    last = nc.tensor.matmul(out, qg[:, j], state[:, j], start=False, stop=True)
            last.then_inc(g.o_in_psum.sem, 1)

        def o_stats_dve(dve, it, n):
            dve.wait_ge(*g.o_in_psum(it, n + 1))
            for j in range(GH):
                last = nc.vector.bn_stats(o_st[:, j], b_o[:, j * P:(j + 1) * P])
            last.then_inc(g.o_stats.sem, 1)
            dve.wait_ge(*g.o_stats(it, n + 1))
            nc.vector.memset(core.carrier[:], 0.0)
            for j in range(GH):
                last = nc.vector.bn_aggr(o_mv[:, j], o_st[:, j])
            last.then_inc(g.o_mv.sem, 1)
            dve.wait_ge(*g.o_mv(it, n + 1))
            nc.vector.tensor_scalar(o_var[:], o_mv[:, :, 1], 1e-5, None, ALU.add)\
                .then_inc(g.o_var.sem, 1)

        def o_rstd_pool(pool, it, n):
            pool.wait_ge(*g.o_var(it, n + 1))
            pool.wait_ge(*g.o_normal(it, n))
            nc.gpsimd.tensor_tensor(o_rs[:], o_var[:], core.minus_half[:, 0:GH], ALU.pow)\
                .then_inc(g.o_rstd.sem, 1)

        def o_normal_dve(dve, it, n):
            dve.wait_ge(*g.o_rstd(it, n + 1))
            dve.wait_ge(*g.oT_in_psum(it, n))
            for j in range(GH):
                last = nc.vector.tensor_scalar(o_n[:, j], b_o[:, j * P:(j + 1) * P],
                                               o_mv[:, j, 0:1], o_rs[:, j:j + 1], ALU.subtract,
                                               ALU.mult)
            last.then_inc(g.o_normal.sem, 1)

        def oT_pe(pe, it, n):
            pe.wait_ge(*g.o_normal(it, n + 1))
            for j in range(GH):
                last = nc.tensor.transpose(b_o[:, j * P:(j + 1) * P], o_n[:, j], core.ident[:])
            last.then_inc(g.oT_in_psum.sem, 1)

        def oT_act(act, it, n):
            act.wait_ge(*g.oT_in_psum(it, n + 1))
            act.wait_ge(*g.og_ready(it, n))
            nc.scalar.activation(wide(oT[:]), b_o[:, :], ACT.Identity, scale=o_w[:], bias=o_b[:])\
                .then_inc(g.oT_affine.sem, 1)

        def og_pool(pool, it, n):
            grp, c, hb, cb, tok = where(n)
            pool.wait_ge(*g.oT_affine(it, n + 1))
            pool.wait_ge(*g.proj_out(it, grp * RPG))
            pool.wait_ge(*g.out_done(it, n))
            nc.gpsimd.tensor_tensor(og[:], oT[:], gT[:, hb, :, tok], ALU.mult)\
                .then_inc(g.og_ready.sem, 1)

        def out_pe(pe, it, n):
            grp, c, hb, cb, tok = where(n)
            pe.wait_ge(*g.og_ready(it, n + 1))
            if n == 0:
                pe.wait_ge(*core.x_updated(it, 0))
            for j in range(GH):
                last = nc.tensor.matmul(b_out[:, c * D:(c + 1) * D], og[:, j], w_o[:, grp * GH + j],
                                        start=(n == 0 and j == 0),
                                        stop=(grp == GROUPS - 1 and j == GH - 1),
                                        skip_group_check=True)
            last.then_inc(g.out_done.sem, 1)

        STEPS = [(n, l) for n in range(CHUNKS) for l in range(LEVELS)]
        round_at = lambda n, l: (n // 2, (n % 2) * 4 + l) if l < 4 else None
        before = lambda n, l: (n, l - 1) if l else (n - 1, LEVELS - 1)

        with nc.Block() as block:
            @block.tensor
            def _(pe):
                def preamble(it, m):
                    decay_pe(pe, it, m)
                    kk_pe(pe, it, m)
                    qk_pe(pe, it, m)
                    n_pe(pe, it, m)
                    v_pe(pe, it, m)
                    k_pe(pe, it, m)
                xnT_pe(pe, -1)
                ab_pe(pe, -1)
                for r in range(RPG):
                    project_pe(pe, -1, 3, r)
                preamble(-1, CHUNKS)
                with pe.Fori(0, NB) as it:
                    for n, l in STEPS:
                        if n % 2 == 1 and l == 0:
                            state_pe(pe, it, n - 1)
                        square_a_pe(pe, it, n, l)
                        if n % 2 == 1 and l == 0:
                            rhs_pe(pe, it, n)
                        square_b_pe(pe, it, n, l)
                        if l == 0 and n > 0:
                            o_pe(pe, it, n - 1)
                        if round_at(n, l):
                            project_pe(pe, it, *round_at(n, l))
                        apply_pe(pe, it, n, l)
                        if l == 2 and n > 0:
                            oT_pe(pe, it, n - 1)
                        if l == 4 and n > 0:
                            out_pe(pe, it, n - 1)
                        if l == 0 and n == CHUNKS - 1:
                            ab_pe(pe, it)
                        if l == 0:
                            decay_pe(pe, it, n + 1)
                        if l == 1:
                            kk_pe(pe, it, n + 1)
                        if l == 2:
                            qk_pe(pe, it, n + 1)
                        if l == 3:
                            n_pe(pe, it, n + 1)
                        if l == 4:
                            v_pe(pe, it, n + 1)
                        if l == 5 and n % 2 == 1:
                            k_pe(pe, it, n + 1)
                        if (n, l) == (5, 4):
                            xnT_pe(pe, it)
                    o_pe(pe, it, CHUNKS - 1)
                    oT_pe(pe, it, CHUNKS - 1)
                    out_pe(pe, it, CHUNKS - 1)

            @block.vector
            def _(dve):
                ln_stats_dve(core, dve, -1, 0)
                ln_normalize_dve(core, dve, -1, 0)
                for r in range(RPG):
                    if r < CONV:
                        taps_dve(dve, -1, 3, r)
                    if r < 2:
                        silu(dve, -1, 3, r)
                decay_dve(dve, -1, CHUNKS)
                nT_dve(dve, -1, CHUNKS)
                pT_dve(dve, -1, CHUNKS)
                with dve.Fori(0, NB) as it:
                    for n, l in STEPS:
                        if n % 2 == 1 and l == 0:
                            rhs_dve(dve, it, n)
                        apply_dve(dve, it, n, l)
                        if l == 0 and n > 0:
                            o_stats_dve(dve, it, n - 1)
                        if l == 1 and n > 0:
                            o_normal_dve(dve, it, n - 1)
                        if n >= 0 and round_at(*before(n, l)) and (n, l) != (0, 0):
                            pos, r = round_at(*before(n, l))
                            if r < 2:
                                silu(dve, it, pos, r)
                        if l == 0:
                            decay_dve(dve, it, n + 1)
                        if l == 1:
                            nT_dve(dve, it, n + 1)
                        if l == 2:
                            pT_dve(dve, it, n + 1)
                        if round_at(n, l) and round_at(n, l)[1] < CONV:
                            taps_dve(dve, it, *round_at(n, l))
                        if (n, l) == (2, 5):
                            ln_stats_dve(core, dve, it, it + 1)
                        if (n, l) == (3, 5):
                            ln_normalize_dve(core, dve, it, it + 1)
                        if l == LEVELS - 1 and n % 2 == 0:
                            yw_dve(dve, it, n)
                    o_stats_dve(dve, it, CHUNKS - 1)
                    o_normal_dve(dve, it, CHUNKS - 1)
                    dve.wait_ge(*g.out_done(it, CHUNKS))
                    xb = core.x[:, it].rearrange("p t d -> p (t d)")
                    nc.vector.tensor_tensor(xb, xb, b_out[:, :], ALU.add)\
                        .then_inc(core.x_updated.sem, 1)

            @block.scalar
            def _(act):
                xnT_act(act, -1)
                ab_act(act, -1)
                for r in range(RPG):
                    evacuate_act(act, -1, 3, r)
                    if r < CONV:
                        sigmoid_act(act, -1, 3, r)
                n_act(act, -1, CHUNKS)
                v_act(act, -1, CHUNKS)
                k_act(act, -1, CHUNKS)
                with act.Fori(0, NB) as it:
                    for n, l in STEPS:
                        if n % 2 == 1 and l == 0:
                            state_act(act, it, n - 1)
                        powers_act(act, it, n, l)
                        if (n, l) != (0, 0) and round_at(*before(n, l)):
                            pos, r = round_at(*before(n, l))
                            if r < CONV:
                                sigmoid_act(act, it, pos, r)
                        if round_at(n, l):
                            evacuate_act(act, it, *round_at(n, l))
                        if l == 2 and n > 0:
                            oT_act(act, it, n - 1)
                        if l == 0 and n == CHUNKS - 1:
                            ab_act(act, it)
                        if l == 3:
                            n_act(act, it, n + 1)
                        if l == 4:
                            v_act(act, it, n + 1)
                        if l == 5 and n % 2 == 1:
                            k_act(act, it, n + 1)
                        if (n, l) == (5, 4):
                            xnT_act(act, it)
                    oT_act(act, it, CHUNKS - 1)

            @block.gpsimd
            def _(pool):
                ln_rstd_pool(core, pool, -1)
                for r in range(2, CONV):
                    silu(pool, -1, 3, r)
                with pool.Fori(0, NB) as it:
                    for n, l in STEPS:
                        if l == 1 and n > 0:
                            o_rstd_pool(pool, it, n - 1)
                        if (n, l) != (0, 0) and round_at(*before(n, l)):
                            pos, r = round_at(*before(n, l))
                            if 2 <= r < CONV:
                                silu(pool, it, pos, r)
                        if l == 2 and n > 0:
                            og_pool(pool, it, n - 1)
                        if (n, l) == (3, 4):
                            ln_rstd_pool(core, pool, it)
                        if l == 5 and n % 2 == 0:
                            kq_pool(pool, it, n + 1)
                    o_rstd_pool(pool, it, CHUNKS - 1)
                    og_pool(pool, it, CHUNKS - 1)

        core.ln_ran()



HD = D // H
HPC = 4
CH = H // HPC
ROUNDS = CH
FF = 1024
FC = FF // P
MR = 16


class Small:
    def __init__(self, ctx, core):
        sig = lambda name, per: Signal(ctx, core.nc, name, per)
        self.sumsq_ready = sig("sumsq_ready", NT)
        self.var2_ready = sig("var2_ready", 1)
        self.rms2_ready = sig("rms2_ready", 1)
        self.r_ready = sig("r_ready", NT)
        self.residual_added = sig("residual_added", 1)
        self.prep = [self.sumsq_ready, self.var2_ready, self.rms2_ready, self.r_ready,
                     self.residual_added]
        self.qk_in_psum = sig("qk_in_psum", ROUNDS)
        self.qk_products = sig("qk_products", ROUNDS)
        self.qk_ready = sig("qk_ready", ROUNDS)
        self.v_in_psum = sig("sv_in_psum", 1)
        self.v_ready = sig("sv_ready", 1)
        self.recip_ready = sig("s_recip_ready", 1)
        self.o_ready = sig("s_o_ready", 1)
        self.oT_in_psum = sig("s_oT_in_psum", 1)
        self.oT_ready = sig("s_oT_ready", 1)
        self.mod_in_psum = sig("mod_in_psum", 1)
        self.tanh_ready = sig("tanh_ready", 1)
        self.modh_ready = sig("modh_ready", 1)
        self.gate_up_in_psum = sig("gate_up_in_psum", FC // 2)
        self.gate_tanh = sig("gate_tanh", FC // 2)
        self.silu_ready = sig("silu_ready", FC // 2)
        self.act_ready = sig("act_ready", FC // 2)
        self.y_done = sig("s_y_done", 1)
        self.loop = [self.qk_in_psum, self.qk_products, self.qk_ready, self.v_in_psum, self.v_ready,
                     self.recip_ready, self.o_ready, self.oT_in_psum, self.oT_ready,
                     self.mod_in_psum, self.tanh_ready, self.modh_ready, self.gate_up_in_psum,
                     self.gate_tanh, self.silu_ready, self.act_ready, self.y_done]
        self.ffn_only = [self.mod_in_psum, self.tanh_ready, self.modh_ready, self.gate_up_in_psum,
                         self.gate_tanh, self.silu_ready, self.act_ready]


def small_sublayer(core, sm, g, ffn, call):
    nc, ins = core.nc, core.ins
    tag = "m_" if ffn else "b_"
    rope = not ffn
    with ExitStack() as ctx:
        def sb(name, shape, dt=F32):
            return ctx.enter_context(nc.sbuf_tensor(f"{tag}{call}_{name}", shape, dt))

        wq = sb("wq", [P, KC, CH, P])
        wk = sb("wk", [P, KC, CH, P])
        wv = sb("wv", [P, KC, D])
        loads = [(wq[:], "wq"), (wk[:], "wk"), (wv[:], "wv")]
        if ffn:
            wo = sb("wo", [P, KC, D])
            wa = sb("wa", [P, KC, MR])
            ln1 = sb("ln1", [P, KC])
            ln2 = sb("ln2", [P, KC])
            w_in = sb("w_in", [P, KC, FF])
            w_up = sb("w_up", [P, KC, FF])
            wb = sb("wb", [MR, FF])
            w_down = sb("w_down", [P, FC, D])
            woa = sb("woa", [P, KC, MR])
            wa2 = sb("wa2", [P, KC, MR])
            loads += [(wo[:], "wo"), (wa[:], "wa"), (ln1[:], "ln1"), (ln2[:], "ln2"),
                      (w_in[:], "w_in"), (w_up[:], "w_up"), (wb[:], "wb"), (w_down[:], "w_down")]
        else:
            wqs = sb("wqs", [P, KC, CH, P])
            wks = sb("wks", [P, KC, CH, P])
            bias_qk = sb("bias_qk", [1, 4, CH * P])
            bias_v = sb("bias_v", [1, D])
            bias_o = sb("bias_o", [1, D])
            wo = sb("wo", [P, KC, D])
            cos = sb("cos", [P, 2, T])
            sin = sb("sin", [P, 2, T])
            loads += [(wqs[:], "wqs"), (wks[:], "wks"), (bias_qk[:], "bias_qk"),
                      (bias_v[:], "bias_v"), (bias_o[:], "bias_o"), (wo[:], "wo"),
                      (cos[:], "cos"), (sin[:], "sin")]
            rope1 = sb("rope1", [P, 2, T])
            rope2 = sb("rope2", [P, 2, T])
        core.weights_count += 16 * len(loads)
        s0 = core.steps_count
        core.steps_count += 1 if ffn else 0

        with nc.Block() as block:
            @block.sync
            def _(sp):
                for dst, name in loads:
                    sp.dma_start(dst, ins[tag + name][:]).then_inc(core.weights_in, 16)
                sp.wait_ge(core.weights_in, core.weights_count)

            if ffn:
                @block.tensor
                def _(pe):
                    pe.wait_ge(core.weights_in, core.weights_count)
                    for e in range(KC):
                        for c in range(KC):
                            last = nc.tensor.matmul(core.bank[0][:, e * MR:(e + 1) * MR],
                                                    wo[:, c, e * P:(e + 1) * P], wa[:, c],
                                                    start=(c == 0), stop=(c == KC - 1))
                    last.then_inc(core.steps, 1)

                @block.vector
                def _(dve):
                    dve.wait_ge(core.weights_in, core.weights_count)
                    for c in range(KC):
                        for w in (wq, wk):
                            wc = w[:, c].rearrange("p a b -> p (a b)")
                            nc.vector.tensor_scalar(wc, wc, ln1[:, c:c + 1], None, ALU.mult)
                        nc.vector.tensor_scalar(wv[:, c], wv[:, c], ln1[:, c:c + 1], None, ALU.mult)
                        for w in (w_in, w_up):
                            nc.vector.tensor_scalar(w[:, c], w[:, c], ln2[:, c:c + 1], None, ALU.mult)
                        nc.vector.tensor_scalar(wa2[:, c], wa[:, c], ln2[:, c:c + 1], None, ALU.mult)
                    dve.wait_ge(core.steps, s0 + 1)
                    nc.vector.tensor_copy(woa[:].rearrange("p c r -> p (c r)"),
                                          core.bank[0][:, 0:KC * MR])

        if ffn:
            sumsq = sb("sumsq", [P, NT])
            squares = sb("squares", [P, NT, D])
            var2 = sb("var2", [P, NT])
            rms2 = sb("rms2", [P, NT])
            r = sb("r", [P, NT, D])
            tanh_mod = sb("tanh_mod", [MR, T])
            modh = sb("modh", [MR, T])
            gate_t = sb("gate_t", [P, 2, 2 * T])
            silu = sb("silu", [P, 2, 2 * T])
            hidden = sb("hidden", [P, FC // 2, 2 * T])
        qk = sb("qk", [P, ROUNDS, 2, T])
        v = sb("v", [P, NT, D])
        nmax = sb("nmax", [P, 2, NT])
        sums = sb("sums", [P, H, NT])
        recip = sb("recip", [P, H, NT])
        probs = sb("probs", [P, 2, SCORE_COLS])
        probsT = sb("probsT", [P, 2, SCORE_COLS])
        o = sb("o", [P, NT, D])
        oT = sb("oT", [P, KC, T])

        bank = core.bank
        b_prep, b_s, b_pT, b_o, b_y = bank[0], bank[3:5], bank[5], bank[6], bank[7]
        src, src_ready = (r, g.r_ready) if ffn else (core.xn, core.ln_out)

        def squares_act(act, it):
            for t in range(NT):
                act.wait_ge(*core.ln_out(it, t + 1))
                act.wait_ge(*g.var2_ready(it, 0))
                nc.scalar.activation(squares[:, t], core.xn[:, t], ACT.Square,
                                     accum_out=sumsq[:, t:t + 1]).then_inc(g.sumsq_ready.sem, 1)

        def var2_dve(dve, it):
            dve.wait_ge(*g.sumsq_ready(it, NT))
            nc.vector.tensor_scalar(var2[:], sumsq[:], 1.0 / D, 1e-6, ALU.mult, ALU.add)\
                .then_inc(g.var2_ready.sem, 1)

        def rms2_pool(pool, it):
            pool.wait_ge(*g.var2_ready(it, 1))
            pool.wait_ge(*g.r_ready(it, 0))
            nc.gpsimd.tensor_tensor(rms2[:], var2[:], core.minus_half[:, 0:NT], ALU.pow)\
                .then_inc(g.rms2_ready.sem, 1)

        def r_dve(dve, it):
            dve.wait_ge(*g.rms2_ready(it, 1))
            dve.wait_ge(*core.xnT_in_psum(it, 0))
            for t in range(NT):
                nc.vector.tensor_scalar(r[:, t], core.xn[:, t], rms2[:, t:t + 1], None, ALU.mult)\
                    .then_inc(g.r_ready.sem, 1)

        def residual_pool(pool, it, b):
            pool.wait_ge(*core.ln_out(it, NT))
            nc.gpsimd.tensor_tensor(core.x[:, b], core.x[:, b], core.xn[:], ALU.add)\
                .then_inc(g.residual_added.sem, 1)

        def transpose_pe(pe, it):
            pe.wait_ge(*src_ready(it, NT))
            pe.wait_ge(*core.xnT_ready(it, 0))
            if it is not -1:
                pe.wait_ge(*g.oT_ready(it, 1))
                pe.wait_ge(*g.v_ready(it, 1))
            transpose_tokens_pe(core, b_prep, src, src_ready, it).then_inc(core.xnT_in_psum.sem, 1)

        def xnT_act(act, it, used):
            act.wait_ge(*core.xnT_in_psum(it, 1))
            for u in used:
                act.wait_ge(*u)
            nc.scalar.copy(core.xnT[:].rearrange("p c t -> p (c t)"), b_prep[:, :])\
                .then_inc(core.xnT_ready.sem, 1)

        def main_bank(r_):
            return bank[1] if rope else bank[1 + r_ % 2]

        def project_pe(pe, it, r_):
            if r_ == 0:
                pe.wait_ge(*core.xnT_ready(it - 1, 1))
                if ffn:
                    pe.wait_ge(*g.act_ready(it, 0))
            if rope:
                pe.wait_ge(*g.qk_products(it, r_))
            else:
                pe.wait_ge(*g.qk_ready(it, r_ - 1))
            of_k = r_ // 2
            jobs = [((wq, wk)[of_k], main_bank(r_), of_k)]
            if rope:
                jobs.append(((wqs, wks)[of_k], bank[2], 2 + of_k))
            for w, out, bias_row in jobs:
                for n in range(2):
                    c4 = (r_ % 2) * 2 + n
                    dst = out[:, n * T:(n + 1) * T]
                    for c in range(KC):
                        last = nc.tensor.matmul(dst, w[:, c, c4], core.xnT[:, c], start=(c == 0),
                                                stop=(c == KC - 1 and not rope))
                    if rope:
                        last = nc.tensor.matmul(dst, bias_qk[:, bias_row, c4 * P:(c4 + 1) * P],
                                                core.ones_row[:], start=False, stop=True)
            last.then_inc(g.qk_in_psum.sem, 1)

        def project_v_pe(pe, it):
            pe.wait_ge(*core.xnT_ready(it - 1, 1))
            for t in range(NT):
                dst = b_prep[:, t * D:(t + 1) * D]
                for c in range(KC):
                    last = nc.tensor.matmul(dst, core.xnT[:, c, t * P:(t + 1) * P], wv[:, c],
                                            start=(c == 0), stop=(c == KC - 1 and not rope))
                if rope:
                    last = nc.tensor.matmul(dst, core.ones_row[:, 0:P], bias_v[:], start=False,
                                            stop=True)
            last.then_inc(g.v_in_psum.sem, 1)

        def v_act(act, it):
            act.wait_ge(*g.v_in_psum(it, 1))
            act.wait_ge(*sm.pv_done(it, 0))
            nc.scalar.copy(v[:].rearrange("p t d -> p (t d)"), b_prep[:, :])\
                .then_inc(g.v_ready.sem, 1)

        def qk_act(act, it, r_):
            act.wait_ge(*g.qk_in_psum(it, r_ + 1))
            act.wait_ge(*sm.scores_in_psum(it, 0))
            nc.scalar.mul(qk[:, r_].rearrange("p n t -> p (n t)"), main_bank(r_)[:, :],
                          HD ** -0.5 if r_ < 2 else 1.0).then_inc(g.qk_ready.sem, 1)

        def rope_dve(dve, it, r_):
            dve.wait_ge(*g.qk_in_psum(it, r_ + 1))
            dve.wait_ge(*g.qk_ready(it, r_))
            for table, src_bank, dst in ((cos, bank[1], rope1), (sin, bank[2], rope2)):
                last = nc.vector.tensor_tensor(
                    dst[:], src_bank[:, :].rearrange("p (n t) -> p n t", n=2),
                    table[:, r_ // 2:r_ // 2 + 1].broadcast_to([P, 2, T]), ALU.mult)
            last.then_inc(g.qk_products.sem, 1)

        def rope_pool(pool, it, r_):
            pool.wait_ge(*g.qk_products(it, r_ + 1))
            pool.wait_ge(*sm.scores_in_psum(it, 0))
            nc.gpsimd.tensor_tensor(qk[:, r_], rope1[:], rope2[:], ALU.add)\
                .then_inc(g.qk_ready.sem, 1)

        def head_rows(h):
            lo = 32 * (h % HPC)
            c4 = h // HPC
            return slice(lo, lo + HD), c4 // 2, c4 % 2

        def head_scores_pe(pe, it, h):
            if h == 0:
                pe.wait_ge(*g.qk_ready(it, ROUNDS))
                if ffn:
                    pe.wait_ge(*g.act_ready(it, 0))
            rows, r_, n = head_rows(h)
            scores_pe(core, pe, sm, it, h, b_s, lambda t: qk[rows, r_, n, t * P:(t + 1) * P],
                      lambda k: qk[rows, 2 + r_, n, 0:k])

        def head_pv_pe(pe, it, h):
            if h == 0:
                pe.wait_ge(*g.v_ready(it, 1))
                pe.wait_ge(*g.o_ready(it, 0))
            pv_pe(core, pe, sm, it, h, probsT,
                  lambda t: b_o[:, t * D + h * HD:t * D + (h + 1) * HD],
                  lambda kt: v[:, kt, h * HD:(h + 1) * HD])

        def probsT_dve(dve, it, h):
            dve.wait_ge(*sm.probsT_in_psum(it, h + 1))
            dve.wait_ge(*sm.pv_done(it, h - 1))
            nc.vector.tensor_copy(probsT[:, h % 2], b_pT[:, 0:SCORE_COLS])\
                .then_inc(sm.probsT_ready.sem, 1)

        def normalise_dve(dve, it):
            dve.wait_ge(*sm.pv_done(it, H))
            nc.vector.reciprocal(recip[:], sums[:]).then_inc(g.recip_ready.sem, 1)
            dve.wait_ge(*g.recip_ready(it, 1))
            dve.wait_ge(*g.oT_in_psum(it, 0))
            for t in range(NT):
                last = nc.vector.tensor_tensor(
                    o[:, t].rearrange("p (h c) -> p h c", h=H),
                    b_o[:, t * D:(t + 1) * D].rearrange("p (h c) -> p h c", h=H),
                    recip[:, :, t:t + 1].broadcast_to([P, H, HD]), ALU.mult)
            last.then_inc(g.o_ready.sem, 1)

        def transpose_o_pe(pe, it):
            pe.wait_ge(*g.o_ready(it, 1))
            pe.wait_ge(*g.v_ready(it, 1))
            transpose_tokens_pe(core, b_prep, o, g.o_ready, it).then_inc(g.oT_in_psum.sem, 1)

        def oT_act(act, it):
            act.wait_ge(*g.oT_in_psum(it, 1))
            act.wait_ge(*(g.mod_in_psum(it, 0) if ffn else g.y_done(it, 0)))
            nc.scalar.copy(oT[:].rearrange("p c t -> p (c t)"), b_prep[:, :])\
                .then_inc(g.oT_ready.sem, 1)

        def attention_out_pe(pe, it):
            pe.wait_ge(*g.oT_ready(it, 1))
            pe.wait_ge(*core.x_updated(it, 0))
            for t in range(NT):
                dst = b_y[:, t * D:(t + 1) * D]
                for c in range(KC):
                    nc.tensor.matmul(dst, oT[:, c, t * P:(t + 1) * P], wo[:, c], start=(c == 0),
                                     stop=False)
                last = nc.tensor.matmul(dst, core.ones_row[:, 0:P], bias_o[:], start=False,
                                        stop=True)
            last.then_inc(g.y_done.sem, 1)

        def gu_banks(f):
            return (bank[1], bank[2]) if f % 2 == 0 else (bank[3], bank[4])

        def gate_up_pe(pe, it, f):
            if f < 2:
                pe.wait_ge(*sm.probs_ready(it, H))
                pe.wait_ge(*g.qk_ready(it, ROUNDS))
            else:
                pe.wait_ge(*g.act_ready(it, f - 1))
            bg, bu = gu_banks(f)
            for n in range(2):
                cols = slice((2 * f + n) * P, (2 * f + n + 1) * P)
                for w, out in ((w_up, bu), (w_in, bg)):
                    for c in range(KC):
                        nc.tensor.matmul(out[:, n * T:(n + 1) * T], w[:, c, cols], core.xnT[:, c],
                                         start=(c == 0 and n == 0), stop=(w is w_up and c == KC - 1),
                                         skip_group_check=True)

        def modulate_pe(pe, it, f):
            if f == 0:
                pe.wait_ge(*g.modh_ready(it, 1))
            bg, bu = gu_banks(f)
            for n in range(2):
                last = nc.tensor.matmul(bg[:, n * T:(n + 1) * T],
                                        wb[:, (2 * f + n) * P:(2 * f + n + 1) * P], modh[:],
                                        start=False, stop=True, skip_group_check=True)
            last.then_inc(g.gate_up_in_psum.sem, 1)

        def mod_pe(pe, it):
            pe.wait_ge(*g.oT_ready(it, 1))
            pe.wait_ge(*sm.probsT_ready(it, H))
            for n, (w, act) in enumerate(((woa, oT), (wa2, core.xnT))):
                for c in range(KC):
                    last = nc.tensor.matmul(b_pT[0:MR, n * T:(n + 1) * T], w[:, c], act[:, c],
                                            start=(c == 0), stop=(c == KC - 1))
            last.then_inc(g.mod_in_psum.sem, 1)

        def tanh_act(act, it):
            act.wait_ge(*g.mod_in_psum(it, 1))
            act.wait_ge(*g.modh_ready(it, 0))
            nc.scalar.activation(tanh_mod[:], b_pT[0:MR, 0:T], ACT.Tanh)\
                .then_inc(g.tanh_ready.sem, 1)

        def modh_dve(dve, it):
            dve.wait_ge(*g.tanh_ready(it, 1))
            dve.wait_ge(*g.gate_up_in_psum(it, 0))
            nc.vector.scalar_tensor_tensor(out=modh[:], in0=tanh_mod[:], scalar=0.1,
                                           in1=b_pT[0:MR, T:2 * T], op0=ALU.mult, op1=ALU.mult)\
                .then_inc(g.modh_ready.sem, 1)

        def gate_act(act, it, f):
            act.wait_ge(*g.gate_up_in_psum(it, f + 1))
            act.wait_ge(*g.silu_ready(it, f - 1))
            nc.scalar.activation(gate_t[:, f % 2], gu_banks(f)[0][:, :], ACT.Tanh, scale=0.5)\
                .then_inc(g.gate_tanh.sem, 1)

        def silu_dve(dve, it, f):
            dve.wait_ge(*g.gate_tanh(it, f + 1))
            dve.wait_ge(*g.act_ready(it, f - 1))
            nc.vector.scalar_tensor_tensor(out=silu[:, f % 2], in0=gate_t[:, f % 2], scalar=1.0,
                                           in1=gu_banks(f)[0][:, :], op0=ALU.add, op1=ALU.mult)\
                .then_inc(g.silu_ready.sem, 1)

        def up_dve(dve, it, f):
            dve.wait_ge(*g.silu_ready(it, f + 1))
            dve.wait_ge(*g.y_done(it, 0))
            nc.vector.tensor_tensor(hidden[:, f], silu[:, f % 2], gu_banks(f)[1][:, :], ALU.mult)\
                .then_inc(g.act_ready.sem, 1)

        def down_pe(pe, it, f):
            pe.wait_ge(*g.act_ready(it, f + 1))
            if f == 0:
                pe.wait_ge(*core.x_updated(it, 0))
            for n in range(2):
                for t in range(NT):
                    last = nc.tensor.matmul(
                        b_y[:, t * D:(t + 1) * D],
                        hidden[:, f, n * T + t * P:n * T + (t + 1) * P], w_down[:, 2 * f + n],
                        start=(f == 0 and n == 0 and t == 0), stop=(f == FC // 2 - 1 and n == 1),
                        skip_group_check=True)
            if f == FC // 2 - 1:
                last.then_inc(g.y_done.sem, 1)

        with nc.Block() as block:
            @block.tensor
            def _(pe):
                transpose_pe(pe, -1)
                with pe.Fori(0, NB) as it:
                    for r_ in range(ROUNDS):
                        project_pe(pe, it, r_)
                    project_v_pe(pe, it)
                    for s in range(H + 2):
                        if s < H:
                            head_scores_pe(pe, it, s)
                        if 1 <= s <= H:
                            transpose_probs_pe(core, pe, sm, it, s - 1, b_pT, probs)
                        if s >= 2:
                            head_pv_pe(pe, it, s - 2)
                    if ffn:
                        gate_up_pe(pe, it, 0)
                        transpose_o_pe(pe, it)
                        gate_up_pe(pe, it, 1)
                        mod_pe(pe, it)
                        modulate_pe(pe, it, 0)
                        modulate_pe(pe, it, 1)
                        for f in range(FC // 2):
                            if f + 2 < FC // 2:
                                gate_up_pe(pe, it, f + 2)
                                modulate_pe(pe, it, f + 2)
                            down_pe(pe, it, f)
                    else:
                        transpose_o_pe(pe, it)
                        attention_out_pe(pe, it)
                    transpose_pe(pe, it)

            @block.vector
            def _(dve):
                def prepare(it, b, part):
                    if part == 0:
                        ln_stats_dve(core, dve, it, b)
                    if part == 1:
                        ln_normalize_dve(core, dve, it, b)
                    if ffn and part == 2:
                        var2_dve(dve, it)
                    if ffn and part == 3:
                        r_dve(dve, it)
                for part in range(4):
                    prepare(-1, 0, part)
                with dve.Fori(0, NB) as it:
                    if rope:
                        for r_ in range(ROUNDS):
                            rope_dve(dve, it, r_)
                    for s in range(H + 2):
                        if s < H:
                            max_dve(core, dve, sm, it, s, b_s, nmax)
                        if 1 <= s <= H:
                            probsT_dve(dve, it, s - 1)
                        if s in (2, 4, 6, 8):
                            prepare(it, it + 1, s // 2 - 1)
                    normalise_dve(dve, it)
                    if ffn:
                        modh_dve(dve, it)
                        for f in range(FC // 2):
                            silu_dve(dve, it, f)
                            up_dve(dve, it, f)
                    dve.wait_ge(*g.y_done(it, 1))
                    xb = core.x[:, it].rearrange("p t d -> p (t d)")
                    if ffn:
                        dve.wait_ge(*g.residual_added(it - 1, 1))
                    nc.vector.scalar_tensor_tensor(out=xb, in0=b_y[:, :], scalar=0.5 if ffn else 1.0,
                                                   in1=xb, op0=ALU.mult, op1=ALU.add)\
                        .then_inc(core.x_updated.sem, 1)

            @block.gpsimd
            def _(pool):
                def prepare(it, b):
                    ln_rstd_pool(core, pool, it)
                    if ffn:
                        residual_pool(pool, it, b)
                        rms2_pool(pool, it)
                prepare(-1, 0)
                with pool.Fori(0, NB) as it:
                    if rope:
                        for r_ in range(ROUNDS):
                            rope_pool(pool, it, r_)
                    prepare(it, it + 1)

            @block.scalar
            def _(act):
                if ffn:
                    squares_act(act, -1)
                xnT_act(act, -1, ())
                with act.Fori(0, NB) as it:
                    if ffn:
                        for r_ in range(ROUNDS):
                            qk_act(act, it, r_)
                    v_act(act, it)
                    for s in range(H + 1):
                        if s < H:
                            exp_act(core, act, sm, it, s, b_s, nmax, probs, sums,
                                    g.recip_ready(it, 0))
                        if ffn and s == 5:
                            squares_act(act, it)
                    oT_act(act, it)
                    if ffn:
                        tanh_act(act, it)
                        for f in range(FC // 2):
                            gate_act(act, it, f)
                    xnT_act(act, it, [g.v_in_psum(it, 1)] +
                            ([g.gate_up_in_psum(it, FC // 2)] if ffn else []))

        core.ln_ran()
        for s in sm.loop:
            s.ran(NB)
        for s in g.loop:
            if ffn or s not in g.ffn_only:
                s.ran(NB)
        if ffn:
            for s in g.prep:
                s.ran(NB + 1)
        if ffn:
            g.qk_products.ran(-NB)


def build(nc, ins, out):
    with ExitStack() as ctx:
        core = Core(ctx, nc, ins, None)
        mla = Mla(ctx, core)
        sm = Softmax(ctx, core)
        ternary = Ternary(ctx, core)
        small = Small(ctx, core)
        load_inputs(core)
        prime_signals(core, [*mla.prep, *small.prep],
                      [*mla.loop, *sm.loop, *ternary.loop, *small.loop])
        for call, s in enumerate(STAGES):
            if s == "mla0":
                mla_sublayer(core, sm, mla, "a0_")
            if s == "mla1":
                mla_sublayer(core, sm, mla, "a1_")
            if s.startswith("ffn"):
                ternary_sublayer(core, ternary, call)
            if s == "l1ffn":
                small_sublayer(core, sm, small, True, call)
            if s == "l1b":
                small_sublayer(core, sm, small, False, call)
            if s == "delta":
                delta_sublayer(core)
        done = ctx.enter_context(nc.semaphore("stored"))
        with nc.Block() as block:
            @block.sync
            def _(sp):
                for b in range(NB):
                    sp.dma_start(out[b], core.x[:, b]).then_inc(done, 16)
                sp.wait_ge(done, 16 * NB)



def layout(i):
    import numpy as np
    a = {k: np.asarray(v) for k, v in i.items()}
    f = {}
    tok = lambda w: np.ascontiguousarray(w)
    swap = np.r_[R // 2:R, 0:R // 2]

    def chunks(w, c=KC):
        return tok(w.reshape(c, P, w.shape[1]).transpose(1, 0, 2))

    f["x"] = tok(a["L0_attn_a_hidden_states"].reshape(NB, NT, P, D).transpose(0, 2, 1, 3))
    f["ident"] = np.eye(P, dtype=np.float32)
    f["mask"] = np.triu(np.full((P, P), MASKED, np.float32), 1)

    def mla(tag, qa, qln, qb, ckv, kpe, kvln, kvb, wo):
        f[tag + "q_nope"] = tok(qb[:, :P].transpose(1, 0, 2))
        pe_ = qb[:, P:].transpose(2, 0, 1)
        f[tag + "q_pe0"], f[tag + "q_pe1"] = tok(pe_[:P]), tok(pe_[P:])
        sw = pe_[:, :, swap]
        f[tag + "q_swap0"], f[tag + "q_swap1"] = tok(sw[:P]), tok(sw[P:])
        f[tag + "k_nope"] = tok(kvb[:, :P].transpose(1, 0, 2))
        f[tag + "w_v"] = tok(kvb[:, P:].transpose(1, 0, 2))
        f[tag + "w_o"] = tok(wo.transpose(1, 0, 2))
        f[tag + "w_lat"] = chunks(np.concatenate([qa, ckv, kpe, kpe[:, swap]], 1))
        f[tag + "norm_w"] = tok(np.broadcast_to(np.concatenate([qln, kvln]), (P, QL + CL)))

    g = lambda n: a["L0_attn_a_" + n]
    mla("a0_", g("q_a_w").T, g("q_a_ln_w"), g("q_b_w").reshape(H, 192, QL), g("kv_a_w")[:CL].T,
        g("kv_a_w")[CL:].T, g("kv_a_ln_w"), g("kv_b_w").reshape(H, 256, CL),
        g("o_w").T.reshape(H, P, D))
    g = lambda n: a["L1_attn_a_" + n]
    mla("a1_", g("Wq_a"), g("q_norm_w"), g("Wq_b").T.reshape(H, 192, QL), g("Wkv_a"), g("Wk_rope"),
        g("kv_norm_w"), g("Wkv_b").T.reshape(H, 256, CL), g("Wo").reshape(H, P, D))

    f["f0_w"] = chunks(a["L0_ffn_weight"].T)
    f["f0_b"] = tok(a["L0_ffn_bias"].reshape(1, D))

    def heads(w):
        wide = np.zeros((w.shape[0], H, 32), w.dtype)
        wide[:, :, :HD] = w.reshape(w.shape[0], H, HD)
        return wide.reshape(w.shape[0], CH * P)

    swap16 = lambda w: w.reshape(w.shape[0], H, HD)[:, :, np.r_[HD // 2:HD, 0:HD // 2]].reshape(w.shape)
    g = lambda n: a["L1_ffn_" + n]
    f["m_wq"] = chunks(heads(g("Wq").T)).reshape(P, KC, CH, P)
    f["m_wk"] = chunks(heads(g("Wk").T)).reshape(P, KC, CH, P)
    f["m_wv"], f["m_wo"], f["m_wa"] = chunks(g("Wv").T), chunks(g("Wo")), chunks(g("A"))
    f["m_ln1"], f["m_ln2"] = tok(g("ln1_w").reshape(KC, P).T), tok(g("ln2_w").reshape(KC, P).T)
    f["m_w_in"], f["m_w_up"] = chunks(g("W_in_base").T), chunks(g("W_up_base").T)
    f["m_wb"], f["m_w_down"] = g("B"), chunks(g("W_down").T, FC)
    g = lambda n: a["L1_attn_b_" + n]
    for n in "qk":
        w, b = g("W" + n).T, g("b" + n).reshape(1, D)
        f[f"b_w{n}"] = chunks(heads(w)).reshape(P, KC, CH, P)
        f[f"b_w{n}s"] = chunks(heads(swap16(w))).reshape(P, KC, CH, P)
    bq, bk = g("bq").reshape(1, D), g("bk").reshape(1, D)
    f["b_bias_qk"] = tok(np.stack([heads(bq), heads(bk), heads(swap16(bq)), heads(swap16(bk))], 1))
    f["b_wv"], f["b_wo"] = chunks(g("Wv").T), chunks(g("Wo").T)
    f["b_bias_v"], f["b_bias_o"] = tok(g("bv").reshape(1, D)), tok(g("bo").reshape(1, D))
    theta = np.float32(10000.0) ** (np.float32(-2.0) * np.arange(HD // 2, dtype=np.float32) / np.float32(HD))
    ang = (np.arange(1, T + 1, dtype=np.float32)[:, None] * theta[None, :]).astype(np.float32)
    cos = np.zeros((HPC, 32, 2, T), np.float32)
    sin = np.zeros((HPC, 32, 2, T), np.float32)
    for half in range(2):
        rows = slice(half * HD // 2, (half + 1) * HD // 2)
        for n, scale in enumerate((HD ** -0.5, 1.0)):
            cos[:, rows, n] = np.cos(ang).T * scale
            sin[:, rows, n] = np.sin(ang).T * (scale if half else -scale)
    f["b_cos"], f["b_sin"] = cos.reshape(P, 2, T), sin.reshape(P, 2, T)

    g = lambda n: a["L0_attn_b_" + n]
    for n in "qkvg":
        f["d_w" + n] = chunks(g("W" + n))
    f["d_wo"], f["d_wa"], f["d_wb"] = chunks(g("Wo"), H), chunks(g("Wa")), chunks(g("Wb"))
    f["d_ba"], f["d_bb"] = tok(g("ba").reshape(H, 1)), tok(g("bb").reshape(1, H))
    f["d_taps"] = tok(np.stack([g(f"conv_{n}_w").reshape(H, P, TAPS).transpose(1, 0, 2)
                                for n in "kqv"], 1))
    f["d_tap_bias"] = tok(np.stack([g(f"conv_{n}_b").reshape(H, P).T for n in "kqv"], 1))
    f["d_o_w"], f["d_o_b"] = tok(g("ln_w").reshape(P, 1)), tok(g("ln_b").reshape(P, 1))

    inv_freq = (1.0 / 10000.0 ** (np.arange(0, R, 2, dtype=np.float32) / np.float32(R))).astype(np.float32)
    ang = np.outer(np.arange(T, dtype=np.float32), inv_freq).astype(np.float32)
    cos = np.concatenate([np.cos(ang)] * 2, 1).astype(np.float32)
    sin = np.concatenate([-np.sin(ang), np.sin(ang)], 1).astype(np.float32)
    f["cosT"] = tok(np.concatenate([cos.T] * 2, 0))
    f["sinT"] = tok(np.concatenate([sin.T] * 2, 0))
    f["cos_tok"] = tok(cos.reshape(NT, P, R).transpose(1, 0, 2))
    f["sin_tok"] = tok(sin.reshape(NT, P, R).transpose(1, 0, 2))
    f["ms_scale"] = np.zeros((P, NT, 2), np.float32) + np.array([1.0 / QL, 1.0 / CL], np.float32)
    f["q_scale"] = np.zeros((P, NT, 2), np.float32) + np.array([192.0 ** -0.5, 1.0], np.float32)
    return f


def kernel(**inputs):
    import numpy as np
    import concourse.bacc as bacc
    from concourse.bass_utils import run_bass_kernel_spmd

    nc = bacc.Bacc("TRN2", target_bir_lowering=False, num_devices=1)
    arrays = {f"in_{k}": v for k, v in layout(inputs).items()}
    ins = {n[3:]: nc.dram_tensor(n, v.shape, mybir.dt.from_np(v.dtype), kind="ExternalInput").ap()
           for n, v in arrays.items()}
    out = nc.dram_tensor("out_x", (NB, P, NT, D), F32, kind="ExternalOutput").ap()
    build(nc, ins, out)
    r = run_bass_kernel_spmd(nc, [arrays], core_ids=[0])
    y = np.asarray(r.results[0]["out_x"])
    return np.ascontiguousarray(y.transpose(0, 2, 1, 3)).reshape(NB, T, D)
```

```python
import concourse.bass as bass
from concourse import mybir
from contextlib import ExitStack

F32 = mybir.dt.float32
BF16 = mybir.dt.bfloat16
ALU = mybir.AluOpType
ACT = mybir.ActivationFunctionType
AX = mybir.AxisListType

P = 128
NB = 8
T = 256
NT = T // P
D = 256
KC = D // P
H = 16
MASKED = -1.0e30


class Signal:

    def __init__(self, ctx, nc, name, per):
        self.sem = ctx.enter_context(nc.semaphore(name))
        self.per, self.base = per, 0

    def prime(self, eng, iterations):
        eng.sem_inc(self.sem, iterations * self.per)

    def __call__(self, it, k):
        return self.sem, it * self.per + (self.base + 2 * self.per + k)

    def ran(self, iterations):
        self.base += iterations * self.per


class Core:

    def __init__(self, ctx, nc, ins):
        def sb(name, shape, dt=F32):
            return ctx.enter_context(nc.sbuf_tensor(name, shape, dt))

        self.nc, self.ins, self.ctx = nc, ins, ctx
        self.x = sb("x", [P, NB + 1, NT, D])
        self.ident = sb("ident", [P, P])
        self.ident_bf = sb("ident_bf", [P, P], BF16)
        self.mask_bf = sb("mask_bf", [P, 2 * P], BF16)
        self.mask_f = sb("mask_f", [P, P])
        self.minus_half = sb("minus_half", [P, 16])
        self.ones_row = sb("ones_row", [1, T])
        self.stats = sb("stats", [P, NT, 6])
        self.mean_var = sb("mean_var", [P, NT, 2])
        self.carrier = sb("carrier", [P, 1])
        self.var_eps = sb("var_eps", [P, NT])
        self.rstd = sb("rstd", [P, NT])
        self.xn = sb("xn", [P, NT, D])
        self.xnT = sb("xnT", [P, KC, T])
        self.bank = [ctx.enter_context(nc.psum_tensor(f"bank{i}", [P, 512], F32)) for i in range(8)]
        self.ready = ctx.enter_context(nc.semaphore("constants_ready"))
        self.weights_in = ctx.enter_context(nc.semaphore("weights_in"))
        self.weights_count = 0
        self.steps = ctx.enter_context(nc.semaphore("setup_steps"))
        self.steps_count = 0
        sig = lambda name, per: Signal(ctx, nc, name, per)
        self.ln_stats = sig("ln_stats", NT)
        self.ln_mv = sig("ln_mv", NT)
        self.ln_var = sig("ln_var", 1)
        self.ln_rstd = sig("ln_rstd", 1)
        self.ln_out = sig("ln_out", NT)
        self.xnT_in_psum = sig("xnT_in_psum", 1)
        self.xnT_ready = sig("xnT_ready", 1)
        self.x_updated = sig("x_updated", 1)

    def ln_ran(self):
        for s in (self.ln_stats, self.ln_mv, self.ln_var, self.ln_rstd, self.ln_out,
                  self.xnT_in_psum, self.xnT_ready):
            s.ran(NB + 1)
        self.x_updated.ran(NB)


class Weights:

    def __init__(self, core, ctx, name, prefix):
        self.core, self.ctx, self.name, self.prefix = core, ctx, name, prefix
        self.loaded = ctx.enter_context(core.nc.semaphore(f"{name}_weights_in"))
        self.jobs, self.issued, self.prepared = [], False, False

    def load(self, name, shape):
        tensor = self.ctx.enter_context(self.core.nc.sbuf_tensor(f"{self.name}_{name}", shape, F32))
        self.jobs.append((tensor, self.prefix + name))
        return tensor

    def issue(self, sp):
        if not self.issued:
            for tensor, name in self.jobs:
                sp.dma_start(tensor[:], self.core.ins[name][:]).then_inc(self.loaded, 16)
        self.issued = True

    def wait(self, eng):
        eng.wait_ge(self.loaded, 16 * len(self.jobs))


def load_inputs(core):
    nc, ins = core.nc, core.ins
    with nc.Block() as block:
        @block.sync
        def _(sp):
            for b in range(NB):
                sp.dma_start(core.x[:, b], ins["x"][b]).then_inc(core.ready, 16)
            sp.dma_start(core.ident[:], ins["ident"][:]).then_inc(core.ready, 16)
            sp.dma_start(core.mask_f[:], ins["mask"][:]).then_inc(core.ready, 16)
            sp.wait_ge(core.ready, 16 * (NB + 2))

        @block.vector
        def _(dve):
            for s in (core.ln_stats, core.ln_mv, core.ln_var, core.ln_out):
                s.prime(dve, 1)
            core.x_updated.prime(dve, 2)
            dve.wait_ge(core.ready, 16 * (NB + 2))
            nc.vector.tensor_copy(core.ident_bf[:], core.ident[:])
            nc.vector.memset(core.mask_bf[:, 0:P], 0.0)
            nc.vector.tensor_copy(core.mask_bf[:, P:2 * P], core.mask_f[:])

        @block.gpsimd
        def _(pool):
            core.ln_rstd.prime(pool, 1)
            nc.gpsimd.memset(core.x[:, NB], 0.0)
            nc.gpsimd.memset(core.minus_half[:], -0.5)
            nc.gpsimd.memset(core.ones_row[:], 1.0)

        @block.scalar
        def _(act):
            core.xnT_ready.prime(act, 1)

        @block.tensor
        def _(pe):
            core.xnT_in_psum.prime(pe, 1)



def ln_stats_dve(core, dve, it, b):
    nc = core.nc
    for t in range(NT):
        nc.vector.bn_stats(core.stats[:, t], core.x[:, b, t]).then_inc(core.ln_stats.sem, 1)
    dve.wait_ge(*core.ln_stats(it, NT))
    nc.vector.memset(core.carrier[:], 0.0)
    for t in range(NT):
        nc.vector.bn_aggr(core.mean_var[:, t], core.stats[:, t]).then_inc(core.ln_mv.sem, 1)
    dve.wait_ge(*core.ln_mv(it, NT))
    nc.vector.tensor_scalar(core.var_eps[:], core.mean_var[:, :, 1], 1e-5, None,
                            ALU.add).then_inc(core.ln_var.sem, 1)


def ln_normalize_dve(core, dve, it, b):
    nc = core.nc
    dve.wait_ge(*core.ln_rstd(it, 1))
    dve.wait_ge(*core.xnT_in_psum(it, 0))
    for t in range(NT):
        nc.vector.tensor_scalar(core.xn[:, t], core.x[:, b, t], core.mean_var[:, t, 0:1],
                                core.rstd[:, t:t + 1], ALU.subtract,
                                ALU.mult).then_inc(core.ln_out.sem, 1)


def ln_rstd_pool(core, pool, it):
    pool.wait_ge(*core.ln_var(it, 1))
    pool.wait_ge(*core.ln_out(it, 0))
    core.nc.gpsimd.tensor_tensor(core.rstd[:], core.var_eps[:], core.minus_half[:, 0:NT],
                                 ALU.pow).then_inc(core.ln_rstd.sem, 1)


def transpose_tokens_pe(core, bank, src, ready, it):
    out = bank[:, :].rearrange("p (c t) -> p c t", c=KC)
    for t in range(NT):
        for c in range(KC):
            last = core.nc.tensor.transpose(out[:, c, t * P:(t + 1) * P], src[:, t, c * P:(c + 1) * P],
                                            core.ident[:])
    return last



QL = 192
QL1 = QL - P
CL = 64
R = 64
LAT = QL + CL + 2 * R
PAIRS = H // 2


class Mla:
    def __init__(self, ctx, core):
        nc = core.nc
        sig = lambda name, per: Signal(ctx, nc, name, per)
        self.lat_in_psum = sig("lat_in_psum", NT)
        self.lat_ready = sig("lat_ready", NT)
        self.squares_ready = sig("squares_ready", 2 * NT)
        self.ms_ready = sig("ms_ready", 1)
        self.ms_eps_ready = sig("ms_eps_ready", 1)
        self.rms_pow = sig("rms_pow", 1)
        self.rms_ready = sig("rms_ready", 1)
        self.norm_ready = sig("norm_ready", 2 * NT)
        self.kpe_products = sig("kpe_products", 2)
        self.kpe_ready = sig("kpe_ready", 1)
        self.latT_in_psum = sig("latT_in_psum", 2)
        self.latT_ready = sig("latT_ready", 2)
        self.v_ready = sig("v_ready", 1)
        self.q_in_psum = sig("q_in_psum", PAIRS)
        self.q_cos = sig("q_cos", PAIRS)
        self.q_sin = sig("q_sin", PAIRS)
        self.q_abs_ready = sig("q_abs_ready", PAIRS)
        self.q_rope_ready = sig("q_rope_ready", PAIRS)
        self.pv_in_psum = sig("pv_in_psum", PAIRS)
        self.recip_ready = sig("recip_ready", PAIRS)
        self.o_ready = sig("o_ready", PAIRS)
        self.oT_in_psum = sig("oT_in_psum", PAIRS)
        self.oT_ready = sig("oT_ready", PAIRS)
        self.y_done = sig("y_done", PAIRS)
        self.prep = [self.lat_in_psum, self.lat_ready, self.squares_ready, self.ms_ready,
                     self.ms_eps_ready, self.rms_pow, self.rms_ready, self.norm_ready,
                     self.kpe_products, self.kpe_ready, self.latT_in_psum, self.latT_ready,
                     self.v_ready]
        self.first_pair = [self.q_in_psum, self.q_cos, self.q_sin, self.q_abs_ready,
                           self.q_rope_ready]
        self.loop = [*self.first_pair, self.pv_in_psum, self.recip_ready, self.o_ready, self.oT_in_psum,
                     self.oT_ready, self.y_done]


class Softmax:

    def __init__(self, ctx, core):
        nc = core.nc
        self.scores_in_psum = Signal(ctx, nc, "scores_in_psum", H)
        self.max_ready = Signal(ctx, nc, "max_ready", H)
        self.probs_ready = Signal(ctx, nc, "probs_ready", H)
        self.probsT_in_psum = Signal(ctx, nc, "probsT_in_psum", H)
        self.probsT_ready = Signal(ctx, nc, "probsT_ready", H)
        self.pv_done = Signal(ctx, nc, "pv_done", H)
        self.loop = [self.scores_in_psum, self.max_ready, self.probs_ready, self.probsT_in_psum,
                     self.probsT_ready, self.pv_done]


def prime_signals(core, prepared, looped):
    with core.nc.Block() as block:
        @block.gpsimd
        def _(pool):
            for s in prepared:
                s.prime(pool, 1)
            for s in looped:
                s.prime(pool, 2)


SCORE_COLS = 3 * P


AHEAD = 4
LAG_T, LAG_V = 2, 3


def scores_pe(core, pe, sm, it, h, banks, q, k):
    nc = core.nc
    depth = len(banks)
    bank = banks[h % depth]
    pe.wait_ge(*sm.probs_ready(it, h + 1 - depth))
    nc.tensor.matmul(bank[:, 0:P], q(0), k(P), start=True, stop=False)
    nc.tensor.matmul(bank[:, 0:P], core.ident_bf[:], core.mask_bf[:, P:2 * P], start=False,
                     stop=True)
    nc.tensor.matmul(bank[:, P:3 * P], q(1), k(2 * P), start=True, stop=False)
    nc.tensor.matmul(bank[:, P:3 * P], core.ident_bf[:], core.mask_bf[:], start=False,
                     stop=True).then_inc(sm.scores_in_psum.sem, 1)


def max_dve(core, dve, sm, it, h, banks, nmax):
    nc = core.nc
    bank, buf = banks[h % len(banks)], h % AHEAD
    dve.wait_ge(*sm.scores_in_psum(it, h + 1))
    dve.wait_ge(*sm.probs_ready(it, h + 1 - AHEAD))
    nc.vector.tensor_reduce(nmax[:, buf, 0:1], bank[:, 0:P], AX.X, ALU.max, negate=True)
    nc.vector.tensor_reduce(nmax[:, buf, 1:2], bank[:, P:3 * P], AX.X, ALU.max,
                            negate=True).then_inc(sm.max_ready.sem, 1)


def exp_act(core, act, sm, it, h, banks, nmax, probs, sums, sums_free):
    nc = core.nc
    bank, buf = banks[h % len(banks)], h % AHEAD
    act.wait_ge(*sm.max_ready(it, h + 1))
    act.wait_ge(*sm.probsT_in_psum(it, h + 1 - AHEAD))
    act.wait_ge(*sums_free)
    nc.scalar.activation(probs[:, buf, 0:P], bank[:, 0:P], ACT.Exp, bias=nmax[:, buf, 0:1],
                         accum_out=sums[:, h, 0:1])
    nc.scalar.activation(probs[:, buf, P:3 * P], bank[:, P:3 * P], ACT.Exp,
                         bias=nmax[:, buf, 1:2],
                         accum_out=sums[:, h, 1:2]).then_inc(sm.probs_ready.sem, 1)


def transpose_probs_pe(core, pe, sm, it, h, banks, probs):
    nc = core.nc
    bank = banks[h % len(banks)]
    pe.wait_ge(*sm.probs_ready(it, h + 1))
    pe.wait_ge(*sm.probsT_ready(it, h + 1 - len(banks)))
    for j in range(3):
        last = nc.tensor.transpose(bank[:, j * P:(j + 1) * P],
                                   probs[:, h % AHEAD, j * P:(j + 1) * P],
                                   core.ident[:])
    last.then_inc(sm.probsT_in_psum.sem, 1)


def probsT_act(core, act, sm, it, h, banks, probsT):
    act.wait_ge(*sm.probsT_in_psum(it, h + 1))
    act.wait_ge(*sm.pv_done(it, h - 1))
    core.nc.scalar.copy(probsT[:, h % 2], banks[h % len(banks)][:, 0:SCORE_COLS])\
        .then_inc(sm.probsT_ready.sem, 1)


def pv_pe(core, pe, sm, it, h, probsT, out, v):
    nc = core.nc
    pe.wait_ge(*sm.probsT_ready(it, h + 1))
    nc.tensor.matmul(out(0), probsT[:, h % 2, 0:P], v(0), start=True, stop=True)
    nc.tensor.matmul(out(1), probsT[:, h % 2, P:2 * P], v(0), start=True, stop=False)
    last = nc.tensor.matmul(out(1), probsT[:, h % 2, 2 * P:3 * P], v(1), start=False, stop=True)
    last.then_inc(sm.pv_done.sem, 1)
    return last


def mla_sublayer(core, sm, g, tag, following):
    nc, ins = core.nc, core.ins
    with ExitStack() as ctx:
        def sb(name, shape, dt=F32):
            return ctx.enter_context(nc.sbuf_tensor(f"{tag}{name}", shape, dt))

        w_lat = sb("w_lat", [P, KC, LAT])
        norm_w = sb("norm_w", [P, QL + CL])
        wq0 = sb("wq0", [P, H, P])
        wq1 = sb("wq1", [QL1, H, P])
        w_out = sb("w_out", [P, PAIRS, D])
        cosT = sb("cosT", [P, T])
        sinT = sb("sinT", [P, T])
        cos_tok = sb("cos_tok", [P, NT, R])
        sin_tok = sb("sin_tok", [P, NT, R])
        ms_scale = sb("ms_scale", [P, NT, 2])
        q_scale = sb("q_scale", [P, NT, 2])

        with ExitStack() as stage_ctx:
            def stage(name, shape):
                return stage_ctx.enter_context(nc.sbuf_tensor(f"{tag}{name}", shape, F32))
            q_nope = stage("q_nope", [P, H, QL])
            k_nope = stage("k_nope", [P, H, CL])
            w_v = stage("w_v", [P, H, CL])
            w_o = stage("w_o", [P, H, D])
            s0 = core.steps_count
            loads = [(q_nope[:], "q_nope"), (k_nope[:], "k_nope"), (w_v[:], "w_v"), (w_o[:], "w_o"),
                     (w_lat[:], "w_lat"), (norm_w[:], "norm_w"), (wq0[:, :, CL:P], "q_pe0"),
                     (wq1[:, :, CL:P], "q_pe1")]
            tables = [(cosT[:], "cosT"), (sinT[:], "sinT"), (cos_tok[:], "cos_tok"),
                      (sin_tok[:], "sin_tok"), (ms_scale[:], "ms_scale"), (q_scale[:], "q_scale")]
            core.weights_count += 16 * (len(loads) + len(tables))

            with nc.Block() as block:
                @block.sync
                def _(sp):
                    for dst, name in loads:
                        sp.dma_start(dst, ins[f"{tag}{name}"][:]).then_inc(core.weights_in, 16)
                    for dst, name in tables:
                        sp.dma_start(dst, ins[name][:]).then_inc(core.weights_in, 16)

                @block.tensor
                def _(pe):
                    pe.wait_ge(core.weights_in, core.weights_count)
                    for half in range(2):
                        for c in range(2):
                            m = (P, QL1)[c]
                            for j in range(8):
                                h = half * 8 + j
                                last = nc.tensor.matmul(
                                    core.bank[2 * half + c][0:m, j * CL:(j + 1) * CL],
                                    q_nope[:, h, c * P:c * P + m], k_nope[:, h], start=True, stop=True)
                            last.then_inc(core.steps, 1)
                    for n in range(4):
                        for j in range(4):
                            h = 4 * n + j
                            lo = CL * (h % 2)
                            last = nc.tensor.matmul(
                                core.bank[4 + n][lo:lo + CL, (j // 2) * D:(j // 2 + 1) * D],
                                w_v[:, h], w_o[:, h], start=True, stop=True)
                        last.then_inc(core.steps, 1)

                @block.vector
                def _(dve):
                    for half in range(2):
                        for c, dst in ((0, wq0), (1, wq1)):
                            m = (P, QL1)[c]
                            dve.wait_ge(core.steps, s0 + 2 * half + c + 1)
                            nc.vector.tensor_copy(
                                dst[0:m, half * 8:half * 8 + 8, 0:CL],
                                core.bank[2 * half + c][0:m].rearrange("p (h c) -> p h c", h=8))

                @block.scalar
                def _(act):
                    for n in range(4):
                        act.wait_ge(core.steps, s0 + 5 + n)
                        nc.scalar.copy(w_out[:, 2 * n:2 * n + 2].rearrange("p a b -> p (a b)"),
                                       core.bank[4 + n][:, :])
            core.steps_count = s0 + 8

        lat = sb("lat", [P, NT, LAT])
        squares = sb("squares", [P, NT, QL + CL])
        sumsq = sb("sumsq", [P, NT, 2])
        ms = sb("ms", [P, NT, 2])
        ms_eps = sb("ms_eps", [P, NT, 2])
        inv_rms0 = sb("inv_rms0", [P, NT, 2])
        inv_rms = sb("inv_rms", [P, NT, 2])
        q_tok = sb("q_tok", [P, NT, QL])
        k_tok = sb("k_tok", [P, NT, CL + R])
        k_t1 = sb("k_t1", [P, NT, R])
        k_t2 = sb("k_t2", [P, NT, R])
        latT = sb("latT", [P, 2, T])
        qT1 = sb("qT1", [QL1, T])
        values = sb("values", [P, NT, CL])
        q = sb("q", [P, 2, 2, T])
        rope1 = sb("rope1", [P, 2, T])
        rope2 = sb("rope2", [P, 2, T])
        nmax = sb("nmax", [P, AHEAD, NT])
        sums = sb("sums", [P, H, NT])
        recip = sb("recip", [P, H, NT])
        probs = sb("probs", [P, AHEAD, SCORE_COLS])
        probsT = sb("probsT", [P, 2, SCORE_COLS])
        o = sb("o", [P, 2, NT, 2, CL])
        oT = sb("oT", [P, 2, T])

        b_prep, b_q, b_s, b_pT, b_o, b_y = (core.bank[0], core.bank[1], core.bank[3:5],
                                            [core.bank[5], core.bank[2]], core.bank[6],
                                            core.bank[7])
        pv_out = b_o[:, 0:2 * P].rearrange("p (t j c) -> p t j c", t=NT, j=2)

        def prep_rms_dve(dve, it):
            dve.wait_ge(*g.squares_ready(it, 2 * NT))
            nc.vector.tensor_tensor(ms[:], sumsq[:], ms_scale[:], ALU.mult)\
                .then_inc(g.ms_ready.sem, 1)
            dve.wait_ge(*g.ms_ready(it, 1))
            nc.vector.tensor_scalar(ms_eps[:], ms[:], 1e-6, None, ALU.add)\
                .then_inc(g.ms_eps_ready.sem, 1)

        def prep_norm_dve(dve, it):
            dve.wait_ge(*g.rms_ready(it, 1))
            dve.wait_ge(*g.latT_in_psum(it, 0))
            dve.wait_ge(*g.v_ready(it, 0))
            for t in range(NT):
                nc.vector.scalar_tensor_tensor(
                    out=q_tok[:, t], in0=lat[:, t, 0:QL], scalar=inv_rms[:, t, 0:1],
                    in1=norm_w[:, 0:QL], op0=ALU.mult, op1=ALU.mult).then_inc(g.norm_ready.sem, 1)
                nc.vector.scalar_tensor_tensor(
                    out=k_tok[:, t, 0:CL], in0=lat[:, t, QL:QL + CL], scalar=inv_rms[:, t, 1:2],
                    in1=norm_w[:, QL:QL + CL], op0=ALU.mult, op1=ALU.mult)\
                    .then_inc(g.norm_ready.sem, 1)

        def prep_latent_pool(pool, it):
            pool.wait_ge(*g.lat_ready(it, NT))
            nc.gpsimd.tensor_tensor(k_t1[:], lat[:, :, QL + CL:QL + CL + R], cos_tok[:],
                                    ALU.mult).then_inc(g.kpe_products.sem, 1)
            nc.gpsimd.tensor_tensor(k_t2[:], lat[:, :, QL + CL + R:LAT], sin_tok[:],
                                    ALU.mult).then_inc(g.kpe_products.sem, 1)
            pool.wait_ge(*g.kpe_products(it, 2))
            pool.wait_ge(*g.latT_in_psum(it, 0))
            nc.gpsimd.tensor_tensor(k_tok[:, :, CL:CL + R], k_t1[:], k_t2[:], ALU.add)\
                .then_inc(g.kpe_ready.sem, 1)
            pool.wait_ge(*g.ms_eps_ready(it, 1))
            nc.gpsimd.tensor_tensor(inv_rms0[:], ms_eps[:], core.minus_half[:, 0:2 * NT].rearrange(
                "p (t c) -> p t c", t=NT), ALU.pow).then_inc(g.rms_pow.sem, 1)
            pool.wait_ge(*g.rms_pow(it, 1))
            pool.wait_ge(*g.norm_ready(it, 0))
            nc.gpsimd.tensor_tensor(inv_rms[:], inv_rms0[:], q_scale[:], ALU.mult)\
                .then_inc(g.rms_ready.sem, 1)

        def prep_early_pe(pe, it):
            pe.wait_ge(*core.ln_out(it, NT))
            pe.wait_ge(*g.latT_ready(it, 0))
            transpose_tokens_pe(core, b_prep, core.xn, core.ln_out, it)\
                .then_inc(core.xnT_in_psum.sem, 1)

        def prep_lat_pe(pe, it, tiles):
            for t in tiles:
                if t == 0:
                    pe.wait_ge(*core.xnT_ready(it, 1))
                else:
                    pe.wait_ge(*g.lat_ready(it, t))
                for c in range(KC):
                    last = nc.tensor.matmul(b_prep[:, 0:LAT], core.xnT[:, c, t * P:(t + 1) * P],
                                            w_lat[:, c], start=(c == 0), stop=(c == KC - 1))
                last.then_inc(g.lat_in_psum.sem, 1)

        def prep_early_act(act, it):
            act.wait_ge(*core.xnT_in_psum(it, 1))
            act.wait_ge(*g.lat_in_psum(it, 0))
            nc.scalar.copy(core.xnT[:].rearrange("p c t -> p (c t)"), b_prep[:, :])\
                .then_inc(core.xnT_ready.sem, 1)

        def prep_lat_act(act, it, tiles):
            for t in tiles:
                if t == 0:
                    act.wait_ge(*g.norm_ready(it, 0))
                    act.wait_ge(*g.kpe_products(it, 0))
                act.wait_ge(*g.lat_in_psum(it, t + 1))
                nc.scalar.copy(lat[:, t], b_prep[:, 0:LAT]).then_inc(g.lat_ready.sem, 1)
            for t in tiles:
                act.wait_ge(*g.lat_ready(it, t + 1))
                nc.scalar.activation(squares[:, t, 0:QL], lat[:, t, 0:QL], ACT.Square,
                                     accum_out=sumsq[:, t, 0:1]).then_inc(g.squares_ready.sem, 1)
                nc.scalar.activation(squares[:, t, QL:QL + CL], lat[:, t, QL:QL + CL], ACT.Square,
                                     accum_out=sumsq[:, t, 1:2]).then_inc(g.squares_ready.sem, 1)

        def prep_late_pe(pe, it):
            pe.wait_ge(*g.norm_ready(it, 2 * NT))
            pe.wait_ge(*g.kpe_ready(it, 1))
            pe.wait_ge(*g.lat_ready(it, NT))
            for t in range(NT):
                nc.tensor.transpose(b_prep[:, t * P:(t + 1) * P], q_tok[:, t, 0:P], core.ident[:])
                last = nc.tensor.transpose(b_prep[:, T + t * P:T + (t + 1) * P], k_tok[:, t],
                                           core.ident[:])
            last.then_inc(g.latT_in_psum.sem, 1)
            pe.wait_ge(core.ready, 16)
            pe.wait_ge(*g.latT_ready(it, 1))
            for t in range(NT):
                last = nc.tensor.transpose(b_prep[0:QL1, t * P:(t + 1) * P], q_tok[:, t, P:QL],
                                           core.ident[:])
            last.then_inc(g.latT_in_psum.sem, 1)

        def prep_late_act(act, it, last_scores):
            act.wait_ge(*g.latT_in_psum(it, 1))
            act.wait_ge(*last_scores)
            nc.scalar.copy(latT[:].rearrange("p a t -> p (a t)"), b_prep[:, :])\
                .then_inc(g.latT_ready.sem, 1)
            act.wait_ge(*g.latT_in_psum(it, 2))
            nc.scalar.copy(qT1[:], b_prep[0:QL1, 0:T]).then_inc(g.latT_ready.sem, 1)

        def prep_late_dve(dve, it, last_pv):
            dve.wait_ge(*g.norm_ready(it, 2 * NT))
            dve.wait_ge(*last_pv)
            nc.vector.tensor_copy(values[:], k_tok[:, :, 0:CL]).then_inc(g.v_ready.sem, 1)

        def project_pe(pe, it, p):
            if p == 0:
                pe.wait_ge(*g.latT_ready(it - 1, 2))
            pe.wait_ge(*g.q_cos(it, p))
            pe.wait_ge(*g.q_sin(it, p))
            pe.wait_ge(*g.q_abs_ready(it, p))
            for j in range(2):
                h = 2 * p + j
                out = b_q[:, j * T:(j + 1) * T]
                nc.tensor.matmul(out, wq0[:, h], latT[:, 0], start=True, stop=False)
                last = nc.tensor.matmul(out, wq1[:, h], qT1[:], start=False, stop=True)
            last.then_inc(g.q_in_psum.sem, 1)

        def rope_dve(dve, it, p):
            dve.wait_ge(*g.q_in_psum(it, p + 1))
            dve.wait_ge(*g.q_rope_ready(it, p))
            nc.vector.tensor_tensor(
                rope1[CL:P], b_q[CL:P, :].rearrange("p (j t) -> p j t", j=2),
                cosT[CL:P].rearrange("p (j t) -> p j t", j=1).broadcast_to([R, 2, T]),
                ALU.mult).then_inc(g.q_cos.sem, 1)
            for lo in (CL, CL + R // 2):
                rows, other = slice(lo, lo + 32), slice(lo ^ 32, (lo ^ 32) + 32)
                last = nc.vector.tensor_tensor(
                    rope2[other], b_q[rows, :].rearrange("p (j t) -> p j t", j=2),
                    sinT[rows].rearrange("p (j t) -> p j t", j=1).broadcast_to([32, 2, T]),
                    ALU.mult)
            last.then_inc(g.q_sin.sem, 1)

        def rope_pool(pool, it, p):
            pool.wait_ge(*g.q_cos(it, p + 1))
            pool.wait_ge(*g.q_sin(it, p + 1))
            pool.wait_ge(*sm.scores_in_psum(it, 2 * p - 2))
            nc.gpsimd.tensor_tensor(q[CL:P, p % 2], rope1[CL:P], rope2[CL:P], ALU.add)\
                .then_inc(g.q_rope_ready.sem, 1)

        def abs_act(act, it, p):
            act.wait_ge(*g.q_in_psum(it, p + 1))
            act.wait_ge(*sm.scores_in_psum(it, 2 * p - 2))
            nc.scalar.copy(q[0:CL, p % 2].rearrange("p j t -> p (j t)"), b_q[0:CL, :])\
                .then_inc(g.q_abs_ready.sem, 1)

        def head_scores_pe(pe, it, h):
            if h % 2 == 0:
                pe.wait_ge(*g.q_abs_ready(it, h // 2 + 1))
                pe.wait_ge(*g.q_rope_ready(it, h // 2 + 1))
            scores_pe(core, pe, sm, it, h, b_s,
                      lambda t: q[:, (h // 2) % 2, h % 2, t * P:(t + 1) * P],
                      lambda n: latT[:, 1, 0:n])

        def head_pv_pe(pe, it, h):
            if h == 0:
                pe.wait_ge(*g.v_ready(it - 1, 1))
            if h % 2 == 0:
                pe.wait_ge(*g.oT_ready(it, h // 2))
            pv_pe(core, pe, sm, it, h, probsT, lambda t: pv_out[:, t, h % 2],
                  lambda kt: values[:, kt])

        def normalise_dve(dve, it, p):
            dve.wait_ge(*sm.pv_done(it, 2 * p + 2))
            nc.vector.reciprocal(recip[:, 2 * p:2 * p + 2], sums[:, 2 * p:2 * p + 2])\
                .then_inc(g.recip_ready.sem, 1)
            dve.wait_ge(*g.recip_ready(it, p + 1))
            dve.wait_ge(*g.oT_in_psum(it, p - 1))
            nc.vector.tensor_tensor(
                o[:, p % 2], pv_out,
                recip[:, 2 * p:2 * p + 2].rearrange("p j (t c) -> p t j c", c=1)
                .broadcast_to([P, NT, 2, CL]), ALU.mult).then_inc(g.o_ready.sem, 1)

        def transpose_o_pe(pe, it, p):
            pe.wait_ge(*g.o_ready(it, p + 1))
            for t in range(NT):
                last = nc.tensor.transpose(b_o[:, T + t * P:T + (t + 1) * P],
                                           o[:, p % 2, t].rearrange("p j c -> p (j c)"), core.ident[:])
            last.then_inc(g.oT_in_psum.sem, 1)

        def oT_dve(dve, it, p):
            dve.wait_ge(*g.oT_in_psum(it, p + 1))
            dve.wait_ge(*g.y_done(it, p))
            nc.vector.tensor_copy(oT[:, p % 2], b_o[:, T:2 * T])\
                .then_inc(g.oT_ready.sem, 1)

        def project_out_pe(pe, it, p):
            pe.wait_ge(*g.oT_ready(it, p + 1))
            if p == 0:
                pe.wait_ge(*core.x_updated(it, 0))
            for t in range(NT):
                last = nc.tensor.matmul(b_y[:, t * D:(t + 1) * D], oT[:, p % 2, t * P:(t + 1) * P],
                                        w_out[:, p], start=(p == 0 and t == 0),
                                        stop=(p == PAIRS - 1), skip_group_check=True)
            last.then_inc(g.y_done.sem, 1)

        with nc.Block() as block:
            def ahead(s):
                if s == 0:
                    return 1
                return (s + 3) // 2 if s % 2 == 1 and (s + 3) // 2 < PAIRS else None

            @block.sync
            def _(sp):
                for w_ in following:
                    w_.issue(sp)

            @block.tensor
            def _(pe):
                prep_early_pe(pe, -1)
                prep_lat_pe(pe, -1, range(NT))
                prep_late_pe(pe, -1)
                project_pe(pe, 0, 0)
                with pe.Fori(0, NB) as it:
                    for s in range(H + LAG_V):
                        if s < H:
                            head_scores_pe(pe, it, s)
                        if s % 2 == 0 and s >= 6:
                            project_out_pe(pe, it, s // 2 - 3)
                        if LAG_T <= s < H + LAG_T:
                            transpose_probs_pe(core, pe, sm, it, s - LAG_T, b_pT, probs)
                        if s % 2 == 1 and s >= 5:
                            transpose_o_pe(pe, it, s // 2 - 2)
                        if ahead(s):
                            project_pe(pe, it, ahead(s))
                        if LAG_V <= s:
                            head_pv_pe(pe, it, s - LAG_V)
                        if s == 4:
                            prep_early_pe(pe, it)
                        if s in (6, 8):
                            prep_lat_pe(pe, it, [s // 2 - 3])
                        if s == H:
                            prep_late_pe(pe, it)
                    project_pe(pe, it + 1, 0)
                    transpose_o_pe(pe, it, PAIRS - 1)
                    project_out_pe(pe, it, PAIRS - 1)

            @block.vector
            def _(dve):
                ln_stats_dve(core, dve, -1, 0)
                ln_normalize_dve(core, dve, -1, 0)
                prep_rms_dve(dve, -1)
                prep_norm_dve(dve, -1)
                prep_late_dve(dve, -1, sm.pv_done(-1, H))
                rope_dve(dve, 0, 0)
                with dve.Fori(0, NB) as it:
                    for s in range(H + LAG_V):
                        if s < H:
                            max_dve(core, dve, sm, it, s, b_s, nmax)
                        if s % 2 == 1 and s >= 5:
                            oT_dve(dve, it, s // 2 - 2)
                        if ahead(s):
                            rope_dve(dve, it, ahead(s))
                        if s % 2 == 0 and s >= 4:
                            normalise_dve(dve, it, s // 2 - 2)
                        if s == 1:
                            ln_stats_dve(core, dve, it, it + 1)
                        if s == 3:
                            ln_normalize_dve(core, dve, it, it + 1)
                        if s == 10:
                            prep_rms_dve(dve, it)
                        if s == 12:
                            prep_norm_dve(dve, it)
                    oT_dve(dve, it, PAIRS - 1)
                    rope_dve(dve, it + 1, 0)
                    prep_late_dve(dve, it, sm.pv_done(it, H))
                    dve.wait_ge(*g.y_done(it, PAIRS))
                    nc.vector.tensor_tensor(
                        core.x[:, it].rearrange("p t d -> p (t d)"),
                        core.x[:, it].rearrange("p t d -> p (t d)"), b_y[:, :], ALU.add)\
                        .then_inc(core.x_updated.sem, 1)

            @block.scalar
            def _(act):
                prep_early_act(act, -1)
                prep_lat_act(act, -1, range(NT))
                prep_late_act(act, -1, sm.scores_in_psum(-1, H))
                abs_act(act, 0, 0)
                with act.Fori(0, NB) as it:
                    for s in range(H + LAG_V):
                        if LAG_T <= s < H + LAG_T:
                            probsT_act(core, act, sm, it, s - LAG_T, b_pT, probsT)
                        if s < H:
                            exp_act(core, act, sm, it, s, b_s, nmax, probs, sums,
                                    g.recip_ready(it - 1, s // 2 + 1))
                        if ahead(s):
                            abs_act(act, it, ahead(s))
                        if s == 4:
                            prep_early_act(act, it)
                        if s in (6, 8):
                            prep_lat_act(act, it, [s // 2 - 3])
                        if s == H:
                            prep_late_act(act, it, sm.scores_in_psum(it, H))
                    abs_act(act, it + 1, 0)

            @block.gpsimd
            def _(pool):
                ln_rstd_pool(core, pool, -1)
                prep_latent_pool(pool, -1)
                pool.wait_ge(*g.rms_ready(-1, 1))
                rope_pool(pool, 0, 0)
                with pool.Fori(0, NB) as it:
                    for s in range(H + LAG_V):
                        if ahead(s):
                            if s == 3:
                                pool.wait_ge(*core.ln_rstd(it, 1))
                            if s == 11:
                                pool.wait_ge(*g.rms_ready(it, 1))
                            rope_pool(pool, it, ahead(s))
                        if s == 2:
                            pool.wait_ge(*g.q_rope_ready(it, 3))
                            ln_rstd_pool(core, pool, it)
                        if s == 10:
                            pool.wait_ge(*g.q_rope_ready(it, 7))
                            prep_latent_pool(pool, it)
                    rope_pool(pool, it + 1, 0)

        core.ln_ran()
        for s in g.prep:
            s.ran(NB + 1)
        for s in g.loop + sm.loop:
            s.ran(NB)
        for s in g.first_pair:
            s.base += 1



class Ternary:
    def __init__(self, ctx, core):
        self.y_in_psum = Signal(ctx, core.nc, "t_y_in_psum", 1)
        self.loop = [self.y_in_psum]


def ternary_sublayer(core, g, call, following):
    nc, ins = core.nc, core.ins
    with ExitStack() as ctx:
        def sb(name, shape, dt=F32):
            return ctx.enter_context(nc.sbuf_tensor(f"t{call}_{name}", shape, dt))

        w = sb("w", [P, KC, D])
        bias = sb("bias", [1, D])
        ones = sb("ones", [P, P])
        row_sum = sb("row_sum", [P, 1])
        scale = sb("scale", [P, 1])
        inv = sb("inv", [P, 2])
        z, up, down, wt, delta, w_ste = (sb(n, [P, KC, D]) for n in
                                         ("z", "up", "down", "wt", "delta", "w_ste"))
        core.weights_count += 32
        s0 = core.steps_count
        core.steps_count += 10

        with nc.Block() as block:
            @block.sync
            def _(sp):
                sp.dma_start(w[:], ins["f0_w"][:]).then_inc(core.weights_in, 16)
                sp.dma_start(bias[:], ins["f0_b"][:]).then_inc(core.weights_in, 16)

            @block.gpsimd
            def _(pool):
                nc.gpsimd.memset(ones[:], 1.0).then_inc(core.steps, 1)

            @block.tensor
            def _(pe):
                pe.wait_ge(core.steps, s0 + 2)
                nc.tensor.matmul(core.bank[0][:, 0:1], ones[:], row_sum[:], start=True, stop=True)\
                    .then_inc(core.steps, 1)

            @block.vector
            def _(dve):
                dve.wait_ge(core.weights_in, core.weights_count)
                nc.vector.tensor_reduce(row_sum[:], w[:], AX.XY, ALU.add,
                                        apply_absolute_value=True).then_inc(core.steps, 1)
                dve.wait_ge(core.steps, s0 + 3)
                nc.vector.tensor_scalar(scale[:], core.bank[0][:, 0:1], 1.0 / (D * D), None,
                                        ALU.mult).then_inc(core.steps, 1)
                dve.wait_ge(core.steps, s0 + 4)
                nc.vector.tensor_scalar(inv[:, 0:1], scale[:], 1e-10, None, ALU.add)\
                    .then_inc(core.steps, 1)
                dve.wait_ge(core.steps, s0 + 5)
                nc.vector.reciprocal(inv[:, 1:2], inv[:, 0:1]).then_inc(core.steps, 1)
                dve.wait_ge(core.steps, s0 + 6)
                nc.vector.tensor_scalar(z[:], w[:], inv[:, 1:2], None, ALU.mult)\
                    .then_inc(core.steps, 1)
                dve.wait_ge(core.steps, s0 + 7)
                nc.vector.tensor_scalar(up[:], z[:], 0.5, scale[:, 0:1], ALU.is_gt, ALU.mult)
                nc.vector.tensor_scalar(down[:], z[:], -0.5, scale[:, 0:1], ALU.is_lt, ALU.mult)\
                    .then_inc(core.steps, 1)
                dve.wait_ge(core.steps, s0 + 8)
                nc.vector.tensor_tensor(wt[:], up[:], down[:], ALU.subtract)\
                    .then_inc(core.steps, 1)
                dve.wait_ge(core.steps, s0 + 9)
                nc.vector.tensor_tensor(delta[:], wt[:], w[:], ALU.subtract)\
                    .then_inc(core.steps, 1)
                dve.wait_ge(core.steps, s0 + 10)
                nc.vector.tensor_tensor(w_ste[:], w[:], delta[:], ALU.add)

        b_prep, b_y = core.bank[0:2], core.bank[2:4]
        with nc.Block() as block:
            @block.sync
            def _(sp):
                for w_ in following:
                    w_.issue(sp)

            def transpose_pe(pe, it):
                pe.wait_ge(*core.ln_out(it, NT))
                pe.wait_ge(*core.xnT_ready(it, 0))
                transpose_tokens_pe(core, b_prep[0], core.xn, core.ln_out, it)\
                    .then_inc(core.xnT_in_psum.sem, 1)

            @block.tensor
            def _(pe):
                transpose_pe(pe, -1)
                with pe.Fori(0, NB) as it:
                    pe.wait_ge(*core.xnT_ready(it - 1, 1))
                    pe.wait_ge(*core.x_updated(it, 0))
                    for t in range(NT):
                        out = b_y[0][:, t * D:(t + 1) * D]
                        for c in range(KC):
                            nc.tensor.matmul(out, core.xnT[:, c, t * P:(t + 1) * P], w_ste[:, c],
                                             start=(c == 0), stop=False)
                        last = nc.tensor.matmul(out, core.ones_row[:, 0:P], bias[:], start=False,
                                                stop=True)
                    last.then_inc(g.y_in_psum.sem, 1)
                    transpose_pe(pe, it)

            @block.vector
            def _(dve):
                ln_stats_dve(core, dve, -1, 0)
                ln_normalize_dve(core, dve, -1, 0)
                with dve.Fori(0, NB) as it:
                    ln_stats_dve(core, dve, it, it + 1)
                    ln_normalize_dve(core, dve, it, it + 1)
                    dve.wait_ge(*g.y_in_psum(it, 1))
                    xb = core.x[:, it].rearrange("p t d -> p (t d)")
                    nc.vector.tensor_tensor(xb, xb, b_y[0][:, :], ALU.add)\
                        .then_inc(core.x_updated.sem, 1)

            @block.gpsimd
            def _(pool):
                ln_rstd_pool(core, pool, -1)
                with pool.Fori(0, NB) as it:
                    ln_rstd_pool(core, pool, it)

            @block.scalar
            def _(act):
                def copy(it):
                    act.wait_ge(*core.xnT_in_psum(it, 1))
                    act.wait_ge(*g.y_in_psum(it, 1))
                    nc.scalar.copy(core.xnT[:].rearrange("p c t -> p (c t)"), b_prep[0][:, :])\
                        .then_inc(core.xnT_ready.sem, 1)
                copy(-1)
                with act.Fori(0, NB) as it:
                    copy(it)

        core.ln_ran()
        for s in g.loop:
            s.ran(NB)



GH = 4
GROUPS = H // GH
CHUNKS = GROUPS * NT
LEVELS = 7
A_PER = LEVELS - 2
B_PER = LEVELS - 1
TAPS = 4
RPG = 8
CONV = 6
KSCALE = 128 ** -0.5


class Delta:
    def __init__(self, ctx, core):
        def sig(name, per, peeled=0):
            s = Signal(ctx, core.nc, name, per)
            s.start = 2 * per - peeled
            self.all.append(s)
            return s
        self.all = []
        self.ab_in_psum = sig("ab_in_psum", 1, 1)
        self.ab_ready = sig("ab_ready", 1, 1)
        self.proj_in_psum = sig("proj_in_psum", GROUPS * RPG, RPG)
        self.proj_out = sig("proj_out", GROUPS * RPG, RPG)
        self.tap_done = sig("tap_done", GROUPS * CONV * 3, CONV * 3)
        self.sigmoid_ready = sig("sigmoid_ready", GROUPS * CONV, CONV)
        self.qkv_ready = sig("qkv_ready", GROUPS * CONV, CONV)
        self.abc_in_psum = sig("abc_in_psum", CHUNKS, 1)
        self.decay_ready = sig("decay_ready", CHUNKS, 1)
        self.kk_in_psum = sig("kk_in_psum", CHUNKS, 1)
        self.nT_ready = sig("nT_ready", CHUNKS, 1)
        self.qk_in_psum = sig("d_qk_in_psum", CHUNKS, 1)
        self.pT_ready = sig("pT_ready", CHUNKS, 1)
        self.n_in_psum = sig("n_in_psum", CHUNKS, 1)
        self.n_ready = sig("n_ready", CHUNKS, 1)
        self.v_in_psum = sig("d_v_in_psum", CHUNKS, 1)
        self.v_ready = sig("d_v_ready", CHUNKS, 1)
        self.k_in_psum = sig("d_k_in_psum", GROUPS, 1)
        self.k_ready = sig("d_k_ready", GROUPS, 1)
        self.kq_decayed = sig("kq_decayed", GROUPS * 2)
        self.a_in_psum = sig("a_in_psum", CHUNKS * A_PER)
        self.a_ready = sig("a_ready", CHUNKS * A_PER)
        self.b_in_psum = sig("b_in_psum", CHUNKS * B_PER)
        self.b_ready = sig("b_ready", CHUNKS * B_PER)
        self.ay_in_psum = sig("ay_in_psum", CHUNKS * LEVELS)
        self.y_ready = sig("dy_ready", CHUNKS * LEVELS)
        self.ks_in_psum = sig("ks_in_psum", GROUPS)
        self.rhs_ready = sig("rhs_ready", GROUPS)
        self.yw_ready = sig("yw_ready", GROUPS)
        self.state_in_psum = sig("state_in_psum", GROUPS)
        self.state_ready = sig("state_ready", GROUPS)
        self.o_in_psum = sig("do_in_psum", CHUNKS)
        self.o_stats = sig("o_stats", CHUNKS)
        self.o_mv = sig("o_mv", CHUNKS)
        self.o_var = sig("o_var", CHUNKS)
        self.o_rstd = sig("o_rstd", CHUNKS)
        self.o_normal = sig("o_normal", CHUNKS)
        self.oT_in_psum = sig("doT_in_psum", CHUNKS)
        self.oT_affine = sig("oT_affine", CHUNKS)
        self.og_ready = sig("og_ready", CHUNKS)
        self.out_done = sig("out_done", CHUNKS)


def delta_weights(core, ctx):
    w = Weights(core, ctx, "d", "d_")
    HW = H * P
    w.k, w.q, w.v, w.g = (w.load(n, [P, KC, HW]) for n in ("wk", "wq", "wv", "wg"))
    w.o = w.load("wo", [P, H, D])
    w.a, w.b = w.load("wa", [P, KC, H]), w.load("wb", [P, KC, H])
    w.bias_a, w.bias_b = w.load("ba", [H, 1]), w.load("bb", [1, H])
    w.taps = w.load("taps", [P, 3, H, TAPS])
    w.tap_bias = w.load("tap_bias", [P, 3, H])
    w.ln_w, w.ln_b = w.load("o_w", [P, 1]), w.load("o_b", [P, 1])
    return w


def delta_sublayer(core, w):
    nc, ins = core.nc, core.ins
    with ExitStack() as ctx:
        def sb(name, shape, dt=F32):
            return ctx.enter_context(nc.sbuf_tensor(f"d_{name}", shape, dt))
        g = Delta(ctx, core)

        w_k, w_q, w_v, w_g, w_o, w_a, w_b = w.k, w.q, w.v, w.g, w.o, w.a, w.b
        b_a, b_b, taps, tap_bias, o_w, o_b = (w.bias_a, w.bias_b, w.taps, w.tap_bias, w.ln_w,
                                              w.ln_b)

        alphaT = sb("alphaT", [H, T])
        beta = sb("beta", [P, NT, H])
        raw, acc, sigm = (sb(n, [P, 2, 2, T]) for n in ("raw", "acc", "sigm"))
        kT, qT, vT, gT = (sb(n, [P, 2, GH, T]) for n in ("kT", "qT", "vT", "gT"))
        decay = sb("decay", [P, 2, GH, P + 1])
        g_decay = sb("g_decay", [P, GH, P + 1])
        zeros = sb("zeros", [P, P])
        nT0, n0, pT, v_tok = (sb(n, [P, 2, GH, P]) for n in ("nT0", "n0", "pT", "v_tok"))
        k_tok, kg, qg = (sb(n, [P, GH, P]) for n in ("k_tok", "kg", "qg"))
        pow_a, pow_b, y = (sb(n, [P, 2, GH, P]) for n in ("pow_a", "pow_b", "y"))
        yw, state = sb("yw", [P, GH, P]), sb("state", [P, GH, P])
        o_st, o_mv = sb("o_st", [P, GH, 6]), sb("o_mv", [P, GH, 2])
        o_var, o_rs = sb("o_var", [P, GH]), sb("o_rs", [P, GH])
        o_n, oT, og = (sb(n, [P, GH, P]) for n in ("o_n", "oT", "og"))

        b_proj, b_pre, b_a2, b_b2, b_y, b_o, b_abc, b_out = core.bank
        wide = lambda ap: ap.rearrange("p h t -> p (h t)")
        quad = lambda bank: bank[:, :].rearrange("p (h t) -> p h t", h=GH)

        with nc.Block() as block:
            @block.sync
            def _(sp):
                w.issue(sp)
                w.wait(sp)

            @block.gpsimd
            def _(pool):
                for s in g.all:
                    pool.sem_inc(s.sem, s.start)
                nc.gpsimd.memset(zeros[:], 0.0)
                nc.gpsimd.memset(decay[:, :, :, 0:1], 0.0)
                nc.gpsimd.memset(g_decay[:, :, 0:1], 1.0)

        def xnT_pe(pe, it):
            pe.wait_ge(*core.ln_out(it, NT))
            pe.wait_ge(*g.proj_out(it, 3 * RPG))
            transpose_tokens_pe(core, b_proj, core.xn, core.ln_out, it)\
                .then_inc(core.xnT_in_psum.sem, 1)

        def xnT_act(act, it):
            act.wait_ge(*core.xnT_in_psum(it, 1))
            act.wait_ge(*g.proj_in_psum(it, 3 * RPG))
            nc.scalar.copy(core.xnT[:].rearrange("p c t -> p (c t)"), b_proj[:, :])\
                .then_inc(core.xnT_ready.sem, 1)

        def ab_pe(pe, it):
            pe.wait_ge(*core.xnT_ready(it, 1))
            pe.wait_ge(*g.v_ready(it, 7))
            for c in range(KC):
                nc.tensor.matmul(b_pre[0:H, 0:T], w_a[:, c], core.xnT[:, c], start=(c == 0),
                                 stop=(c == KC - 1))
            for t in range(NT):
                out = b_pre[:, T + t * H:T + (t + 1) * H]
                for c in range(KC):
                    nc.tensor.matmul(out, core.xnT[:, c, t * P:(t + 1) * P], w_b[:, c],
                                     start=(c == 0), stop=False)
                last = nc.tensor.matmul(out, core.ones_row[:, 0:P], b_b[:], start=False, stop=True)
            last.then_inc(g.ab_in_psum.sem, 1)

        def ab_act(act, it):
            act.wait_ge(*g.ab_in_psum(it, 1))
            act.wait_ge(*g.abc_in_psum(it, 7))
            act.wait_ge(*g.pT_ready(it, 7))
            act.wait_ge(*g.yw_ready(it, GROUPS))
            nc.scalar.activation(alphaT[:], b_pre[0:H, 0:T], ACT.Sigmoid, bias=b_a[:])
            nc.scalar.activation(beta[:].rearrange("p t h -> p (t h)"), b_pre[:, T:T + NT * H],
                                 ACT.Sigmoid).then_inc(g.ab_ready.sem, 1)

        def round_of(pos, r):
            return pos * RPG + r, pos * CONV + r, (pos + 1) % GROUPS, (pos + 1) % 2

        def project_pe(pe, it, pos, r):
            n, _, grp, _ = round_of(pos, r)
            if r == 0:
                pe.wait_ge(*core.xnT_ready(it if pos == 3 else it - 1, 1))
            pe.wait_ge(*g.proj_out(it, n))
            weight = (w_k, w_q, w_v, w_g)[r // 2]
            for j in range(2):
                h = grp * GH + 2 * (r % 2) + j
                for c in range(KC):
                    last = nc.tensor.matmul(b_proj[:, j * T:(j + 1) * T], weight[:, c, h * P:(h + 1) * P],
                                            core.xnT[:, c], start=(c == 0), stop=(c == KC - 1))
            last.then_inc(g.proj_in_psum.sem, 1)

        def evacuate_act(act, it, pos, r):
            n, m, grp, buf = round_of(pos, r)
            act.wait_ge(*g.proj_in_psum(it, n + 1))
            if r >= CONV:
                act.wait_ge(*g.og_ready(it, 2 * pos))
                hp = 2 * (r % 2)
                nc.scalar.activation(wide(gT[:, buf, hp:hp + 2]), b_proj[:, :], ACT.Sigmoid)\
                    .then_inc(g.proj_out.sem, 1)
                return
            act.wait_ge(*g.qkv_ready(it, m - 1))
            for j in range(2):
                h = grp * GH + 2 * (r % 2) + j
                nc.scalar.activation(acc[:, r % 2, j], b_proj[:, j * T:(j + 1) * T], ACT.Identity,
                                     scale=taps[:, r // 2, h, 3:4], bias=tap_bias[:, r // 2, h:h + 1])
            nc.scalar.copy(wide(raw[:, r % 2]), b_proj[:, :]).then_inc(g.proj_out.sem, 1)

        def taps_dve(dve, it, pos, r):
            n, m, grp, buf = round_of(pos, r)
            dve.wait_ge(*g.proj_out(it, n + 1))
            for d in range(1, TAPS):
                if d > 1:
                    dve.wait_ge(*g.tap_done(it, 3 * m + d - 1))
                for j in range(2):
                    h = grp * GH + 2 * (r % 2) + j
                    last = nc.vector.scalar_tensor_tensor(
                        out=acc[:, r % 2, j, d:T], in0=raw[:, r % 2, j, 0:T - d],
                        scalar=taps[:, r // 2, h, 3 - d:4 - d], in1=acc[:, r % 2, j, d:T],
                        op0=ALU.mult, op1=ALU.add)
                last.then_inc(g.tap_done.sem, 1)

        def sigmoid_act(act, it, pos, r):
            _, m, _, _ = round_of(pos, r)
            act.wait_ge(*g.tap_done(it, 3 * m + 3))
            act.wait_ge(*g.qkv_ready(it, m - 1))
            nc.scalar.activation(wide(sigm[:, r % 2]), wide(acc[:, r % 2]), ACT.Sigmoid)\
                .then_inc(g.sigmoid_ready.sem, 1)

        def silu(eng, it, pos, r):
            _, m, _, buf = round_of(pos, r)
            hp = 2 * (r % 2)
            eng.wait_ge(*g.sigmoid_ready(it, m + 1))
            eng.wait_ge(*g.v_in_psum(it, 2 * pos - 1))
            eng.wait_ge(*g.k_in_psum(it, pos - 1))
            eng.wait_ge(*g.kq_decayed(it, 2 * pos))
            eng.wait_ge(*g.qkv_ready(it, m))
            if r < 2:
                nc.vector.scalar_tensor_tensor(
                    out=wide(kT[:, buf, hp:hp + 2]), in0=wide(acc[:, r % 2]), scalar=KSCALE,
                    in1=wide(sigm[:, r % 2]), op0=ALU.mult, op1=ALU.mult)\
                    .then_inc(g.qkv_ready.sem, 1)
            else:
                nc.gpsimd.tensor_tensor((qT if r < 4 else vT)[:, buf, hp:hp + 2], acc[:, r % 2],
                                        sigm[:, r % 2], ALU.mult).then_inc(g.qkv_ready.sem, 1)

        def where(m):
            grp, c = (m // 2) % GROUPS, m % 2
            return grp, c, grp % 2, m % 2, slice(c * P, (c + 1) * P)

        def kT_count(m):
            return ((m // 2) - 1) * CONV

        def decay_pe(pe, it, m):
            grp, c, hb, cb, tok = where(m)
            if m == CHUNKS:
                pe.wait_ge(*g.ab_ready(it, 1))
            pe.wait_ge(*g.decay_ready(it, m - 1))
            for j in range(GH):
                h = grp * GH + j
                last = nc.tensor.matmul(b_abc[:, j * P:(j + 1) * P],
                                        core.ident[0:H, h:h + 1].broadcast_to([H, P]),
                                        alphaT[:, tok], start=True, stop=True)
            last.then_inc(g.abc_in_psum.sem, 1)

        def decay_dve(dve, it, m):
            grp, c, hb, cb, tok = where(m)
            dve.wait_ge(*g.abc_in_psum(it, m))
            for j in range(GH):
                last = nc.vector.tensor_tensor_scan(
                    decay[:, cb, j, 1:P + 1], b_abc[:, j * P:(j + 1) * P], core.ident[:], 0.0,
                    ALU.mult, ALU.add)
            if c == 1:
                dve.wait_ge(*g.kq_decayed(it, m - 1))
                for j in range(GH):
                    last = nc.vector.tensor_tensor_scan(
                        g_decay[:, j, 1:P + 1], b_abc[:, j * P:(j + 1) * P], zeros[:], 1.0,
                        ALU.mult, ALU.add)
            last.then_inc(g.decay_ready.sem, 1)

        def kk_pe(pe, it, m):
            grp, c, hb, cb, tok = where(m)
            pe.wait_ge(*g.qkv_ready(it, kT_count(m) + 2))
            pe.wait_ge(*g.v_ready(it, m - 1))
            pe.wait_ge(*g.k_ready(it, (m - 1) // 2))
            if m == CHUNKS:
                pe.wait_ge(*g.ab_ready(it, 1))
            for j in range(GH):
                last = nc.tensor.matmul(b_pre[:, j * P:(j + 1) * P], kT[:, hb, j, tok],
                                        kT[:, hb, j, tok], start=True, stop=True)
            last.then_inc(g.kk_in_psum.sem, 1)

        def nT_dve(dve, it, m):
            grp, c, hb, cb, tok = where(m)
            dve.wait_ge(*g.kk_in_psum(it, m))
            dve.wait_ge(*g.decay_ready(it, m))
            dve.wait_ge(*g.b_in_psum(it, (m - 2) * B_PER + 1))
            dve.wait_ge(*g.ay_in_psum(it, (m - 2) * LEVELS + 1))
            for j in range(GH):
                h = grp * GH + j
                last = nc.vector.scalar_tensor_tensor(
                    out=nT0[:, cb, j], in0=b_pre[:, j * P:(j + 1) * P], scalar=beta[:, c, h:h + 1],
                    in1=decay[:, cb, j, 0:P], op0=ALU.mult, op1=ALU.mult)
            last.then_inc(g.nT_ready.sem, 1)

        def qk_pe(pe, it, m):
            grp, c, hb, cb, tok = where(m)
            pe.wait_ge(*g.qkv_ready(it, kT_count(m) + 4))
            pe.wait_ge(*g.nT_ready(it, m))
            for j in range(GH):
                last = nc.tensor.matmul(b_pre[:, j * P:(j + 1) * P], kT[:, hb, j, tok],
                                        qT[:, hb, j, tok], start=True, stop=True)
            last.then_inc(g.qk_in_psum.sem, 1)

        def pT_dve(dve, it, m):
            grp, c, hb, cb, tok = where(m)
            dve.wait_ge(*g.qk_in_psum(it, m))
            dve.wait_ge(*g.o_in_psum(it, m - 1))
            for j in range(GH):
                h = grp * GH + j
                last = nc.vector.scalar_tensor_tensor(
                    out=pT[:, cb, j], in0=b_pre[:, j * P:(j + 1) * P], scalar=beta[:, c, h:h + 1],
                    in1=decay[:, cb, j, 1:P + 1], op0=ALU.mult, op1=ALU.mult)
            last.then_inc(g.pT_ready.sem, 1)

        def n_pe(pe, it, m):
            cb = where(m)[3]
            pe.wait_ge(*g.nT_ready(it, m))
            pe.wait_ge(*g.pT_ready(it, m))
            for j in range(GH):
                last = nc.tensor.transpose(b_pre[:, j * P:(j + 1) * P], nT0[:, cb, j], core.ident[:])
            last.then_inc(g.n_in_psum.sem, 1)

        def n_act(act, it, m):
            cb = where(m)[3]
            act.wait_ge(*g.n_in_psum(it, m))
            act.wait_ge(*g.b_in_psum(it, (m - 2) * B_PER + 1))
            nc.scalar.copy(wide(n0[:, cb]), b_pre[:, :]).then_inc(g.n_ready.sem, 1)

        def v_pe(pe, it, m):
            grp, c, hb, cb, tok = where(m)
            pe.wait_ge(*g.qkv_ready(it, kT_count(m) + 6))
            pe.wait_ge(*g.n_ready(it, m))
            for j in range(GH):
                last = nc.tensor.transpose(b_pre[:, j * P:(j + 1) * P], vT[:, hb, j, tok],
                                           core.ident[:])
            last.then_inc(g.v_in_psum.sem, 1)

        def v_act(act, it, m):
            cb = where(m)[3]
            act.wait_ge(*g.v_in_psum(it, m))
            act.wait_ge(*g.y_ready(it, (m - 2) * LEVELS + 1))
            act.wait_ge(*g.ay_in_psum(it, (m - 2) * LEVELS + 1))
            nc.scalar.copy(wide(v_tok[:, cb]), b_pre[:, :]).then_inc(g.v_ready.sem, 1)

        def k_pe(pe, it, m):
            grp, c, hb, cb, tok = where(m)
            pe.wait_ge(*g.v_ready(it, m))
            for j in range(GH):
                last = nc.tensor.transpose(b_pre[:, j * P:(j + 1) * P], kT[:, hb, j, tok],
                                           core.ident[:])
            last.then_inc(g.k_in_psum.sem, 1)

        def k_act(act, it, m):
            act.wait_ge(*g.k_in_psum(it, m // 2))
            act.wait_ge(*g.state_in_psum(it, m // 2 - 1))
            nc.scalar.copy(wide(k_tok[:]), b_pre[:, :]).then_inc(g.k_ready.sem, 1)

        def kq_pool(pool, it, m):
            grp, c, hb, cb, tok = where(m)
            pool.wait_ge(*g.decay_ready(it, m))
            pool.wait_ge(*g.qkv_ready(it, kT_count(m) + 4))
            pool.wait_ge(*g.ks_in_psum(it, m // 2))
            pool.wait_ge(*g.o_in_psum(it, m - 1))
            nc.gpsimd.tensor_tensor(kg[:], kT[:, hb, :, tok], g_decay[:, :, 0:P], ALU.mult)\
                .then_inc(g.kq_decayed.sem, 1)
            nc.gpsimd.tensor_tensor(qg[:], qT[:, hb, :, tok], g_decay[:, :, 1:P + 1], ALU.mult)\
                .then_inc(g.kq_decayed.sem, 1)

        def level(n, l):
            cb = n % 2
            a = n0[:, cb] if l == 0 else pow_a[:, l % 2]
            b = nT0[:, cb] if l == 0 else pow_b[:, l % 2]
            y_in = (v_tok[:, cb] if cb == 0 else y[:, 1]) if l == 0 else y[:, (l + 1) % 2]
            return n * LEVELS + l, a, b, y_in, y[:, l % 2]

        def powers_ready(pe, it, n, l):
            at = level(n, l)[0]
            if l == 0:
                pe.wait_ge(*g.nT_ready(it, n))
                pe.wait_ge(*g.n_ready(it, n))
            else:
                pe.wait_ge(*g.a_ready(it, n * A_PER + min(l, A_PER)))
                pe.wait_ge(*g.b_ready(it, n * B_PER + min(l, B_PER)))

        def square_pe(pe, it, n, l):
            at, a, b, _, _ = level(n, l)
            powers_ready(pe, it, n, l)
            pe.wait_ge(*g.b_ready(it, n * B_PER + min(l, B_PER)))
            if l < LEVELS - 1:
                for j in range(GH):
                    last = nc.tensor.matmul(b_b2[:, j * P:(j + 1) * P], a[:, j], b[:, j],
                                            start=True, stop=True)
                last.then_inc(g.b_in_psum.sem, 1)

        def transpose_power_pe(pe, it, n, l):
            pe.wait_ge(*g.b_ready(it, n * B_PER + l + 1))
            pe.wait_ge(*g.a_ready(it, n * A_PER + l))
            for j in range(GH):
                last = nc.tensor.transpose(b_a2[:, j * P:(j + 1) * P], pow_b[:, (l + 1) % 2, j],
                                           core.ident[:])
            last.then_inc(g.a_in_psum.sem, 1)

        def apply_pe(pe, it, n, l):
            at, a, b, y_in, _ = level(n, l)
            if l == 0 and n % 2 == 0:
                pe.wait_ge(*g.v_ready(it, n))
            elif l == 0:
                pe.wait_ge(*g.rhs_ready(it, n // 2 + 1))
            else:
                pe.wait_ge(*g.y_ready(it, at))
            if l == LEVELS - 1:
                pe.wait_ge(*g.b_ready(it, (n + 1) * B_PER))
            pe.wait_ge(*g.y_ready(it, at))
            for j in range(GH):
                last = nc.tensor.matmul(b_y[:, j * P:(j + 1) * P], b[:, j], y_in[:, j],
                                        start=True, stop=True)
            last.then_inc(g.ay_in_psum.sem, 1)

        def square_act(act, it, n, l):
            act.wait_ge(*g.b_in_psum(it, n * B_PER + l + 1))
            act.wait_ge(*g.ay_in_psum(it, level(n, l)[0] - (l == 0)))
            act.wait_ge(*g.a_in_psum(it, n * A_PER + max(l - 1, 0)))
            nc.scalar.copy(wide(pow_b[:, (l + 1) % 2]), b_b2[:, :]).then_inc(g.b_ready.sem, 1)

        def transposed_act(act, it, n, l):
            act.wait_ge(*g.a_in_psum(it, n * A_PER + l + 1))
            act.wait_ge(*g.b_in_psum(it, n * B_PER + l))
            nc.scalar.copy(wide(pow_a[:, (l + 1) % 2]), b_a2[:, :]).then_inc(g.a_ready.sem, 1)

        def apply_dve(dve, it, n, l):
            at, _, _, y_in, y_out = level(n, l)
            dve.wait_ge(*g.ay_in_psum(it, at + 1))
            if l == 0:
                dve.wait_ge(*g.o_in_psum(it, n))
            dve.wait_ge(*g.y_ready(it, at))
            nc.vector.tensor_tensor(wide(y_out), wide(y_in), b_y[:, :],
                                    ALU.subtract if l == 0 else ALU.add).then_inc(g.y_ready.sem, 1)

        def yw_dve(dve, it, n):
            dve.wait_ge(*g.y_ready(it, (n + 1) * LEVELS))
            dve.wait_ge(*g.state_in_psum(it, n // 2))
            for j in range(GH):
                h = (n // 2) * GH + j
                last = nc.vector.tensor_scalar(yw[:, j], y[:, 0, j], decay[:, n % 2, j, P:P + 1],
                                               beta[:, 0, h:h + 1], ALU.mult, ALU.mult)
            last.then_inc(g.yw_ready.sem, 1)

        def state_pe(pe, it, n):
            grp = n // 2
            pe.wait_ge(*g.yw_ready(it, grp + 1))
            pe.wait_ge(*g.k_ready(it, grp))
            pe.wait_ge(*g.o_normal(it, n))
            pe.wait_ge(*g.oT_affine(it, n))
            for j in range(GH):
                last = nc.tensor.matmul(b_o[:, j * P:(j + 1) * P], k_tok[:, j], yw[:, j],
                                        start=True, stop=True)
            last.then_inc(g.state_in_psum.sem, 1)

        def state_act(act, it, n):
            grp = n // 2
            act.wait_ge(*g.state_in_psum(it, grp + 1))
            act.wait_ge(*g.ks_in_psum(it, grp))
            act.wait_ge(*g.o_in_psum(it, n))
            nc.scalar.copy(wide(state[:]), b_o[:, :]).then_inc(g.state_ready.sem, 1)

        def rhs_pe(pe, it, n):
            grp = n // 2
            pe.wait_ge(*g.state_ready(it, grp + 1))
            pe.wait_ge(*g.kq_decayed(it, 2 * grp + 2))
            pe.wait_ge(*g.y_ready(it, n * LEVELS))
            for j in range(GH):
                last = nc.tensor.matmul(b_y[:, j * P:(j + 1) * P], kg[:, j], state[:, j],
                                        start=True, stop=True)
            last.then_inc(g.ks_in_psum.sem, 1)

        def rhs_dve(dve, it, n):
            grp = n // 2
            dve.wait_ge(*g.ks_in_psum(it, grp + 1))
            dve.wait_ge(*g.v_ready(it, n))
            nc.vector.tensor_tensor(wide(y[:, 1]), wide(v_tok[:, 1]), b_y[:, :], ALU.subtract)\
                .then_inc(g.rhs_ready.sem, 1)

        def o_pe(pe, it, n):
            grp, c, hb, cb, tok = where(n)
            pe.wait_ge(*g.y_ready(it, (n + 1) * LEVELS))
            pe.wait_ge(*g.pT_ready(it, n))
            pe.wait_ge(*g.oT_affine(it, n))
            if c == 0:
                pe.wait_ge(*g.state_ready(it, grp + 1))
            for j in range(GH):
                out = b_o[:, j * P:(j + 1) * P]
                last = nc.tensor.matmul(out, pT[:, cb, j], y[:, 0, j], start=True, stop=(c == 0))
                if c == 1:
                    last = nc.tensor.matmul(out, qg[:, j], state[:, j], start=False, stop=True)
            last.then_inc(g.o_in_psum.sem, 1)

        def o_stats_dve(dve, it, n):
            dve.wait_ge(*g.o_in_psum(it, n + 1))
            for j in range(GH):
                last = nc.vector.bn_stats(o_st[:, j], b_o[:, j * P:(j + 1) * P])
            last.then_inc(g.o_stats.sem, 1)
            dve.wait_ge(*g.o_stats(it, n + 1))
            nc.vector.memset(core.carrier[:], 0.0)
            for j in range(GH):
                last = nc.vector.bn_aggr(o_mv[:, j], o_st[:, j])
            last.then_inc(g.o_mv.sem, 1)
            dve.wait_ge(*g.o_mv(it, n + 1))
            nc.vector.tensor_scalar(o_var[:], o_mv[:, :, 1], 1e-5, None, ALU.add)\
                .then_inc(g.o_var.sem, 1)

        def o_rstd_pool(pool, it, n):
            pool.wait_ge(*g.o_var(it, n + 1))
            pool.wait_ge(*g.o_normal(it, n))
            nc.gpsimd.tensor_tensor(o_rs[:], o_var[:], core.minus_half[:, 0:GH], ALU.pow)\
                .then_inc(g.o_rstd.sem, 1)

        def o_normal_dve(dve, it, n):
            dve.wait_ge(*g.o_rstd(it, n + 1))
            dve.wait_ge(*g.oT_in_psum(it, n))
            for j in range(GH):
                last = nc.vector.tensor_scalar(o_n[:, j], b_o[:, j * P:(j + 1) * P],
                                               o_mv[:, j, 0:1], o_rs[:, j:j + 1], ALU.subtract,
                                               ALU.mult)
            last.then_inc(g.o_normal.sem, 1)

        def oT_pe(pe, it, n):
            pe.wait_ge(*g.o_normal(it, n + 1))
            for j in range(GH):
                last = nc.tensor.transpose(b_o[:, j * P:(j + 1) * P], o_n[:, j], core.ident[:])
            last.then_inc(g.oT_in_psum.sem, 1)

        def oT_act(act, it, n):
            act.wait_ge(*g.oT_in_psum(it, n + 1))
            act.wait_ge(*g.og_ready(it, n))
            nc.scalar.activation(wide(oT[:]), b_o[:, :], ACT.Identity, scale=o_w[:], bias=o_b[:])\
                .then_inc(g.oT_affine.sem, 1)

        def og_pool(pool, it, n):
            grp, c, hb, cb, tok = where(n)
            pool.wait_ge(*g.oT_affine(it, n + 1))
            pool.wait_ge(*g.proj_out(it, grp * RPG))
            pool.wait_ge(*g.out_done(it, n))
            nc.gpsimd.tensor_tensor(og[:], oT[:], gT[:, hb, :, tok], ALU.mult)\
                .then_inc(g.og_ready.sem, 1)

        def out_pe(pe, it, n):
            grp, c, hb, cb, tok = where(n)
            pe.wait_ge(*g.og_ready(it, n + 1))
            if n == 0:
                pe.wait_ge(*core.x_updated(it, 0))
            for j in range(GH):
                last = nc.tensor.matmul(b_out[:, c * D:(c + 1) * D], og[:, j], w_o[:, grp * GH + j],
                                        start=(n == 0 and j == 0),
                                        stop=(grp == GROUPS - 1 and j == GH - 1),
                                        skip_group_check=True)
            last.then_inc(g.out_done.sem, 1)

        STEPS = [(n, l) for n in range(CHUNKS) for l in range(LEVELS)]
        ROUND_LEVELS = (0, 1, 3, 4)
        XNT_STEP = (5, 6)
        round_at = lambda n, l: (
            (n // 2, (n % 2) * 4 + ROUND_LEVELS.index(l)) if l in ROUND_LEVELS else None)


        def round_due(n, l, after_taps):
            for steps in range(1, 4):
                at = n * LEVELS + l - steps
                found = round_at(at // LEVELS, at % LEVELS) if at >= 0 else None
                late = 2 if at % LEVELS == ROUND_LEVELS[-1] else 1
                if found and found[1] < CONV and late + after_taps == steps:
                    return found
            return None

        with nc.Block() as block:
            @block.tensor
            def _(pe):
                def preamble(it, m):
                    decay_pe(pe, it, m)
                    kk_pe(pe, it, m)
                    qk_pe(pe, it, m)
                    n_pe(pe, it, m)
                    v_pe(pe, it, m)
                    k_pe(pe, it, m)
                xnT_pe(pe, -1)
                ab_pe(pe, -1)
                for r in range(RPG):
                    project_pe(pe, -1, 3, r)
                preamble(-1, CHUNKS)
                square_pe(pe, 0, 0, 0)
                with pe.Fori(0, NB) as it:
                    for n, l in STEPS:
                        if l > 0 and l < LEVELS - 1:
                            square_pe(pe, it, n, l)
                        if l == LEVELS - 1:
                            square_pe(pe, it, n + 1, 0)
                        if round_at(n, l):
                            project_pe(pe, it, *round_at(n, l))
                        if l == 0 and n % 2 == 1:
                            state_pe(pe, it, n - 1)
                        if l == 1:
                            kk_pe(pe, it, n + 1)
                        if l == 2 and n > 0:
                            oT_pe(pe, it, n - 1)
                        if l < LEVELS - 2:
                            transpose_power_pe(pe, it, n, l)
                        if l == 0 and n > 0:
                            o_pe(pe, it, n - 1)
                        if l == 0 and n == CHUNKS - 1:
                            ab_pe(pe, it)
                        if l == 0:
                            decay_pe(pe, it, n + 1)
                        if l == 0 and n % 2 == 1:
                            rhs_pe(pe, it, n)
                        apply_pe(pe, it, n, l)
                        if l == 2:
                            qk_pe(pe, it, n + 1)
                        if l == 4 and n > 0:
                            out_pe(pe, it, n - 1)
                        if l == 3:
                            n_pe(pe, it, n + 1)
                        if l == 5:
                            v_pe(pe, it, n + 1)
                        if l == 6 and n % 2 == 1 and n < CHUNKS - 1:
                            k_pe(pe, it, n + 1)
                        if (n, l) == XNT_STEP:
                            xnT_pe(pe, it)
                    o_pe(pe, it, CHUNKS - 1)
                    k_pe(pe, it, CHUNKS)
                    oT_pe(pe, it, CHUNKS - 1)
                    out_pe(pe, it, CHUNKS - 1)

            @block.vector
            def _(dve):
                ln_stats_dve(core, dve, -1, 0)
                ln_normalize_dve(core, dve, -1, 0)
                for r in range(RPG):
                    if r < CONV:
                        taps_dve(dve, -1, 3, r)
                    if r < 2:
                        silu(dve, -1, 3, r)
                decay_dve(dve, -1, CHUNKS)
                nT_dve(dve, -1, CHUNKS)
                pT_dve(dve, -1, CHUNKS)
                with dve.Fori(0, NB) as it:
                    for n, l in STEPS:
                        if n % 2 == 1 and l == 0:
                            rhs_dve(dve, it, n)
                        apply_dve(dve, it, n, l)
                        if l == 0 and n > 0:
                            o_stats_dve(dve, it, n - 1)
                        if l == 1 and n > 0:
                            o_normal_dve(dve, it, n - 1)
                        silu_round = round_due(n, l, 1)
                        if silu_round and silu_round[1] < 2:
                            silu(dve, it, *silu_round)
                        if l == 0:
                            decay_dve(dve, it, n + 1)
                        if l == 1:
                            nT_dve(dve, it, n + 1)
                        if l == 2:
                            pT_dve(dve, it, n + 1)
                        if l == LEVELS - 1 and n % 2 == 0:
                            yw_dve(dve, it, n)
                        if round_due(n, l, 0):
                            taps_dve(dve, it, *round_due(n, l, 0))
                        if (n, l) == (2, 5):
                            ln_stats_dve(core, dve, it, it + 1)
                        if (n, l) == (3, 5):
                            ln_normalize_dve(core, dve, it, it + 1)
                    o_stats_dve(dve, it, CHUNKS - 1)
                    o_normal_dve(dve, it, CHUNKS - 1)
                    dve.wait_ge(*g.out_done(it, CHUNKS))
                    xb = core.x[:, it].rearrange("p t d -> p (t d)")
                    nc.vector.tensor_tensor(xb, xb, b_out[:, :], ALU.add)\
                        .then_inc(core.x_updated.sem, 1)

            @block.scalar
            def _(act):
                xnT_act(act, -1)
                ab_act(act, -1)
                for r in range(RPG):
                    evacuate_act(act, -1, 3, r)
                    if r < CONV:
                        sigmoid_act(act, -1, 3, r)
                n_act(act, -1, CHUNKS)
                v_act(act, -1, CHUNKS)
                k_act(act, -1, CHUNKS)
                square_act(act, 0, 0, 0)
                with act.Fori(0, NB) as it:
                    for n, l in STEPS:
                        if l > 0 and l < LEVELS - 1:
                            square_act(act, it, n, l)
                        if l == LEVELS - 1:
                            square_act(act, it, n + 1, 0)
                        if l == 0 and n % 2 == 1:
                            state_act(act, it, n - 1)
                        if l < LEVELS - 2:
                            transposed_act(act, it, n, l)
                        if l == 3:
                            n_act(act, it, n + 1)
                        if round_at(n, l):
                            evacuate_act(act, it, *round_at(n, l))
                        if round_due(n, l, 1):
                            sigmoid_act(act, it, *round_due(n, l, 1))
                        if l == 2 and n > 0:
                            oT_act(act, it, n - 1)
                        if l == 0 and n == CHUNKS - 1:
                            ab_act(act, it)
                        if l == 5:
                            v_act(act, it, n + 1)
                        if l == 6 and n % 2 == 1 and n < CHUNKS - 1:
                            k_act(act, it, n + 1)
                        if (n, l) == XNT_STEP:
                            xnT_act(act, it)
                    k_act(act, it, CHUNKS)
                    oT_act(act, it, CHUNKS - 1)

            @block.gpsimd
            def _(pool):
                ln_rstd_pool(core, pool, -1)
                for r in range(2, CONV):
                    silu(pool, -1, 3, r)
                with pool.Fori(0, NB) as it:
                    for n, l in STEPS:
                        if l == 1 and n > 0:
                            o_rstd_pool(pool, it, n - 1)
                        silu_round = round_due(n, l, 1)
                        if silu_round and silu_round[1] >= 2:
                            silu(pool, it, *silu_round)
                        if l == 2 and n > 0:
                            og_pool(pool, it, n - 1)
                        if (n, l) == (3, 4):
                            ln_rstd_pool(core, pool, it)
                        if l == 5 and n % 2 == 0:
                            kq_pool(pool, it, n + 1)
                    o_rstd_pool(pool, it, CHUNKS - 1)
                    og_pool(pool, it, CHUNKS - 1)

        core.ln_ran()



HD = D // H
HPC = 4
CH = H // HPC
HPR = P // HD
ROUNDS = H // HPR
FF = 1024
FC = FF // P
MR = 16
LAG_NT, LAG_NV = 3, 4


class Small:
    def __init__(self, ctx, core):
        sig = lambda name, per: Signal(ctx, core.nc, name, per)
        self.sumsq_ready = sig("sumsq_ready", NT)
        self.var2_ready = sig("var2_ready", 1)
        self.rms2_ready = sig("rms2_ready", 1)
        self.r_ready = sig("r_ready", NT)
        self.residual_added = sig("residual_added", 1)
        self.prep = [self.sumsq_ready, self.var2_ready, self.rms2_ready, self.r_ready,
                     self.residual_added]
        self.qk_in_psum = sig("qk_in_psum", ROUNDS)
        self.qk_products = sig("qk_products", ROUNDS)
        self.qk_ready = sig("qk_ready", ROUNDS)
        self.qm_ready = sig("qm_ready", H)
        self.v_in_psum = sig("sv_in_psum", 1)
        self.v_ready = sig("sv_ready", 1)
        self.recip_ready = sig("s_recip_ready", H)
        self.probs_normal = sig("probs_normal", H)
        self.oT_ready = sig("s_oT_ready", CH)
        self.mod_in_psum = sig("mod_in_psum", 1)
        self.tanh_ready = sig("tanh_ready", 1)
        self.modh_ready = sig("modh_ready", 1)
        self.gate_up_in_psum = sig("gate_up_in_psum", FC // 2)
        self.gate_tanh = sig("gate_tanh", FC // 2)
        self.silu_ready = sig("silu_ready", FC // 2)
        self.act_ready = sig("act_ready", FC // 2)
        self.y_done = sig("s_y_done", 1)
        self.loop = [self.qk_in_psum, self.qk_products, self.qk_ready, self.qm_ready, self.v_in_psum, self.v_ready,
                     self.recip_ready, self.probs_normal, self.oT_ready,
                     self.mod_in_psum, self.tanh_ready, self.modh_ready, self.gate_up_in_psum,
                     self.gate_tanh, self.silu_ready, self.act_ready, self.y_done]
        self.ffn_only = [self.mod_in_psum, self.tanh_ready, self.modh_ready, self.gate_up_in_psum,
                         self.gate_tanh, self.silu_ready, self.act_ready]


def small_weights(core, ctx, ffn):
    w = Weights(core, ctx, "m" if ffn else "b", "m_" if ffn else "b_")
    w.q, w.k = (w.load(n, [P, KC, ROUNDS, P]) for n in ("wq", "wk"))
    w.v = w.load("wv", [P, KC, D])
    w.own_rows = w.load("own_rows", [P, HPR])
    if ffn:
        w.o = w.load("wo", [P, KC, CH * P])
        w.a = w.load("wa", [P, KC, MR])
        w.ln1, w.ln2 = w.load("ln1", [P, KC]), w.load("ln2", [P, KC])
        w.w_in, w.w_up = w.load("w_in", [P, KC, FF]), w.load("w_up", [P, KC, FF])
        w.b = w.load("wb", [MR, FF])
        w.down = w.load("w_down", [P, FC, D])
        w.oa = ctx.enter_context(core.nc.sbuf_tensor("m_woa", [P, CH, MR], F32))
        w.a2 = ctx.enter_context(core.nc.sbuf_tensor("m_wa2", [P, KC, MR], F32))
    else:
        w.bias_qk = w.load("bias_qk", [P, 2, ROUNDS])
        w.bias_v = w.load("bias_v", [P, CH])
        w.bias_o = w.load("bias_o", [P, 1, D])
        w.o = w.load("wo", [P, CH, D])
        w.cos, w.sin = (w.load(n, [P, 2, T]) for n in ("cos", "sin"))
    return w


def small_sublayer(core, sm, g, ffn, call, weights):
    nc = core.nc
    tag = "m_" if ffn else "b_"
    rope = not ffn
    with ExitStack() as ctx:
        def sb(name, shape, dt=F32):
            return ctx.enter_context(nc.sbuf_tensor(f"{tag}{call}_{name}", shape, dt))

        wq, wk, wv, wo, own_rows = weights.q, weights.k, weights.v, weights.o, weights.own_rows
        if ffn:
            wa, ln1, ln2, w_in, w_up = (weights.a, weights.ln1, weights.ln2, weights.w_in,
                                        weights.w_up)
            wb, w_down, woa, wa2 = weights.b, weights.down, weights.oa, weights.a2
        else:
            bias_qk, bias_v, bias_o = weights.bias_qk, weights.bias_v, weights.bias_o
            cos, sin = weights.cos, weights.sin
            rope1 = sb("rope1", [P, 2, T])
            rope2 = sb("rope2", [P, 2, T])
        v = sb("v", [P, NT, H, 32])
        prepare_weights = ffn and not weights.prepared
        weights.prepared = True
        s0 = core.steps_count
        core.steps_count += 1 if prepare_weights else 0

        with nc.Block() as block:
            @block.sync
            def _(sp):
                weights.issue(sp)
                weights.wait(sp)

            if prepare_weights:
                @block.tensor
                def _(pe):
                    weights.wait(pe)
                    for e in range(CH):
                        for c in range(KC):
                            last = nc.tensor.matmul(core.bank[0][:, e * MR:(e + 1) * MR],
                                                    wo[:, c, e * P:(e + 1) * P], wa[:, c],
                                                    start=(c == 0), stop=(c == KC - 1))
                    last.then_inc(core.steps, 1)

                @block.vector
                def _(dve):
                    weights.wait(dve)
                    for c in range(KC):
                        for w in (wq, wk):
                            wc = w[:, c].rearrange("p a b -> p (a b)")
                            nc.vector.tensor_scalar(wc, wc, ln1[:, c:c + 1], None, ALU.mult)
                        nc.vector.tensor_scalar(wv[:, c], wv[:, c], ln1[:, c:c + 1], None, ALU.mult)
                        for w in (w_in, w_up):
                            nc.vector.tensor_scalar(w[:, c], w[:, c], ln2[:, c:c + 1], None, ALU.mult)
                        nc.vector.tensor_scalar(wa2[:, c], wa[:, c], ln2[:, c:c + 1], None, ALU.mult)
                    dve.wait_ge(core.steps, s0 + 1)
                    nc.vector.tensor_copy(woa[:].rearrange("p c r -> p (c r)"),
                                          core.bank[0][:, 0:CH * MR])

            @block.gpsimd
            def _(pool):
                nc.gpsimd.memset(v[:], 0.0)

        if ffn:
            sumsq = sb("sumsq", [P, NT])
            squares = sb("squares", [P, NT, D])
            var2 = sb("var2", [P, NT])
            rms2 = sb("rms2", [P, NT])
            r = sb("r", [P, NT, D])
            tanh_mod = sb("tanh_mod", [MR, T])
            modh = sb("modh", [MR, T])
            gate_t = sb("gate_t", [P, 2, 2 * T])
            silu = sb("silu", [P, 2, 2 * T])
            hidden = sb("hidden", [P, FC // 2, 2 * T])
        qk = sb("qk", [P, ROUNDS, 2, T])
        qm = sb("qm", [P, AHEAD, T])
        nmax = sb("nmax", [P, AHEAD, NT])
        sums = sb("sums", [P, H, NT])
        recip = sb("recip", [P, H, NT])
        probs = sb("probs", [P, AHEAD, SCORE_COLS])
        probsT = sb("probsT", [P, 2, SCORE_COLS])
        oT = sb("oT", [P, CH, T])

        bank = core.bank
        b_prep, b_y = bank[0], bank[7]
        b_o = [bank[6], b_prep]
        b_s = bank[3:5] + bank[1:3]
        b_pT = [bank[5], b_y]
        src, src_ready = (r, g.r_ready) if ffn else (core.xn, core.ln_out)

        def squares_act(act, it):
            for t in range(NT):
                act.wait_ge(*core.ln_out(it, t + 1))
                act.wait_ge(*g.var2_ready(it, 0))
                nc.scalar.activation(squares[:, t], core.xn[:, t], ACT.Square,
                                     accum_out=sumsq[:, t:t + 1]).then_inc(g.sumsq_ready.sem, 1)

        def var2_dve(dve, it):
            dve.wait_ge(*g.sumsq_ready(it, NT))
            nc.vector.tensor_scalar(var2[:], sumsq[:], 1.0 / D, 1e-6, ALU.mult, ALU.add)\
                .then_inc(g.var2_ready.sem, 1)

        def rms2_pool(pool, it):
            pool.wait_ge(*g.var2_ready(it, 1))
            pool.wait_ge(*g.r_ready(it, 0))
            nc.gpsimd.tensor_tensor(rms2[:], var2[:], core.minus_half[:, 0:NT], ALU.pow)\
                .then_inc(g.rms2_ready.sem, 1)

        def r_dve(dve, it):
            dve.wait_ge(*g.rms2_ready(it, 1))
            dve.wait_ge(*core.xnT_in_psum(it, 0))
            for t in range(NT):
                nc.vector.tensor_scalar(r[:, t], core.xn[:, t], rms2[:, t:t + 1], None, ALU.mult)\
                    .then_inc(g.r_ready.sem, 1)

        def residual_pool(pool, it, b):
            pool.wait_ge(*core.ln_out(it, NT))
            nc.gpsimd.tensor_tensor(core.x[:, b], core.x[:, b], core.xn[:], ALU.add)\
                .then_inc(g.residual_added.sem, 1)

        def transpose_pe(pe, it, first=False):
            pe.wait_ge(*src_ready(it, NT))
            pe.wait_ge(*core.xnT_ready(it, 0))
            if not first:
                pe.wait_ge(*g.oT_ready(it, CH))
                pe.wait_ge(*g.v_ready(it, 1))
            transpose_tokens_pe(core, b_prep, src, src_ready, it).then_inc(core.xnT_in_psum.sem, 1)

        def xnT_act(act, it, used):
            act.wait_ge(*core.xnT_in_psum(it, 1))
            for u in used:
                act.wait_ge(*u)
            nc.scalar.copy(core.xnT[:].rearrange("p c t -> p (c t)"), b_prep[:, :])\
                .then_inc(core.xnT_ready.sem, 1)

        def project_pe(pe, it, r_):
            if r_ == 0:
                pe.wait_ge(*core.xnT_ready(it - 1, 1))
                if ffn:
                    pe.wait_ge(*g.act_ready(it, 0))
                else:
                    pe.wait_ge(*sm.probs_ready(it, 0))
            for n, w in enumerate((wq, wk)):
                for c in range(KC):
                    last = nc.tensor.matmul(bank[1 + r_][:, n * T:(n + 1) * T], w[:, c, r_],
                                            core.xnT[:, c], start=(c == 0), stop=(c == KC - 1))
            last.then_inc(g.qk_in_psum.sem, 1)

        def project_v_pe(pe, it):
            pe.wait_ge(*core.xnT_ready(it - 1, 1))
            for t in range(NT):
                dst = b_prep[:, t * D:(t + 1) * D]
                for c in range(KC):
                    last = nc.tensor.matmul(dst, core.xnT[:, c, t * P:(t + 1) * P], wv[:, c],
                                            start=(c == 0), stop=(c == KC - 1))
            last.then_inc(g.v_in_psum.sem, 1)

        def v_act(act, it):
            act.wait_ge(*g.v_in_psum(it, 1))
            act.wait_ge(*sm.pv_done(it, 0))
            nc.scalar.copy(v[:, :, :, 0:HD],
                           b_prep[:, :].rearrange("p (t h c) -> p t h c", t=NT, h=H))\
                .then_inc(g.v_ready.sem, 1)

        def bias_pool(pool, it, b):
            pool.wait_ge(*core.ln_out(it, NT))
            nc.gpsimd.tensor_tensor(core.x[:, b], core.x[:, b], bias_o[:].broadcast_to([P, NT, D]),
                                    ALU.add).then_inc(g.residual_added.sem, 1)

        def qk_act(act, it, r_):
            act.wait_ge(*g.qk_in_psum(it, r_ + 1))
            act.wait_ge(*sm.scores_in_psum(it, 0))
            act.wait_ge(*g.qm_ready(it, 0))
            nc.scalar.copy(qk[:, r_].rearrange("p n t -> p (n t)"), bank[1 + r_][:, :])\
                .then_inc(g.qk_ready.sem, 1)

        def rope_dve(dve, it, r_):
            dve.wait_ge(*g.qk_in_psum(it, r_ + 1))
            dve.wait_ge(*g.qk_ready(it, r_))
            for n in range(2):
                src_ = bank[1 + r_][:, n * T:(n + 1) * T]
                bias = bias_qk[:, n, r_:r_ + 1]
                nc.vector.scalar_tensor_tensor(out=rope1[:, n], in0=src_, scalar=bias,
                                               in1=cos[:, n], op0=ALU.add, op1=ALU.mult)
                for lo in range(0, P, 32):
                    rows, other = slice(lo, lo + 32), slice(lo ^ 32, (lo ^ 32) + 32)
                    last = nc.vector.scalar_tensor_tensor(
                        out=rope2[other, n], in0=src_[rows], scalar=bias[rows], in1=sin[rows, n],
                        op0=ALU.add, op1=ALU.mult)
            last.then_inc(g.qk_products.sem, 1)

        def rope_pool(pool, it, r_):
            pool.wait_ge(*g.qk_products(it, r_ + 1))
            pool.wait_ge(*sm.scores_in_psum(it, 0))
            pool.wait_ge(*g.qm_ready(it, 0))
            nc.gpsimd.tensor_tensor(qk[:, r_], rope1[:], rope2[:], ALU.add)\
                .then_inc(g.qk_ready.sem, 1)

        def own_rows_act(act, it, h):
            act.wait_ge(*g.qk_ready(it, h // HPR + 1))
            act.wait_ge(*sm.scores_in_psum(it, h + 1 - AHEAD))
            nc.scalar.mul(qm[:, h % AHEAD], qk[:, h // HPR, 0], own_rows[:, h % HPR:h % HPR + 1])\
                .then_inc(g.qm_ready.sem, 1)

        def head_scores_pe(pe, it, h):
            if h == 0 and ffn:
                pe.wait_ge(*g.act_ready(it, 0))
            if h == 2:
                pe.wait_ge(*g.qk_ready(it, ROUNDS))
            pe.wait_ge(*g.qm_ready(it, h + 1))
            scores_pe(core, pe, sm, it, h, b_s, lambda t: qm[:, h % AHEAD, t * P:(t + 1) * P],
                      lambda k: qk[:, h // HPR, 1, 0:k])

        def recip_dve(dve, it, h):
            dve.wait_ge(*sm.probs_ready(it, h + 1))
            dve.wait_ge(*g.probs_normal(it, 0))
            nc.vector.reciprocal(recip[:, h], sums[:, h]).then_inc(g.recip_ready.sem, 1)

        def normalise_pool(pool, it, h):
            pool.wait_ge(*g.recip_ready(it, h + 1))
            for tile, (lo, hi) in enumerate(((0, P), (P, 3 * P))):
                block = probs[:, h % AHEAD, lo:hi]
                last = nc.gpsimd.tensor_tensor(
                    block, block, recip[:, h, tile:tile + 1].broadcast_to([P, hi - lo]), ALU.mult)
            last.then_inc(g.probs_normal.sem, 1)

        def head_pv_pe(pe, it, h):
            c4, j = h // HPC, h % HPC
            if h == 0:
                pe.wait_ge(*g.v_ready(it, 1))
            if j == 0:
                pe.wait_ge(*g.oT_ready(it, c4 - 1))
            pe.wait_ge(*sm.probsT_ready(it, h + 1))
            out = b_o[c4 % 2][32 * j:32 * (j + 1), 0:T]
            nc.tensor.matmul(out[:, 0:P], v[:, 0, h], probsT[:, h % 2, 0:P], start=True, stop=True,
                             tile_position=(0, 32 * j))
            nc.tensor.matmul(out[:, P:T], v[:, 0, h], probsT[:, h % 2, P:2 * P], start=True,
                             stop=False, tile_position=(0, 32 * j))
            nc.tensor.matmul(out[:, P:T], v[:, 1, h], probsT[:, h % 2, 2 * P:3 * P], start=False,
                             stop=True, tile_position=(0, 32 * j)).then_inc(sm.pv_done.sem, 1)

        def oT_act(act, it, c4):
            act.wait_ge(*sm.pv_done(it, (c4 + 1) * HPC))
            act.wait_ge(*(g.mod_in_psum(it, 0) if ffn else g.y_done(it, 0)))
            if ffn:
                last = nc.scalar.copy(oT[:, c4], b_o[c4 % 2][:, 0:T])
            else:
                last = nc.scalar.activation(oT[:, c4], b_o[c4 % 2][:, 0:T], ACT.Identity,
                                            bias=bias_v[:, c4:c4 + 1])
            last.then_inc(g.oT_ready.sem, 1)

        def probsT_dve(dve, it, h):
            dve.wait_ge(*sm.probsT_in_psum(it, h + 1))
            dve.wait_ge(*sm.pv_done(it, h - 1))
            nc.vector.tensor_copy(probsT[:, h % 2], b_pT[h % 2][:, 0:SCORE_COLS])\
                .then_inc(sm.probsT_ready.sem, 1)

        def attention_out_pe(pe, it):
            pe.wait_ge(*g.oT_ready(it, CH))
            for t in range(NT):
                dst = b_y[:, t * D:(t + 1) * D]
                for c in range(CH):
                    last = nc.tensor.matmul(dst, oT[:, c, t * P:(t + 1) * P], wo[:, c],
                                            start=(c == 0), stop=(c == CH - 1))
            last.then_inc(g.y_done.sem, 1)

        def gu_banks(f):
            return (bank[1], bank[2]) if f % 2 == 0 else (bank[3], bank[4])

        def gate_up_pe(pe, it, f, parts=(0, 1)):
            if f < 2:
                pe.wait_ge(*sm.probs_ready(it, H))
                pe.wait_ge(*g.qk_ready(it, ROUNDS))
            else:
                pe.wait_ge(*g.act_ready(it, f - 1))
            bg, bu = gu_banks(f)
            for n in parts:
                cols = slice((2 * f + n) * P, (2 * f + n + 1) * P)
                for w, out in ((w_up, bu), (w_in, bg)):
                    for c in range(KC):
                        nc.tensor.matmul(out[:, n * T:(n + 1) * T], w[:, c, cols], core.xnT[:, c],
                                         start=(c == 0 and n == 0), stop=(w is w_up and c == KC - 1),
                                         skip_group_check=True)

        def modulate_pe(pe, it, f):
            if f == 0:
                pe.wait_ge(*g.modh_ready(it, 1))
            bg, bu = gu_banks(f)
            for n in range(2):
                last = nc.tensor.matmul(bg[:, n * T:(n + 1) * T],
                                        wb[:, (2 * f + n) * P:(2 * f + n + 1) * P], modh[:],
                                        start=False, stop=True, skip_group_check=True)
            last.then_inc(g.gate_up_in_psum.sem, 1)

        def mod_pe(pe, it):
            pe.wait_ge(*g.oT_ready(it, CH))
            pe.wait_ge(*sm.probsT_ready(it, H))
            for n, (w, act, chunks) in enumerate(((woa, oT, CH), (wa2, core.xnT, KC))):
                for c in range(chunks):
                    last = nc.tensor.matmul(b_pT[0][0:MR, n * T:(n + 1) * T], w[:, c], act[:, c],
                                            start=(c == 0), stop=(c == chunks - 1))
            last.then_inc(g.mod_in_psum.sem, 1)

        def tanh_act(act, it):
            act.wait_ge(*g.mod_in_psum(it, 1))
            act.wait_ge(*g.modh_ready(it, 0))
            nc.scalar.activation(tanh_mod[:], b_pT[0][0:MR, 0:T], ACT.Tanh)\
                .then_inc(g.tanh_ready.sem, 1)

        def modh_dve(dve, it):
            dve.wait_ge(*g.tanh_ready(it, 1))
            dve.wait_ge(*g.gate_up_in_psum(it, 0))
            nc.vector.scalar_tensor_tensor(out=modh[:], in0=tanh_mod[:], scalar=0.1,
                                           in1=b_pT[0][0:MR, T:2 * T], op0=ALU.mult, op1=ALU.mult)\
                .then_inc(g.modh_ready.sem, 1)

        def gate_act(act, it, f):
            act.wait_ge(*g.gate_up_in_psum(it, f + 1))
            act.wait_ge(*g.silu_ready(it, f - 1))
            nc.scalar.activation(gate_t[:, f % 2], gu_banks(f)[0][:, :], ACT.Tanh, scale=0.5)\
                .then_inc(g.gate_tanh.sem, 1)

        def silu_dve(dve, it, f):
            dve.wait_ge(*g.gate_tanh(it, f + 1))
            dve.wait_ge(*g.act_ready(it, f - 1))
            nc.vector.scalar_tensor_tensor(out=silu[:, f % 2], in0=gate_t[:, f % 2], scalar=1.0,
                                           in1=gu_banks(f)[0][:, :], op0=ALU.add, op1=ALU.mult)\
                .then_inc(g.silu_ready.sem, 1)

        def up_dve(dve, it, f):
            dve.wait_ge(*g.silu_ready(it, f + 1))
            dve.wait_ge(*g.y_done(it, 0))
            nc.vector.tensor_tensor(hidden[:, f], silu[:, f % 2], gu_banks(f)[1][:, :], ALU.mult)\
                .then_inc(g.act_ready.sem, 1)

        def down_pe(pe, it, f):
            pe.wait_ge(*g.act_ready(it, f + 1))
            if f == 0:
                pe.wait_ge(*core.x_updated(it, 0))
            for n in range(2):
                for t in range(NT):
                    last = nc.tensor.matmul(
                        b_y[:, t * D:(t + 1) * D],
                        hidden[:, f, n * T + t * P:n * T + (t + 1) * P], w_down[:, 2 * f + n],
                        start=(f == 0 and n == 0 and t == 0), stop=(f == FC // 2 - 1 and n == 1),
                        skip_group_check=True)
            if f == FC // 2 - 1:
                last.then_inc(g.y_done.sem, 1)

        with nc.Block() as block:
            @block.tensor
            def _(pe):
                transpose_pe(pe, -1, first=True)
                with pe.Fori(0, NB) as it:
                    for r_ in range(ROUNDS):
                        project_pe(pe, it, r_)
                    project_v_pe(pe, it)
                    for s in range(H + LAG_NV):
                        if s == LAG_NT + 1:
                            pe.wait_ge(*core.x_updated(it, 0))
                        if s < H:
                            head_scores_pe(pe, it, s)
                        if LAG_NT <= s < H + LAG_NT:
                            pe.wait_ge(*g.probs_normal(it, s - LAG_NT + 1))
                            transpose_probs_pe(core, pe, sm, it, s - LAG_NT, b_pT, probs)
                        if s >= LAG_NV:
                            head_pv_pe(pe, it, s - LAG_NV)
                        if ffn and s == H + 1:
                            gate_up_pe(pe, it, 0, parts=(0,))
                    if ffn:
                        gate_up_pe(pe, it, 0, parts=(1,))
                        mod_pe(pe, it)
                        gate_up_pe(pe, it, 1, parts=(0,))
                        modulate_pe(pe, it, 0)
                        gate_up_pe(pe, it, 1, parts=(1,))
                        modulate_pe(pe, it, 1)
                        for f in range(FC // 2):
                            if f + 2 < FC // 2:
                                gate_up_pe(pe, it, f + 2)
                                modulate_pe(pe, it, f + 2)
                            if f == FC // 2 - 2:
                                transpose_pe(pe, it)
                            down_pe(pe, it, f)
                    else:
                        transpose_pe(pe, it)
                        attention_out_pe(pe, it)

            @block.vector
            def _(dve):
                def prepare(it, b, part):
                    if part == 0:
                        ln_stats_dve(core, dve, it, b)
                    if part == 1:
                        ln_normalize_dve(core, dve, it, b)
                    if ffn and part == 2:
                        var2_dve(dve, it)
                    if ffn and part == 3:
                        r_dve(dve, it)
                for part in range(4):
                    prepare(-1, 0, part)
                with dve.Fori(0, NB) as it:
                    if rope:
                        for r_ in range(ROUNDS):
                            rope_dve(dve, it, r_)
                    for s in range(H + LAG_NT):
                        if s < H:
                            max_dve(core, dve, sm, it, s, b_s, nmax)
                        if s >= LAG_NT:
                            probsT_dve(dve, it, s - LAG_NT)
                        if 1 <= s <= H:
                            recip_dve(dve, it, s - 1)
                        if s in (2, 4, 6, 8):
                            prepare(it, it + 1, s // 2 - 1)
                    if ffn:
                        modh_dve(dve, it)
                        for f in range(FC // 2):
                            silu_dve(dve, it, f)
                            up_dve(dve, it, f)
                    dve.wait_ge(*g.y_done(it, 1))
                    xb = core.x[:, it].rearrange("p t d -> p (t d)")
                    dve.wait_ge(*g.residual_added(it - 1, 1))
                    nc.vector.scalar_tensor_tensor(out=xb, in0=b_y[:, :], scalar=0.5 if ffn else 1.0,
                                                   in1=xb, op0=ALU.mult, op1=ALU.add)\
                        .then_inc(core.x_updated.sem, 1)

            @block.gpsimd
            def _(pool):
                def prepare_x_pool(pool, it, b):
                    if ffn:
                        residual_pool(pool, it, b)
                        rms2_pool(pool, it)
                    else:
                        bias_pool(pool, it, b)
                ln_rstd_pool(core, pool, -1)
                prepare_x_pool(pool, -1, 0)
                with pool.Fori(0, NB) as it:
                    if rope:
                        for r_ in range(ROUNDS):
                            rope_pool(pool, it, r_)
                    for h in range(H):
                        normalise_pool(pool, it, h)
                        if h == 3:
                            ln_rstd_pool(core, pool, it)
                        if h == 6:
                            prepare_x_pool(pool, it, it + 1)

            @block.scalar
            def _(act):
                if ffn:
                    squares_act(act, -1)
                xnT_act(act, -1, ())
                with act.Fori(0, NB) as it:
                    if ffn:
                        for r_ in range(ROUNDS):
                            qk_act(act, it, r_)
                            if r_ == 0:
                                own_rows_act(act, it, 0)
                                own_rows_act(act, it, 1)
                        v_act(act, it)
                    else:
                        v_act(act, it)
                        own_rows_act(act, it, 0)
                        own_rows_act(act, it, 1)
                    for s in range(H + LAG_NV + 1):
                        if s + 2 < H:
                            own_rows_act(act, it, s + 2)
                        if s < H:
                            exp_act(core, act, sm, it, s, b_s, nmax, probs, sums,
                                    g.recip_ready(it - 1, s + 1))
                        done = s - LAG_NV
                        if done >= 0 and done % HPC == 0 and done > 0:
                            oT_act(act, it, done // HPC - 1)
                        if ffn and s == 5:
                            squares_act(act, it)
                    if ffn:
                        tanh_act(act, it)
                        for f in range(FC // 2):
                            gate_act(act, it, f)
                    xnT_act(act, it, [g.v_in_psum(it, 1)] +
                            ([g.gate_up_in_psum(it, FC // 2)] if ffn else []))

        core.ln_ran()
        for s in sm.loop:
            s.ran(NB)
        for s in g.loop:
            if ffn or s not in g.ffn_only:
                s.ran(NB)
        for s in g.prep if ffn else [g.residual_added]:
            s.ran(NB + 1)
        if ffn:
            g.qk_products.ran(-NB)


def build(nc, ins, out):
    with ExitStack() as ctx:
        core = Core(ctx, nc, ins)
        mla = Mla(ctx, core)
        sm = Softmax(ctx, core)
        ternary = Ternary(ctx, core)
        small = Small(ctx, core)
        load_inputs(core)
        prime_signals(core, [*mla.prep, *small.prep],
                      [*mla.loop, *sm.loop, *ternary.loop, *small.loop])
        mla_sublayer(core, sm, mla, "a0_", [])
        with ExitStack() as weights_ctx:
            w = delta_weights(core, weights_ctx)
            ternary_sublayer(core, ternary, 0, [w])
            delta_sublayer(core, w)
        ternary_sublayer(core, ternary, 1, [])
        with ExitStack() as weights_ctx:
            w_ffn = small_weights(core, weights_ctx, True)
            w_rope = small_weights(core, weights_ctx, False)
            mla_sublayer(core, sm, mla, "a1_", [w_ffn, w_rope])
            small_sublayer(core, sm, small, True, 0, w_ffn)
            small_sublayer(core, sm, small, False, 1, w_rope)
            small_sublayer(core, sm, small, True, 2, w_ffn)
        done = ctx.enter_context(nc.semaphore("stored"))
        with nc.Block() as block:
            @block.sync
            def _(sp):
                for b in range(NB):
                    sp.dma_start(out[b], core.x[:, b]).then_inc(done, 16)
                sp.wait_ge(done, 16 * NB)



def layout(i):
    import numpy as np
    a = {k: np.asarray(v) for k, v in i.items()}
    f = {}
    tok = lambda w: np.ascontiguousarray(w)
    swap = np.r_[R // 2:R, 0:R // 2]

    def chunks(w, c=KC):
        return tok(w.reshape(c, P, w.shape[1]).transpose(1, 0, 2))

    f["x"] = tok(a["L0_attn_a_hidden_states"].reshape(NB, NT, P, D).transpose(0, 2, 1, 3))
    f["ident"] = np.eye(P, dtype=np.float32)
    f["mask"] = np.triu(np.full((P, P), MASKED, np.float32), 1)

    def mla(tag, qa, qln, qb, ckv, kpe, kvln, kvb, wo):
        f[tag + "q_nope"] = tok(qb[:, :P].transpose(1, 0, 2))
        pe_ = qb[:, P:].transpose(2, 0, 1)
        f[tag + "q_pe0"], f[tag + "q_pe1"] = tok(pe_[:P]), tok(pe_[P:])
        f[tag + "k_nope"] = tok(kvb[:, :P].transpose(1, 0, 2))
        f[tag + "w_v"] = tok(kvb[:, P:].transpose(1, 0, 2))
        f[tag + "w_o"] = tok(wo.transpose(1, 0, 2))
        f[tag + "w_lat"] = chunks(np.concatenate([qa, ckv, kpe, kpe[:, swap]], 1))
        f[tag + "norm_w"] = tok(np.broadcast_to(np.concatenate([qln, kvln]), (P, QL + CL)))

    g = lambda n: a["L0_attn_a_" + n]
    mla("a0_", g("q_a_w").T, g("q_a_ln_w"), g("q_b_w").reshape(H, 192, QL), g("kv_a_w")[:CL].T,
        g("kv_a_w")[CL:].T, g("kv_a_ln_w"), g("kv_b_w").reshape(H, 256, CL),
        g("o_w").T.reshape(H, P, D))
    g = lambda n: a["L1_attn_a_" + n]
    mla("a1_", g("Wq_a"), g("q_norm_w"), g("Wq_b").T.reshape(H, 192, QL), g("Wkv_a"), g("Wk_rope"),
        g("kv_norm_w"), g("Wkv_b").T.reshape(H, 256, CL), g("Wo").reshape(H, P, D))

    f["f0_w"] = chunks(a["L0_ffn_weight"].T)
    f["f0_b"] = tok(a["L0_ffn_bias"].reshape(1, D))

    def heads(w):
        wide = np.zeros((w.shape[0], H, 32), w.dtype)
        wide[:, :, :HD] = w.reshape(w.shape[0], H, HD)
        return wide.reshape(w.shape[0], CH * P)

    def halves(w):
        wide = w.reshape(w.shape[0], ROUNDS, 2, HPR // 2, 2, HD // 2)
        return wide.transpose(0, 1, 2, 4, 3, 5).reshape(w.shape[0], D)

    own = np.zeros((2, 2, HPR // 2, HD // 2, HPR), np.float32)
    for j in range(HPR):
        own[j // 4, :, j % 4, :, j] = 1.0
    own = own.reshape(P, HPR)
    f["m_own_rows"], f["b_own_rows"] = own * np.float32(HD ** -0.5), own
    g = lambda n: a["L1_ffn_" + n]
    f["m_wq"] = chunks(halves(g("Wq").T)).reshape(P, KC, ROUNDS, P)
    f["m_wk"] = chunks(halves(g("Wk").T)).reshape(P, KC, ROUNDS, P)
    f["m_wv"], f["m_wo"], f["m_wa"] = chunks(g("Wv").T), chunks(heads(g("Wo"))), chunks(g("A"))
    f["m_ln1"], f["m_ln2"] = tok(g("ln1_w").reshape(KC, P).T), tok(g("ln2_w").reshape(KC, P).T)
    f["m_w_in"], f["m_w_up"] = chunks(g("W_in_base").T), chunks(g("W_up_base").T)
    f["m_wb"], f["m_w_down"] = g("B"), chunks(g("W_down").T, FC)
    g = lambda n: a["L1_attn_b_" + n]
    for n in "qk":
        f["b_w" + n] = chunks(halves(g("W" + n).T)).reshape(P, KC, ROUNDS, P)
    f["b_bias_qk"] = tok(np.stack([halves(g(n).reshape(1, D)).reshape(ROUNDS, P).T
                                   for n in ("bq", "bk")], 1))
    f["b_wv"], f["b_wo"] = chunks(g("Wv").T), chunks(heads(g("Wo")).T, CH)
    f["b_bias_v"] = tok(heads(g("bv").reshape(1, D)).reshape(CH, P).T)
    f["b_bias_o"] = tok(np.broadcast_to(g("bo").reshape(1, 1, D), (P, 1, D)))
    theta = np.float32(10000.0) ** (np.float32(-2.0) * np.arange(HD // 2, dtype=np.float32) / np.float32(HD))
    ang = (np.arange(1, T + 1, dtype=np.float32)[:, None] * theta[None, :]).astype(np.float32)
    cos = np.zeros((2, 2, HPR // 2, HD // 2, 2, T), np.float32)
    sin = np.zeros((2, 2, HPR // 2, HD // 2, 2, T), np.float32)
    for half in range(2):
        for n, scale in enumerate((HD ** -0.5, 1.0)):
            cos[:, half, :, :, n] = np.cos(ang).T * scale
            sin[:, half, :, :, n] = np.sin(ang).T * (-scale if half else scale)
    f["b_cos"], f["b_sin"] = cos.reshape(P, 2, T), sin.reshape(P, 2, T)

    g = lambda n: a["L0_attn_b_" + n]
    for n in "qkvg":
        f["d_w" + n] = chunks(g("W" + n))
    f["d_wo"], f["d_wa"], f["d_wb"] = chunks(g("Wo"), H), chunks(g("Wa")), chunks(g("Wb"))
    f["d_ba"], f["d_bb"] = tok(g("ba").reshape(H, 1)), tok(g("bb").reshape(1, H))
    f["d_taps"] = tok(np.stack([g(f"conv_{n}_w").reshape(H, P, TAPS).transpose(1, 0, 2)
                                for n in "kqv"], 1))
    f["d_tap_bias"] = tok(np.stack([g(f"conv_{n}_b").reshape(H, P).T for n in "kqv"], 1))
    f["d_o_w"], f["d_o_b"] = tok(g("ln_w").reshape(P, 1)), tok(g("ln_b").reshape(P, 1))

    inv_freq = (1.0 / 10000.0 ** (np.arange(0, R, 2, dtype=np.float32) / np.float32(R))).astype(np.float32)
    ang = np.outer(np.arange(T, dtype=np.float32), inv_freq).astype(np.float32)
    cos = np.concatenate([np.cos(ang)] * 2, 1).astype(np.float32)
    sin = np.concatenate([-np.sin(ang), np.sin(ang)], 1).astype(np.float32)
    f["cosT"] = tok(np.concatenate([cos.T] * 2, 0))
    f["sinT"] = tok(np.concatenate([-sin.T] * 2, 0))
    f["cos_tok"] = tok(cos.reshape(NT, P, R).transpose(1, 0, 2))
    f["sin_tok"] = tok(sin.reshape(NT, P, R).transpose(1, 0, 2))
    f["ms_scale"] = np.zeros((P, NT, 2), np.float32) + np.array([1.0 / QL, 1.0 / CL], np.float32)
    f["q_scale"] = np.zeros((P, NT, 2), np.float32) + np.array([192.0 ** -0.5, 1.0], np.float32)
    return f


def kernel(**inputs):
    import numpy as np
    import concourse.bacc as bacc
    from concourse.bass_utils import run_bass_kernel_spmd

    nc = bacc.Bacc("TRN2", target_bir_lowering=False, num_devices=1)
    arrays = {f"in_{k}": v for k, v in layout(inputs).items()}
    ins = {n[3:]: nc.dram_tensor(n, v.shape, mybir.dt.from_np(v.dtype), kind="ExternalInput").ap()
           for n, v in arrays.items()}
    out = nc.dram_tensor("out_x", (NB, P, NT, D), F32, kind="ExternalOutput").ap()
    build(nc, ins, out)
    r = run_bass_kernel_spmd(nc, [arrays], core_ids=[0])
    y = np.asarray(r.results[0]["out_x"])
    return np.ascontiguousarray(y.transpose(0, 2, 1, 3)).reshape(NB, T, D)
```
